# Optimizing a Trainium2 kernel written in Bass

```python
import numpy as np
import jax
import jax.numpy as jnp

def _softmax(x, axis=-1):
    return jax.nn.softmax(x, axis=axis)

def _gelu(x):
    return jax.nn.gelu(x, approximate=True)

def _silu(x):
    return jax.nn.silu(x)

def _sigmoid(x):
    return jax.nn.sigmoid(x)

def _layernorm(x, axis=-1, eps=1e-05):
    m = jnp.mean(x, axis=axis, keepdims=True)
    v = jnp.var(x, axis=axis, keepdims=True)
    return (x - m) / jnp.sqrt(v + eps)

def _scatter_add(tgt, idx, src, axis=0):
    return tgt.at[idx].add(src)

def _segment_sum(src, seg, n):
    return jax.ops.segment_sum(src, seg, n)
kernel_name = 'mk_xattn_ffn_d2_seqx_r8_7acc7f'

def setup_inputs(seed: int=0):
    np.random.seed(seed)
    _w = jnp.asarray

    def _rec_inputs():
        import jax
        import jax.numpy as jnp
        _rk = jax.random.key(seed)
        x = -0.0002928 + 1 * jax.random.normal(jax.random.fold_in(_rk, 1), (8, 256, 128), jnp.float32)
        _lenS = 256 - jax.random.randint(jax.random.fold_in(_rk, 7), (8,), 0, max(1, 256 // 4) + 1, jnp.int32)
        _lenS2 = 256 - jax.random.randint(jax.random.fold_in(_rk, 8), (8,), 0, max(1, 256 // 4) + 1, jnp.int32)
        _ctx_1024P = jax.random.normal(jax.random.fold_in(_rk, 11), (8, 16, 128), jnp.float32)
        _ctx_1024c = jax.random.dirichlet(jax.random.fold_in(_rk, 511), 0.3 * jnp.ones((16,), jnp.float32), (8, 256))
        _ctx_1024t = jnp.einsum('bsk,bkd->bsd', _ctx_1024c, _ctx_1024P)
        _ctx_1024t = _ctx_1024t * jax.lax.rsqrt(jnp.mean(jnp.square(_ctx_1024t)) + 1e-12) * 0.953939
        ctx_1024 = -1.39393e-06 + 0.999914 * (_ctx_1024t + 0.3 * jax.random.normal(jax.random.fold_in(_rk, 611), (8, 256, 128), jnp.float32))
        _validS = jnp.arange(256)[None, :] < _lenS[:, None]
        _validS2 = jnp.arange(256)[None, :] < _lenS2[:, None]
        _causal = jnp.tril(jnp.ones((256, 256), dtype=bool))
        mask_Bx16xS2_ik1 = jnp.where(jnp.broadcast_to(_validS2[:, None, :], (8, 16, 256)), 1, 0).astype(jnp.int32)
        return (x, ctx_1024, mask_Bx16xS2_ik1)
    x, ctx_1024, mask_Bx16xS2_ik1 = _rec_inputs()

    def _L0_xattn_setup():
        import jax, jax.numpy as jnp
        import numpy as np
        D_MODEL = 128
        NUM_HEADS = 16
        D_K = D_MODEL // NUM_HEADS
        NEG = -1000000000.0

        def _split_heads(x, B, L):
            return x.reshape(B, L, NUM_HEADS, D_K).transpose(0, 2, 1, 3)
        key = jax.random.key(seed)
        ks = jax.random.split(key, 12)
        B, L = (2, 256)
        s = 1.0 / np.sqrt(D_MODEL)
        inp = {'query': jax.random.normal(ks[0], (B, L, D_MODEL), jnp.float32), 'key': jax.random.normal(ks[1], (B, L, D_MODEL), jnp.float32), 'value': jax.random.normal(ks[2], (B, L, D_MODEL), jnp.float32), 'hash_q': jax.random.randint(ks[3], (B, NUM_HEADS, L), 0, 2, jnp.int32), 'hash_k': jax.random.randint(ks[4], (B, NUM_HEADS, L), 0, 2, jnp.int32), 'Wq': jax.random.normal(ks[5], (D_MODEL, D_MODEL), jnp.float32) * s, 'bq': jnp.zeros((D_MODEL,), jnp.float32), 'Wk': jax.random.normal(ks[6], (D_MODEL, D_MODEL), jnp.float32) * s, 'bk': jnp.zeros((D_MODEL,), jnp.float32), 'Wv': jax.random.normal(ks[7], (D_MODEL, D_MODEL), jnp.float32) * s, 'bv': jnp.zeros((D_MODEL,), jnp.float32)}
        return inp
    _L0_xattn_all = _L0_xattn_setup()
    _L0_xattn_in = {k: v for k, v in _L0_xattn_all.items() if k in ('Wq', 'bq', 'Wk', 'bk', 'Wv', 'bv')}
    del _L0_xattn_all

    def _L0_ffn_setup():
        import jax, jax.numpy as jnp
        import numpy as np
        N_EMBD = 128
        NUM_EXPERTS = 8
        TOP_K = 2
        D_FF = 4 * N_EMBD
        B, S = (4, 256)
        key = jax.random.key(seed)
        ks = jax.random.split(key, 7)
        scale = lambda fan_in: 1.0 / np.sqrt(fan_in)
        x = jax.random.normal(ks[0], (B, S, N_EMBD), dtype=jnp.float32)
        W_router = jax.random.normal(ks[1], (N_EMBD, NUM_EXPERTS), dtype=jnp.float32) * scale(N_EMBD)
        b_router = jnp.zeros((NUM_EXPERTS,), dtype=jnp.float32)
        W1 = jax.random.normal(ks[2], (NUM_EXPERTS, N_EMBD, D_FF), dtype=jnp.float32) * scale(N_EMBD)
        b1 = jnp.zeros((NUM_EXPERTS, D_FF), dtype=jnp.float32)
        W2 = jax.random.normal(ks[3], (NUM_EXPERTS, D_FF, N_EMBD), dtype=jnp.float32) * scale(D_FF)
        b2 = jnpp = jnp.zeros((NUM_EXPERTS, N_EMBD), dtype=jnp.float32)
        return {'x': x, 'W_router': W_router, 'b_router': b_router, 'W1': W1, 'b1': b1, 'W2': W2, 'b2': b2}
    _L0_ffn_all = _L0_ffn_setup()
    _L0_ffn_in = {k: v for k, v in _L0_ffn_all.items() if k in ('W_router', 'b_router', 'W1', 'b1', 'W2', 'b2')}
    del _L0_ffn_all

    def _L1_xattn_setup():
        import math
        import jax, jax.numpy as jnp
        import numpy as np
        H = 16
        D_MODEL = 128
        D_K = 64
        D_V = 64
        key = jax.random.key(seed)
        ks = jax.random.split(key, 7)
        b, n = (2, 256)
        scale = 1.0 / math.sqrt(D_MODEL)
        return {'q': jax.random.normal(ks[0], (b, n, D_MODEL), jnp.float32), 'k': jax.random.normal(ks[1], (b, n, D_MODEL), jnp.float32), 'v': jax.random.normal(ks[2], (b, n, D_MODEL), jnp.float32), 'w_q': jax.random.normal(ks[3], (H * D_K, D_MODEL), jnp.float32) * scale, 'w_k': jax.random.normal(ks[4], (H * D_K, D_MODEL), jnp.float32) * scale, 'w_v': jax.random.normal(ks[5], (H * D_V, D_MODEL), jnp.float32) * scale, 'w_o': jax.random.normal(ks[6], (D_MODEL, H * D_V), jnp.float32) * scale}
    _L1_xattn_all = _L1_xattn_setup()
    _L1_xattn_in = {k: v for k, v in _L1_xattn_all.items() if k in ('w_q', 'w_k', 'w_v', 'w_o')}
    del _L1_xattn_all

    def _L1_ffn_setup():
        import jax, jax.numpy as jnp
        import numpy as np
        DIM = 128
        HID = 352
        E = 8
        TOPK = 2
        key = jax.random.key(seed)
        ks = jax.random.split(key, 5)
        x = jax.random.normal(ks[0], (4, 256, DIM), dtype=jnp.float32)
        W_gate = jax.random.normal(ks[1], (DIM, E), dtype=jnp.float32) * 0.02
        Wg = jax.random.normal(ks[2], (E, DIM, HID), dtype=jnp.float32) * 0.02
        Wu = jax.random.normal(ks[3], (E, DIM, HID), dtype=jnp.float32) * 0.02
        Wd = jax.random.normal(ks[4], (E, HID, DIM), dtype=jnp.float32) * 0.02
        return {'x': x, 'W_gate': W_gate, 'Wg': Wg, 'Wu': Wu, 'Wd': Wd}
    _L1_ffn_all = _L1_ffn_setup()
    _L1_ffn_in = {k: v for k, v in _L1_ffn_all.items() if k in ('W_gate', 'Wg', 'Wu', 'Wd')}
    del _L1_ffn_all
    return {'x': x, 'ctx_1024': ctx_1024, 'mask_Bx16xS2_ik1': mask_Bx16xS2_ik1, 'L0_xattn_Wq': _L0_xattn_in['Wq'], 'L0_xattn_bq': _L0_xattn_in['bq'], 'L0_xattn_Wk': _L0_xattn_in['Wk'], 'L0_xattn_bk': _L0_xattn_in['bk'], 'L0_xattn_Wv': _L0_xattn_in['Wv'], 'L0_xattn_bv': _L0_xattn_in['bv'], 'L0_ffn_W_router': _L0_ffn_in['W_router'], 'L0_ffn_b_router': _L0_ffn_in['b_router'], 'L0_ffn_W1': _L0_ffn_in['W1'], 'L0_ffn_b1': _L0_ffn_in['b1'], 'L0_ffn_W2': _L0_ffn_in['W2'], 'L0_ffn_b2': _L0_ffn_in['b2'], 'L1_xattn_w_q': _L1_xattn_in['w_q'], 'L1_xattn_w_k': _L1_xattn_in['w_k'], 'L1_xattn_w_v': _L1_xattn_in['w_v'], 'L1_xattn_w_o': _L1_xattn_in['w_o'], 'L1_ffn_W_gate': _L1_ffn_in['W_gate'], 'L1_ffn_Wg': _L1_ffn_in['Wg'], 'L1_ffn_Wu': _L1_ffn_in['Wu'], 'L1_ffn_Wd': _L1_ffn_in['Wd']}

def reference(x, ctx_1024, mask_Bx16xS2_ik1, L0_xattn_Wq, L0_xattn_bq, L0_xattn_Wk, L0_xattn_bk, L0_xattn_Wv, L0_xattn_bv, L0_ffn_W_router, L0_ffn_b_router, L0_ffn_W1, L0_ffn_b1, L0_ffn_W2, L0_ffn_b2, L1_xattn_w_q, L1_xattn_w_k, L1_xattn_w_v, L1_xattn_w_o, L1_ffn_W_gate, L1_ffn_Wg, L1_ffn_Wu, L1_ffn_Wd):
    import jax
    import jax.numpy as jnp

    def _L0_xattn_ref(query, key, value, hash_q, hash_k, Wq, bq, Wk, bk, Wv, bv):
        import jax, jax.numpy as jnp
        import numpy as np
        D_MODEL = 128
        NUM_HEADS = 16
        D_K = D_MODEL // NUM_HEADS
        NEG = -1000000000.0

        def _split_heads(x, B, L):
            return x.reshape(B, L, NUM_HEADS, D_K).transpose(0, 2, 1, 3)
        B, Lq, _ = query.shape
        Lk = key.shape[1]
        q = _split_heads(query @ Wq.T + bq, B, Lq)
        k = _split_heads(key @ Wk.T + bk, B, Lk)
        v = _split_heads(value @ Wv.T + bv, B, Lk)
        scores = jnp.einsum('bhqd,bhkd->bhqk', q, k) / jnp.sqrt(jnp.float32(D_K))
        mask = (hash_q[:, :, :, None] != hash_k[:, :, None, :]).astype(scores.dtype) * NEG
        attn = jax.nn.softmax(scores + mask, axis=-1)
        out = jnp.einsum('bhqk,bhkd->bhqd', attn, v)
        return out.transpose(0, 2, 1, 3).reshape(B, Lq, D_MODEL)

    def _L0_ffn_ref(x, W_router, b_router, W1, b1, W2, b2):
        import jax, jax.numpy as jnp
        import numpy as np
        N_EMBD = 128
        NUM_EXPERTS = 8
        TOP_K = 2
        D_FF = 4 * N_EMBD
        B, S = (4, 256)
        Bv, Sv, D = x.shape
        flat_x = x.reshape(-1, D)
        T = flat_x.shape[0]
        logits = flat_x @ W_router + b_router
        top_vals, top_idx = jax.lax.top_k(logits, TOP_K)
        neg_inf = jnp.full_like(logits, -jnp.inf)
        sparse_logits = neg_inf.at[jnp.arange(T)[:, None], top_idx].set(top_vals)
        router_weights = jax.nn.softmax(sparse_logits, axis=-1)
        final_output = jnp.zeros_like(flat_x)
        for e in range(NUM_EXPERTS):
            expert_mask = jnp.any(top_idx == e, axis=-1)
            h = jax.nn.relu(flat_x @ W1[e] + b1[e])
            y = h @ W2[e] + b2[e]
            w = router_weights[:, e] * expert_mask.astype(x.dtype)
            final_output = final_output + y * w[:, None]
        return final_output.reshape(Bv, Sv, D)

    def _L1_xattn_ref(q, k, v, w_q, w_k, w_v, w_o):
        import math
        import jax, jax.numpy as jnp
        import numpy as np
        H = 16
        D_MODEL = 128
        D_K = 64
        D_V = 64
        b, n, _ = q.shape
        qh = (q @ w_q.T).reshape(b, n, H, D_K).transpose(0, 2, 1, 3)
        kh = (k @ w_k.T).reshape(b, n, H, D_K).transpose(0, 2, 1, 3)
        vh = (v @ w_v.T).reshape(b, n, H, D_V).transpose(0, 2, 1, 3)
        scores = jnp.einsum('bhid,bhjd->bhij', qh, kh) / math.sqrt(D_K)
        causal = jnp.tril(jnp.ones((n, n), dtype=bool))
        scores = jnp.where(causal[None, None], scores, -jnp.inf)
        attn = jax.nn.softmax(scores, axis=-1)
        out = jnp.einsum('bhij,bhjd->bhid', attn, vh)
        out = out.transpose(0, 2, 1, 3).reshape(b, n, H * D_V)
        return out @ w_o.T

    def _L1_ffn_ref(x, W_gate, Wg, Wu, Wd):
        import jax, jax.numpy as jnp
        import numpy as np
        DIM = 128
        HID = 352
        E = 8
        TOPK = 2
        B, T, D = x.shape
        xf = x.reshape(-1, D)
        N = xf.shape[0]
        logits = xf @ W_gate
        w, idx = jax.lax.top_k(logits, TOPK)
        w = jax.nn.softmax(w, axis=-1)
        cw = jnp.zeros((N, E), dtype=x.dtype).at[jnp.arange(N)[:, None], idx].add(w)
        out = jnp.zeros_like(xf)
        for e in range(E):
            h = jax.nn.silu(xf @ Wg[e]) * (xf @ Wu[e])
            out = out + h @ Wd[e] * cw[:, e:e + 1]
        return out.reshape(B, T, D)
    x = x + _L0_xattn_ref(_layernorm(x, axis=-1), ctx_1024, ctx_1024, mask_Bx16xS2_ik1, mask_Bx16xS2_ik1, L0_xattn_Wq, L0_xattn_bq, L0_xattn_Wk, L0_xattn_bk, L0_xattn_Wv, L0_xattn_bv)
    x = x + _L0_ffn_ref(_layernorm(x, axis=-1), L0_ffn_W_router, L0_ffn_b_router, L0_ffn_W1, L0_ffn_b1, L0_ffn_W2, L0_ffn_b2)
    x = x + _L1_xattn_ref(_layernorm(x, axis=-1), ctx_1024, ctx_1024, L1_xattn_w_q, L1_xattn_w_k, L1_xattn_w_v, L1_xattn_w_o)
    x = x + _L1_ffn_ref(_layernorm(x, axis=-1), L1_ffn_W_gate, L1_ffn_Wg, L1_ffn_Wu, L1_ffn_Wd)
    return x

_drawn_inputs = setup_inputs


def setup_inputs(seed=0):
    import zlib

    import numpy as np

    out = dict(_drawn_inputs(seed))
    spreads = {'L0_xattn_bq': (0.0, 0.1),
     'L0_xattn_bk': (0.0, 0.8),
     'L0_xattn_bv': (0.0, 0.1),
     'L0_ffn_b_router': (0.0, 0.1),
     'L0_ffn_b1': (0.0, 0.269),
     'L0_ffn_b2': (0.0, 0.1)}
    factors = {'L1_ffn_W_gate': 8.0, 'L1_ffn_Wg': 8.0, 'L1_ffn_Wu': 8.0, 'L1_ffn_Wd': 8.0}
    for name, (base, spread) in spreads.items():
        noise = np.random.default_rng([zlib.crc32(name.encode()), seed]).standard_normal(out[name].shape)
        drawn = base * np.exp(spread * noise) if base else spread * noise
        out[name] = jnp.asarray(drawn.astype(out[name].dtype))
    for name, factor in factors.items():
        out[name] = (out[name] * factor).astype(out[name].dtype)
    return out
```

```python
from contextlib import ExitStack

import numpy as np

import concourse.bass as bass
import concourse.mybir as mybir
from concourse.alu_op_type import AluOpType as ALU

F32, F32R, BF16 = mybir.dt.float32, mybir.dt.float32r, mybir.dt.bfloat16
I32, U32 = mybir.dt.int32, mybir.dt.uint32
ACT = mybir.ActivationFunctionType
AX = mybir.AxisListType.X

P = 128
B, S, D, H = 8, 256, 128, 16
QT = S // P
T = B * S
TT = T // P
DK0 = D // H
DK1 = 64
HB = 4
G = H // HB
M1 = H // 2
E, TOPK = 8, 2
F0, F1 = 512, 352
C0 = F0 // P
C1 = -(-F1 // P)
FP1 = C1 * P
NTILE = 40
IDLE = NTILE - T * TOPK // P
ROWS = E * T + IDLE * P
PAY = D + 1
NOWHERE = 5000
EPS = 1e-5
MASKED0 = float(2 ** 30)
MASKED1 = 1e30
SC0 = float(DK0) ** -0.5
SC1 = float(DK1) ** -0.5

_c = {}
_n = 0
for _name, _w in (("ident", P), ("cq", 1), ("ck", 1), ("one8", E), ("choice", TOPK * E), ("region", E),
                  ("lots", T // P), ("tile", NTILE), ("dest", TT * TOPK)):
    _c[_name] = (_n, _n + _w)
    _n += _w
CF = _n
_b = {}
_n = 0
for _name, _w in (("tri", P), ("ones", P), ("ident", P), ("causal", 2 * P), ("selq", G * P), ("selk", G * P)):
    _b[_name] = (_n, _n + _w)
    _n += _w
CB = _n


def constants():
    f = np.zeros((P, CF), np.float32)
    p = np.arange(P)
    f[:, slice(*_c["ident"])] = np.eye(P)
    f[:, _c["cq"][0]] = (p % 32 >= 16) & (p % 32 < 24)
    f[:, _c["ck"][0]] = (p % 32 >= 8) & (p % 32 < 16)
    f[:, slice(*_c["one8"])] = 1
    f[:, slice(*_c["choice"])] = np.tile(np.arange(E), TOPK)
    f[:, slice(*_c["region"])] = np.arange(E) * T
    f[:, slice(*_c["lots"])] = np.arange(T // P) * P
    f[:, slice(*_c["tile"])] = np.arange(NTILE)
    dest = p[:, None, None] + P * np.arange(TT)[None, :, None] + T * np.arange(TOPK)[None, None, :]
    f[:, slice(*_c["dest"])] = dest.reshape(P, -1)
    b = np.zeros((P, CB), np.float32)
    b[:, slice(*_b["tri"])] = p[:, None] < p[None, :]
    b[:, slice(*_b["ones"])] = 1
    b[:, slice(*_b["ident"])] = np.eye(P)
    b[:, slice(*_b["causal"])] = np.tile(np.where(p[None, :] > p[:, None], -MASKED1, 0), (1, 2))
    for h in range(H):
        g, j = divmod(h, HB)
        b[h, _b["selq"][0] + g * P + 32 * j + 24] = 1
        b[h, _b["selq"][0] + g * P + 32 * j + 25] = -1
        b[h, _b["selk"][0] + g * P + 32 * j + 24] = MASKED0
        b[h, _b["selk"][0] + g * P + 32 * j + 25] = -MASKED0
    return f, b


def program(nc, a, out):
    xs = [nc.dram_tensor(f"dispatch{n}", (ROWS, PAY), F32, kind="Internal").ap() for n in range(2)]
    yc = [nc.dram_tensor(f"results{n}", (TOPK * T, D), F32, kind="Internal").ap() for n in range(2)]

    with ExitStack() as ctx:
        def sb(name, shape, dt=F32):
            return ctx.enter_context(nc.sbuf_tensor(name, shape, dt))

        ps = ctx.enter_context(nc.psum_tensor("ps", [P, 8, 512], F32))

        x_sb = sb("x_sb", [P, TT, D])
        cf = sb("cf", [P, CF])
        cb = sb("cb", [P, CB], BF16)
        bias0 = sb("bias0", [P, 2, G])
        bias0c = sb("bias0c", [P, 2, G])
        bv_bc = sb("bv_bc", [P, D])
        br_bc = sb("br_bc", [P, E])
        wv0 = sb("wv0", [P, D])
        wr = sb("wr", [P, 2, E])
        wo1 = sb("wo1", [P, M1, D])
        b1t = sb("b1t", [P, E, C0])
        stage = sb("stage", [P, 2, 1024])
        w_up = sb("w_up", [P, E * 2 * 2 * F1], F32R)
        w_dn = sb("w_dn", [P, E * C0 * D])
        ra = sb("ra", [P, 3 * 2 * H * DK1], F32R)
        hl = sb("hl", [P, 2, 2, 2, S], F32R)
        ct = sb("ct", [P, 2, S])
        work = sb("work", [P, 17408])
        pay = sb("pay", [P, 2, QT, TOPK, PAY])
        xnt = sb("xnt", [P, S])
        ybuf = sb("ybuf", [P, 2, TOPK, QT, D])
        blank = sb("blank", [P, PAY])
        bn6 = sb("bn6", [P, 2, QT, 6])
        mv = sb("mv", [P, 2, QT, 2])
        rstd = sb("rstd", [P, 2, QT])
        var = sb("var", [P, 2, QT])
        varh = sb("varh", [P, 2, QT])
        rsq = sb("rsq", [P, 2, QT])
        xn = sb("xn", [P, 2, QT, D])
        wts = sb("wts", [P, 2, TT, TOPK])
        lg = sb("lg", [P, QT, E])
        top = sb("top", [P, QT, 8])
        topi = sb("topi", [P, QT, 8], U32)
        topf = sb("topf", [P, QT, TOPK])
        hot = sb("hot", [P, QT, TOPK, E])
        hotb = sb("hotb", [P, QT, E], BF16)
        dlt = sb("dlt", [P, QT])
        edl = sb("edl", [P, QT])
        den = sb("den", [P, QT])
        base = sb("base", [P, 2, E])
        pos = sb("pos", [P, QT, E])
        hp = sb("hp", [P, QT, TOPK, E])
        slotf = sb("slotf", [P, QT, TOPK])
        sloti = sb("sloti", [P, 2, QT, TOPK], U32)
        cnt = sb("cnt", [1, E])
        ntl = sb("ntl", [1, E])
        ends = sb("ends", [1, E])
        which = sb("which", [1, NTILE])
        before = sb("before", [1, NTILE])
        tile_e = sb("tile_e", [1, 2, NTILE], I32)
        tile_row = sb("tile_row", [1, 2, NTILE], I32)
        rec0 = sb("rec0", [P, H])
        att0 = sb("att0", [P, H, DK0])
        chib = sb("chib", [P, 2, S], F32R)
        ex = chib[:, :, :].rearrange("p r (l n) -> p r l n", l=2)
        dsti = sb("dsti", [P, 4], U32)
        mx1 = sb("mx1", [P, 2, 2, 3])
        nb1 = sb("nb1", [P, 2, 2, 2])
        rs1 = sb("rs1", [P, 2, 2, 2])
        rc1 = sb("rc1", [P, 2, 2, 2])

        def cst(name):
            return cf[:, slice(*_c[name])]

        def cstb(name):
            return cb[:, slice(*_b[name])]

        ident = cst("ident")
        maskraw = work[0:H, 8192:8192 + T].bitcast(I32).rearrange("h (b s) -> h b s", b=B)
        dest = cst("dest").rearrange("p (t c) -> p t c", c=TOPK)
        maskb = work[0:H, 13312:14336].bitcast(BF16).rearrange("h (b s) -> h b s", b=B)
        b2_bc = work[:, 12288:13312]
        mx0 = work[:, 14336:15360].rearrange("p (g t n) -> p g t n", g=G, t=QT)
        scratch = ybuf[0:1, :, :, :, :].rearrange("p r c t d -> p (r c t d)")
        lots = scratch[:, 0:E * T // P].rearrange("p (e n) -> p e n", e=E)
        past = scratch[:, 256:256 + NTILE * E].rearrange("p (n e) -> p n e", e=E)
        pastn = scratch[:, 640:640 + NTILE * E].rearrange("p (n e) -> p n e", e=E)
        wqk = ra[:, 0:2048].rearrange("p (w l n) -> p w l n", w=2, l=2)
        qb = ra[:, 2048:4096].rearrange("p (r g n) -> p r g n", r=2, g=G)
        kb = ra[:, 4096:6144].rearrange("p (r g n) -> p r g n", r=2, g=G)
        v0 = work[:, 0:2048].rearrange("p (r t h n) -> p r t h n", r=2, t=QT, h=H)
        pt0 = work[:, 2048:6144].rearrange("p (h n) -> p h n", h=8)
        ot0 = work[:, 6144:8192].rearrange("p (r g n) -> p r g n", r=2, g=G)
        w1p = ra[:, :].rearrange("p (w l n) -> p w l n", w=3, l=2)
        qt1 = work[:, 0:4096].rearrange("p (r m n) -> p r m n", r=2, m=M1)
        kt1 = work[:, 4096:8192].rearrange("p (r m n) -> p r m n", r=2, m=M1)
        v1 = work[:, 8192:12288].rearrange("p (r t n) -> p r t n", r=2, t=QT)
        p1 = work[:, 12288:13824].rearrange("p (r h n) -> p r h n", r=2, h=2)
        pt1 = work[:, 13824:15360].rearrange("p (r h n) -> p r h n", r=2, h=2)
        ot1 = work[:, 15360:17408].rearrange("p (m n) -> p m n", m=M1)
        xt = work[:, 0:4 * PAY].rearrange("p (r n) -> p r n", r=4)
        he = work[:, 1024:2048].rearrange("p (r n) -> p r n", r=2)
        ht = work[:, 2048:3072].rearrange("p (r n) -> p r n", r=2)
        hb = work[:, 3072:4096].rearrange("p (r n) -> p r n", r=2)
        ye = work[:, 4096:4096 + 4 * D].rearrange("p (r n) -> p r n", r=4)
        sg = work[:, 5120:5120 + 2 * F1].rearrange("p (r n) -> p r n", r=2)

        once = """consts_in bias_in xa_in xb_in wv_in wr_in wo_in b1_in b2_in mask_in
            st_in0 st_in1 wqk_in he_pad wqk_split wup_split st_split w2_in wd_in
            cb_ready mask_ready v0_clear v0_ready bias_ready blank_set blank_ready slots_blank0 slots_blank1
            qk_chi v_evac a_psum a_max mt_psum qm_ready b_psum b_exp ot_psum o_rec o_mul base_set mx_clear
            s_psum s_max s_nb s_exp s_rec s_norm pt_psum pt_evac v1_evac op_psum wl_hi wl_split out_done0 out_done1
            passed_sp passed_ve passed_po""".split()
        twice = dict(ctx_in0=64, ctx_in1=64, ctx_hi=B, ctx_split=B, ln_stats0=4 * B, ln_stats1=4 * B, rs_chain0=14 * B, rs_chain1=14 * B, rs_ready0=B, rs_ready1=B, xn_ready=B, xt_psum=B, x_hi=B, x_split=B,
                     qk_psum=4 * B, qk_ready=4 * B, v_psum=B, pv_psum=4 * B, pv_evac=2 * B, x_add=2 * B, 
                     pay_ready=B, pay_dest=2 * B, pay_copy=B, t2_psum=B, t2_evac=B, lg_psum=B, lg_done=B, top_done=5 * B,
                     hot_done=B, hotb_done=B, diff_done=B, exp_done=B, wts_den=B, wts_one=B, wts_done=B, pfx_psum=B,
                     pos_done=B, slot_chain=3 * B, slot_ready=B, sent0=256, sent1=256, table=13, table_ready=1,
                     e_x=NTILE, e_xhi=NTILE, e_xlo=NTILE, e_h=NTILE, e_hs=0, e_hcopy=NTILE, e_ht=NTILE, e_hb=NTILE,
                     e_htev=NTILE, e_y=NTILE, e_yev=NTILE, e_dst=NTILE, comb_one=B, comb=B, y_in0=128, y_in1=128)
        for k in range(4):
            twice.update({f"xe_in{k}": 4 * NTILE, f"es_out{k}": 4 * NTILE})
        s = {n: ctx.enter_context(nc.semaphore(n)) for n in [*once, *twice]}

        def after(l, name, count):
            return s[name], count + l * twice[name]

        block = ctx.enter_context(nc.Block())

        def settle(eng):
            eng.sem_inc(s[{nc.sync: "passed_sp", nc.vector: "passed_ve"}.get(eng, "passed_po")], 1)

        def no(b):
            return 2 * b[0] + b[1]

        def par(b):
            return b[1] % 2

        def half(b):
            return b[0] + b[1] // 2

        def off(b, d):
            return (b[0], b[1] + d)

        def tno(t):
            return 4 * t[0] + t[1]

        def tq(t):
            return t[0] + t[1] // 4

        def pipeline(eng, prologue, body, epilogue):
            prologue()
            body((0, 0), True, False)
            with eng.Fori(0, 3) as i:
                body((i, 1), True, True)
                body((i, 2), True, True)
            body((0, 7), False, True)
            epilogue((0, 7))

        def steps(eng, step):
            for k in range(4):
                step((0, k), k)
            with eng.Fori(1, NTILE // 4) as i:
                for k in range(4):
                    step((i, k), 4)
            for k in range(3):
                step((0, NTILE + k), NTILE + k)

        def live(known, d):
            return known - d >= 0 and (known < NTILE or known - d < NTILE)

        @block.sync
        def _(sp):
            sp.dma_start(cf[:, :], a["cf"]).then_inc(s["consts_in"], 16)
            sp.dma_start(ct[:, 0, :], a["ctxT"][:, 0:S]).then_inc(s["ctx_in0"], 16)
            sp.dma_start(x_sb[:, 0:4, :], a["x"][0:4 * P, :].rearrange("(t p) d -> p t d", p=P)).then_inc(s["xa_in"], 16)
            sp.dma_start(wv0[:, :], a["wv0"]).then_inc(s["wv_in"], 16)
            sp.dma_start(ct[:, 1, :], a["ctxT"][:, S:2 * S]).then_inc(s["ctx_in1"], 16)
            sp.dma_start(bv_bc[:, :], a["bv"].to_broadcast([P, D])).then_inc(s["wv_in"], 16)
            sp.dma_start(x_sb[:, 4:TT, :], a["x"][4 * P:T, :].rearrange("(t p) d -> p t d", p=P)).then_inc(s["xb_in"], 16)
            sp.dma_start(wr[:, 0, :], a["wr0"]).then_inc(s["wr_in"], 16)
            sp.dma_start(wr[:, 1, :], a["wr1"]).then_inc(s["wr_in"], 16)
            sp.dma_start(br_bc[:, :], a["br"].to_broadcast([P, E])).then_inc(s["wr_in"], 16)
            sp.dma_start(b1t[:, :, :], a["b1t"]).then_inc(s["b1_in"], 16)
            sp.dma_start(b2_bc[:, :], a["b2"].to_broadcast([P, E * D])).then_inc(s["b2_in"], 16)
            sp.dma_start(wo1[:, :, :], a["wo1"]).then_inc(s["wo_in"], 16)
            sp.wait_ge(s["blank_ready"], 1)
            for l in range(2):
                sp.dma_start(xs[l].rearrange("(t p) c -> p t c", p=P),
                             blank[:, None, :].broadcast_to([P, ROWS // P, PAY])).then_inc(s[f"slots_blank{l}"], 16)
            sp.dma_start(w_dn[:, :], a["w2"]).then_inc(s["w2_in"], 16)

            def context(l, c):
                sp.wait_ge(*after(l, "v_psum", (no(c) - 1) * (4 if l else 1)))
                settle(sp)
                sp.wait_ge(*after(l, "ctx_split", no(c) - 1))
                settle(sp)
                sp.dma_start(ct[:, par(c), :], a["ctxT"][:, bass.ds(no(c) * S, S)]).then_inc(s[f"ctx_in{par(c)}"], 16)

            with sp.Fori(0, 3) as i:
                for k in (2, 3):
                    context(0, (i, k))

            def tiles(l):
                sp.wait_ge(*after(l, "table_ready", 1))
                sp.wait_ge(*after(l, "sent0", 16 * QT * TOPK * B // 2))
                sp.wait_ge(*after(l, "sent1", 16 * QT * TOPK * B // 2))
                for k in range(4):
                    row = sp.value_load(tile_row[0:1, l, k:k + 1], min_val=0, max_val=ROWS - P)
                    sp.dma_start(xt[:, k, :], xs[l][bass.ds(row, P), :]).then_inc(s[f"xe_in{k}"], 16)
                with sp.Fori(1, NTILE // 4) as i:
                    for k in range(4):
                        sp.wait_ge(*after(l, "e_x", 4 * i + k - 3))
                        sp.wait_ge(*after(l, "e_dst", 4 * i + k - 3))
                        settle(sp)
                        row = sp.value_load(tile_row[0:1, l, bass.ds(4 * i + k, 1)], min_val=0, max_val=ROWS - P)
                        sp.dma_start(xt[:, k, :], xs[l][bass.ds(row, P), :]).then_inc(s[f"xe_in{k}"], 16)

            def results(l, c):
                for ch in range(TOPK):
                    src = yc[l][bass.ds(ch * T + no(c) * S, S), :].rearrange("(t p) d -> p t d", p=P)
                    sp.dma_start(ybuf[:, par(c), ch, :, :], src).then_inc(s[f"y_in{par(c)}"], 16)

            def all_out(l):
                for k in range(4):
                    sp.wait_ge(*after(l, f"es_out{k}", 16 * (NTILE // 4)))

            tiles(0)
            all_out(0)
            sp.dma_start(w_dn[:, 0:E * C1 * D], a["wd"]).then_inc(s["wd_in"], 16)
            for k in range(2):
                results(0, (0, k))
                sp.dma_start(ct[:, k, :], a["ctxT"][:, k * S:(k + 1) * S]).then_inc(s[f"ctx_in{k}"], 16)
            with sp.Fori(0, 3) as i:
                for k in (2, 3):
                    sp.wait_ge(*after(0, "comb", no((i, k)) - 1))
                    settle(sp)
                    results(0, (i, k))
                    context(1, (i, k))
            tiles(1)
            all_out(1)
            for k in range(2):
                results(1, (0, k))
            with sp.Fori(0, 3) as i:
                for k in (2, 3):
                    sp.wait_ge(*after(1, "comb", no((i, k)) - 1))
                    settle(sp)
                    results(1, (i, k))

        @block.tensor
        def _(pe):
            m = ps[:, 7, :]

            def transpose_x(l, c, free):
                if free:
                    pe.wait_ge(*free)
                pe.wait_ge(*after(l, "xn_ready", no(c) + 1))
                for t in range(QT):
                    tr = pe.transpose(m[:, t * P:(t + 1) * P], xn[:, par(c), t, :], ident)
                tr.then_inc(s["xt_psum"], 1)

            def project0(c, u):
                w, gp = 1 - u % 2, u // 2
                if u == 0:
                    pe.wait_ge(*after(0, "x_split", no(c) + 1))
                    pe.wait_ge(*after(0, "ctx_split", no(c) + 1))
                elif u == 2:
                    pe.wait_ge(s["v_evac"], no(c) + 1)
                else:
                    pe.wait_ge(*after(0, "qk_ready", 4 * no(c) + u))
                sel = cstb("selk" if w else "selq")[0:H, :]
                for gi in range(2):
                    g = 2 * gp + gi
                    o = m[:, gi * S:(gi + 1) * S]
                    for n, (i, j) in enumerate(((0, 0), (1, 0), (0, 1))):
                        pe.matmul(o, wqk[:, w, i, g * P:(g + 1) * P], hl[:, par(c), w, j, :], start=(n == 0), stop=False)
                    mm = pe.matmul(o, sel[:, g * P:(g + 1) * P], maskb[:, bass.ds(no(c), 1), :], start=False, stop=True)
                mm.then_inc(s["qk_psum"], 1)

            def values0(c):
                pe.wait_ge(*after(0, "qk_ready", 4 * no(c) + 2))
                for t in range(QT):
                    mm = pe.matmul(m[:, t * P:(t + 1) * P], ct[:, par(c), t * P:(t + 1) * P], wv0[:, :], start=True, stop=True)
                mm.then_inc(s["v_psum"], 1)

            def scores_q(c, h, first=False):
                g, j = divmod(h, HB)
                if h % 8 == 0:
                    pe.wait_ge(*after(0, "qk_ready", 4 * no(c) + 2 + h // 4))
                if not (first and h < 2):
                    pe.wait_ge(s["a_max"], H * no(c) + h - 1)
                for t in range(QT):
                    mm = pe.matmul(ps[:, h % 2, t * S:(t + 1) * S], qb[32 * j:32 * j + 32, par(c), g, t * P:(t + 1) * P],
                                   kb[32 * j:32 * j + 32, par(c), g, :], start=True, stop=True)
                mm.then_inc(s["a_psum"], 1)

            def transpose_max(c, gp, free):
                pe.wait_ge(*free)
                pe.wait_ge(s["a_max"], H * no(c) + 8 * gp + 8)
                for gi in range(2):
                    for t in range(QT):
                        tr = pe.transpose(m[:, (2 * gi + t) * P:(2 * gi + t + 1) * P], mx0[:, 2 * gp + gi, t, :], ident)
                tr.then_inc(s["mt_psum"], 1)

            def scores_k(b, pp, first):
                if pp % 4 == 0:
                    pe.wait_ge(s["qm_ready"], 2 * no(b) + pp // 4 + 1)
                if not (first and pp < 2):
                    pe.wait_ge(s["b_exp"], 8 * no(b) + pp - 1)
                for e in range(2):
                    g, j = divmod(2 * pp + e, HB)
                    for t in range(QT):
                        mm = pe.matmul(ps[:, 2 + 2 * (pp % 2) + e, t * S:(t + 1) * S],
                                       kb[32 * j:32 * j + 32, par(b), g, t * P:(t + 1) * P],
                                       qb[32 * j:32 * j + 32, par(b), g, :], start=True, stop=True)
                mm.then_inc(s["b_psum"], 1)

            def mix0(b, g, first=False):
                pe.wait_ge(s["b_exp"], 8 * no(b) + 2 * g + 2)
                if g % 2 == 0 and not (first and g == 0):
                    pe.wait_ge(*after(0, "pv_evac", 2 * no(b) + g // 2))
                for t in range(QT):
                    for j in range(HB):
                        h = HB * g + j
                        mm = pe.matmul(ps[32 * j:32 * j + 32, 6, (g % 2) * S:(g % 2 + 1) * S], v0[:, par(b), t, h, :],
                                       pt0[:, h % 8, t * S:(t + 1) * S], start=(t == 0), stop=(t == QT - 1),
                                       skip_group_check=True)
                mm.then_inc(s["pv_psum"], 1)

            def untranspose0(b, t, free):
                if t == 0:
                    pe.wait_ge(*free)
                    pe.wait_ge(*after(0, "pv_evac", 2 * no(b) + 2))
                else:
                    pe.wait_ge(s["o_mul"], 2 * no(b) + 1)
                for g in range(G):
                    tr = pe.transpose(m[:, g * P:(g + 1) * P], ot0[:, par(b), g, t * P:(t + 1) * P], ident)
                tr.then_inc(s["ot_psum"], 1)

            def transpose_t2(l, b, free):
                if free:
                    pe.wait_ge(*free)
                pe.wait_ge(*after(l, "pay_ready", no(b) + 1))
                for t in range(QT):
                    tr = pe.transpose(m[:, t * P:(t + 1) * P], pay[:, par(b), t, 0, 0:D], ident)
                tr.then_inc(s["t2_psum"], 1)

            def logits(l, b, free):
                if free:
                    pe.wait_ge(*free)
                pe.wait_ge(*after(l, "t2_evac", no(b) + 1))
                for t in range(QT):
                    mm = pe.matmul(m[:, t * E:(t + 1) * E], xnt[:, t * P:(t + 1) * P], wr[:, l, :], start=True, stop=True)
                mm.then_inc(s["lg_psum"], 1)

            def prefix(l, b, free):
                if free:
                    pe.wait_ge(*free)
                pe.wait_ge(*after(l, "hotb_done", no(b) + 1))
                tri, ones = cstb("tri"), cstb("ones")
                pe.matmul(m[:, 0:E], tri, hotb[:, 0, :], start=True, stop=True)
                pe.matmul(m[:, E:2 * E], tri, hotb[:, 1, :], start=True, stop=False)
                pe.matmul(m[:, E:2 * E], ones, hotb[:, 0, :], start=False, stop=True)
                pe.matmul(m[:, 2 * E:3 * E], ones, hotb[:, 0, :], start=True, stop=False)
                pe.matmul(m[:, 2 * E:3 * E], ones, hotb[:, 1, :], start=False, stop=True).then_inc(s["pfx_psum"], 1)

            pe.wait_ge(s["consts_in"], 16)
            pe.wait_ge(s["cb_ready"], 1)
            pe.wait_ge(s["wqk_split"], 4)
            pe.wait_ge(s["mask_ready"], 1)
            pe.wait_ge(s["wv_in"], 32)
            pe.wait_ge(s["wr_in"], 48)

            def prologue0():
                c = (0, 0)
                transpose_x(0, c, None)
                project0(c, 0)
                project0(c, 1)
                values0(c)
                project0(c, 2)
                project0(c, 3)
                for h in range(H):
                    scores_q(c, h, first=True)
                transpose_max(c, 0, after(0, "qk_ready", 4))
                transpose_max(c, 1, (s["qm_ready"], 1))

            def body0(b, ahead, behind):
                first = no(b) == 0 if isinstance(b[0], int) else False
                c, d = off(b, 1), off(b, -1)
                kq_done = after(0, "qk_ready", 4 * no(c) + 4)
                if behind:
                    mix0(d, 3)
                if ahead:
                    transpose_x(0, c, (s["qm_ready"], 2 * no(c)))
                    project0(c, 0)
                scores_k(b, 0, first)
                if ahead:
                    project0(c, 1)
                scores_k(b, 1, first)
                if ahead:
                    values0(c)
                scores_k(b, 2, first)
                mix0(b, 0, first)
                if ahead:
                    for h in (0, 1, 2):
                        scores_q(c, h)
                    project0(c, 2)
                scores_k(b, 3, first)
                if ahead:
                    for h in (3, 4, 5):
                        scores_q(c, h)
                    project0(c, 3)
                scores_k(b, 4, first)
                mix0(b, 1)
                if ahead:
                    for h in (6, 7, 8):
                        scores_q(c, h)
                if behind:
                    untranspose0(d, 0, kq_done if ahead else (s["qm_ready"], 2 * B))
                scores_k(b, 5, first)
                if behind:
                    untranspose0(d, 1, None)
                if ahead:
                    for h in (9, 10, 11):
                        scores_q(c, h)
                    transpose_max(c, 0, (s["o_mul"], 2 * no(d) + 2) if behind else kq_done)
                scores_k(b, 6, first)
                mix0(b, 2)
                if ahead:
                    for h in (12, 13, 14):
                        scores_q(c, h)
                if behind:
                    transpose_t2(0, d, (s["qm_ready"], 2 * no(c) + 1) if ahead else (s["o_mul"], 2 * no(d) + 2))
                scores_k(b, 7, first)
                if behind:
                    logits(0, d, None)
                if ahead:
                    scores_q(c, 15)
                if behind:
                    prefix(0, d, None)
                if ahead:
                    transpose_max(c, 1, after(0, "pos_done", no(d) + 1) if behind else (s["qm_ready"], 2 * no(c) + 1))

            def epilogue0(b):
                mix0(b, 3)
                untranspose0(b, 0, after(0, "pos_done", no(b)))
                untranspose0(b, 1, None)
                transpose_t2(0, b, (s["o_mul"], 2 * no(b) + 2))
                logits(0, b, None)
                prefix(0, b, None)

            pipeline(pe, prologue0, body0, epilogue0)

            def experts(l):
                pe.wait_ge(*after(l, "table_ready", 1))
                pe.wait_ge(s["wup_split"], E if l == 0 else 3 * E)
                pe.wait_ge(s["wd_in" if l else "w2_in"], 16)
                pe.wait_ge(*after(l, "pos_done", B))
                if l == 1:
                    pe.wait_ge(s["he_pad"], 1)
                cc, ff = (C1, F1) if l else (C0, F0)

                def expert(t):
                    return pe.value_load(tile_e[0:1, l, bass.ds(tno(t), 1)], min_val=0, max_val=E - 1)

                def step(t, known):
                    if live(known, 0):
                        pe.wait_ge(*after(l, f"xe_in{t[1] % 4}", 16 * (tq(t) + 1)))
                        if known:
                            pe.wait_ge(*after(l, "e_xlo", tno(t)))
                        pe.transpose(ps[:, 0, 0:P], xt[:, t[1] % 4, 0:D], ident).then_inc(s["e_x"], 1)
                    if live(known, 1):
                        u = off(t, -1)
                        e = expert(u)
                        pe.wait_ge(*after(l, "e_xlo", tno(u) + 1))
                        if known > 2:
                            pe.wait_ge(*after(l, "e_hcopy", tno(u) - 1))
                        for half_ in range(2 if l else 1):
                            bk = 1 + 2 * par(u) + half_ if l else 1 + par(u)
                            for n, (i, j) in enumerate(((0, 0), (1, 0), (0, 1))):
                                w = w_up[:, bass.ds(e * (ff * (4 if l else 2)) + (2 * half_ + j) * ff, ff)]
                                mm = pe.matmul(ps[:, bk, 0:ff], ex[:, par(u), i, :], w, start=(n == 0), stop=(n == 2))
                        mm.then_inc(s["e_h"], 1)
                    if live(known, 2):
                        u = off(t, -2)
                        pe.wait_ge(*after(l, "e_hcopy", tno(u) + 1))
                        if known > 3:
                            pe.wait_ge(*after(l, "e_htev" if l else "e_hb", tno(u) - 1))
                        for k in range(cc):
                            tr = pe.transpose(ps[:, 5 + par(u), k * P:(k + 1) * P], he[:, par(u), k * P:(k + 1) * P], ident)
                        tr.then_inc(s["e_ht"], 1)
                    if live(known, 3):
                        u = off(t, -3)
                        e = expert(u)
                        pe.wait_ge(*after(l, "e_htev", tno(u) + 1))
                        if known > 3:
                            pe.wait_ge(*after(l, "e_yev", tno(u)))
                        for k in range(cc):
                            mm = pe.matmul(ps[:, 7, 0:D], ht[:, par(u), k * P:(k + 1) * P],
                                           w_dn[:, bass.ds(e * (cc * D) + k * D, D)], start=(k == 0), stop=(k == cc - 1))
                        mm.then_inc(s["e_y"], 1)

                steps(pe, step)

            experts(0)

            def project1(c, u):
                w, mm_ = u // 4, 2 * (u % 4)
                if u == 0:
                    pe.wait_ge(*after(1, "x_split", no(c) + 1))
                if u == 4:
                    pe.wait_ge(*after(1, "ctx_split", no(c) + 1))
                for k in range(2):
                    for n, (i, j) in enumerate(((0, 0), (1, 0), (0, 1))):
                        mm = pe.matmul(m[:, k * S:(k + 1) * S], w1p[:, w, i, (mm_ + k) * P:(mm_ + k + 1) * P],
                                       hl[:, par(c), w, j, :], start=(n == 0), stop=(n == 2))
                mm.then_inc(s["qk_psum"], 1)

            def project1_after(c, u, free):
                if free:
                    pe.wait_ge(*free)
                project1(c, u)

            def values1(c, n, free):
                t, hf = divmod(n, 2)
                pe.wait_ge(*free)
                for k, (i, j) in enumerate(((0, 0), (1, 0), (0, 1))):
                    mm = pe.matmul(m[:, :], hl[:, par(c), 1, i, t * P:(t + 1) * P], w1p[:, 2, j, hf * 512:(hf + 1) * 512],
                                   start=(k == 0), stop=(k == 2))
                mm.then_inc(s["v_psum"], 1)

            def scores1(b, pp, first):
                if pp == 0:
                    pe.wait_ge(*after(1, "qk_ready", 8 * no(b) + 8))
                if not (first and pp < 2):
                    pe.wait_ge(s["s_exp"], 8 * no(b) + pp - 1)
                for e in range(2):
                    bk = ps[:, 2 * (pp % 2) + e, :]
                    rows = slice(64 * e, 64 * e + 64)
                    pe.matmul(bk[:, 0:P], qt1[rows, par(b), pp, 0:P], kt1[rows, par(b), pp, 0:P],
                              start=True, stop=True, skip_group_check=True)
                    pe.matmul(bk[:, P:3 * P], qt1[rows, par(b), pp, P:2 * P], kt1[rows, par(b), pp, :],
                              start=False, stop=True, skip_group_check=True)
                    mm = pe.matmul(bk[:, 0:3 * P].rearrange("p (c n) -> p c n", c=3)[:, 0:3:2, :], cstb("ident"),
                                   cstb("causal").rearrange("p (c n) -> p c n", c=2), start=False, stop=True,
                                   skip_group_check=True)
                mm.then_inc(s["s_psum"], 1)

            def turn1(b, pp, first):
                n = 8 * no(b) + pp
                pe.wait_ge(s["s_norm"], n + 1)
                if not (first and pp == 0):
                    pe.wait_ge(s["pt_evac"], n)
                for e in range(2):
                    for k in range(3):
                        tr = pe.transpose(ps[:, 4 + e, k * P:(k + 1) * P], p1[:, pp % 2, e, k * P:(k + 1) * P], ident)
                tr.then_inc(s["pt_psum"], 1)

            def mix1(b, pp, first):
                n = 8 * no(b) + pp
                pe.wait_ge(s["pt_evac"], n + 1)
                if pp == 0:
                    pe.wait_ge(s["v1_evac"], 4 * no(b) + 4)
                if pp % 2 == 0 and not (first and pp == 0):
                    pe.wait_ge(*after(1, "pv_evac", 4 * no(b) + pp // 2))
                c0 = (pp % 2) * S
                for e in range(2):
                    pe.matmul(ps[64 * e:64 * e + 64, 6, c0:c0 + S], v1[:, par(b), 0, (2 * pp + e) * DK1:(2 * pp + e + 1) * DK1],
                              pt1[:, pp % 2, e, 0:S], start=True, stop=False, skip_group_check=True)
                for e in range(2):
                    mm = pe.matmul(ps[64 * e:64 * e + 64, 6, c0 + P:c0 + S],
                                   v1[:, par(b), 1, (2 * pp + e) * DK1:(2 * pp + e + 1) * DK1],
                                   pt1[:, pp % 2, e, S:3 * P], start=False, stop=True, skip_group_check=True)
                mm.then_inc(s["pv_psum"], 1)

            def output1(b, free):
                pe.wait_ge(*free)
                pe.wait_ge(*after(1, "pv_evac", 4 * no(b) + 4))
                for t in range(QT):
                    for k in range(M1):
                        mm = pe.matmul(m[:, t * P:(t + 1) * P], ot1[:, k, t * P:(t + 1) * P], wo1[:, k, :],
                                       start=(k == 0), stop=(k == M1 - 1))
                mm.then_inc(s["op_psum"], 1)

            pe.wait_ge(s["wl_split"], 3)
            pe.wait_ge(s["wo_in"], 16)
            pe.wait_ge(*after(0, "e_yev", NTILE))

            def qk(c, u):
                return after(1, "qk_ready", 8 * no(c) + u)

            def vv(c, n):
                return (s["v1_evac"], 4 * no(c) + n)

            def prologue1():
                c = (0, 0)
                transpose_x(1, c, None)
                for u in range(8):
                    project1_after(c, u, qk(c, u) if u else None)
                for n in range(4):
                    values1(c, n, vv(c, n) if n else qk(c, 8))

            def body1(b, ahead, behind):
                first = no(b) == 0 if isinstance(b[0], int) else False
                c, d = off(b, 1), off(b, -1)
                if behind:
                    turn1(d, 6, False)
                scores1(b, 0, first)
                if ahead:
                    transpose_x(1, c, vv(c, 0))
                    project1_after(c, 0, None)
                if behind:
                    mix1(d, 6, False)
                    turn1(d, 7, False)
                scores1(b, 1, first)
                if ahead:
                    project1_after(c, 1, qk(c, 1))
                    project1_after(c, 2, qk(c, 2))
                if behind:
                    mix1(d, 7, False)
                turn1(b, 0, first)
                scores1(b, 2, first)
                if ahead:
                    project1_after(c, 3, qk(c, 3))
                if behind:
                    output1(d, qk(c, 4) if ahead else (s["v1_evac"], 4 * B))
                mix1(b, 0, first)
                turn1(b, 1, first)
                scores1(b, 3, first)
                if ahead:
                    project1_after(c, 4, after(1, "x_add", 2 * no(d) + 2) if behind else qk(c, 4))
                    project1_after(c, 5, qk(c, 5))
                mix1(b, 1, first)
                turn1(b, 2, first)
                scores1(b, 4, first)
                if ahead:
                    project1_after(c, 6, qk(c, 6))
                if behind:
                    transpose_t2(1, d, qk(c, 7) if ahead else None)
                mix1(b, 2, first)
                turn1(b, 3, first)
                scores1(b, 5, first)
                if ahead:
                    project1_after(c, 7, after(1, "t2_evac", no(d) + 1) if behind else qk(c, 7))
                if behind:
                    logits(1, d, qk(c, 8) if ahead else None)
                if ahead:
                    values1(c, 0, after(1, "lg_done", no(d) + 1) if behind else qk(c, 8))
                mix1(b, 3, first)
                turn1(b, 4, first)
                scores1(b, 6, first)
                if behind:
                    prefix(1, d, vv(c, 1) if ahead else None)
                if ahead:
                    values1(c, 1, after(1, "pos_done", no(d) + 1) if behind else vv(c, 1))
                mix1(b, 4, first)
                turn1(b, 5, first)
                scores1(b, 7, first)
                if ahead:
                    values1(c, 2, vv(c, 2))
                    values1(c, 3, vv(c, 3))
                mix1(b, 5, first)

            def epilogue1(b):
                for pp in (6, 7):
                    turn1(b, pp, False)
                    mix1(b, pp, False)
                output1(b, after(1, "pos_done", no(b)))
                transpose_t2(1, b, None)
                logits(1, b, None)
                prefix(1, b, None)

            pipeline(pe, prologue1, body1, epilogue1)
            experts(1)

        @block.scalar
        def _(act):
            act.dma_start(stage[:, 0, :], a["wqk"]).then_inc(s["wqk_in"], 16)
            act.dma_start(bias0[:, :, :], a["bias0"]).then_inc(s["bias_in"], 16)
            act.dma_start(maskraw, a["mask"]).then_inc(s["mask_in"], 16)
            m = ps[:, 7, :]

            def x_high(l, c):
                act.wait_ge(*after(l, "xt_psum", no(c) + 1))
                act.activation(hl[:, par(c), 0, 0, :], m[:, 0:S], ACT.Copy).then_inc(s["x_hi"], 1)

            def low_base(c, u):
                w, gp = 1 - u % 2, u // 2
                act.wait_ge(*after(0, "qk_psum", 4 * no(c) + u + 1))
                if not (isinstance(c[0], int) and no(c) == 0 and u == 0):
                    act.wait_ge(*after(0, "qk_ready", 4 * no(c) + u))
                for gi in range(2):
                    g = 2 * gp + gi
                    ac = act.activation(chib[:, gi, :], m[:, gi * S:(gi + 1) * S], ACT.Identity,
                                        bias=bias0c[:, w, g:g + 1], scale=cst("ck" if w else "cq"))
                ac.then_inc(s["qk_chi"], 1)

            def exps0(b, pp, first):
                act.wait_ge(s["b_psum"], 8 * no(b) + pp + 1)
                if not (first and pp < 4):
                    act.wait_ge(*after(0, "pv_psum", 4 * no(b) + pp // 2 - 1))
                b0 = 2 + 2 * (pp % 2)
                act.activation(pt0[:, (2 * pp) % 8:(2 * pp) % 8 + 2, :], ps[:, b0:b0 + 2, :], ACT.Exp, scale=SC0).then_inc(s["b_exp"], 1)

            def take_out0(b, hf):
                act.wait_ge(*after(0, "pv_psum", 4 * no(b) + 2 * hf + 2))
                act.activation(ot0[:, par(b), 2 * hf:2 * hf + 2, :], ps[:, 6, :].rearrange("p (g n) -> p g n", g=2),
                               ACT.Copy).then_inc(s["pv_evac"], 1)

            def t2_out(l, b):
                act.wait_ge(*after(l, "t2_psum", no(b) + 1))
                act.activation(xnt[:, :], m[:, 0:S], ACT.Copy).then_inc(s["t2_evac"], 1)

            def weight_exp(l, b):
                act.wait_ge(*after(l, "diff_done", no(b) + 1))
                act.activation(edl[:, :], dlt[:, :], ACT.Exp).then_inc(s["exp_done"], 1)

            act.wait_ge(s["consts_in"], 16)
            act.wait_ge(s["bias_ready"], 2)

            def prologue0():
                c = (0, 0)
                x_high(0, c)
                for u in range(4):
                    low_base(c, u)

            def body0(b, ahead, behind):
                first = no(b) == 0 if isinstance(b[0], int) else False
                c, d = off(b, 1), off(b, -1)
                if behind:
                    take_out0(d, 1)
                if ahead:
                    x_high(0, c)
                    low_base(c, 0)
                exps0(b, 0, first)
                if ahead:
                    low_base(c, 1)
                exps0(b, 1, first)
                exps0(b, 2, first)
                if ahead:
                    low_base(c, 2)
                exps0(b, 3, first)
                if ahead:
                    low_base(c, 3)
                exps0(b, 4, first)
                take_out0(b, 0)
                exps0(b, 5, first)
                exps0(b, 6, first)
                if behind:
                    t2_out(0, d)
                exps0(b, 7, first)
                if behind:
                    weight_exp(0, d)

            def epilogue0(b):
                take_out0(b, 1)
                t2_out(0, b)
                weight_exp(0, b)

            pipeline(act, prologue0, body0, epilogue0)

            def experts(l):
                def step(t, known):
                    if live(known, 0):
                        act.wait_ge(*after(l, "e_x", tno(t) + 1))
                        if known > 1:
                            act.wait_ge(*after(l, "e_h", tno(t) - 1))
                        act.activation(ex[:, par(t), 0, :], ps[:, 0, 0:P], ACT.Copy).then_inc(s["e_xhi"], 1)
                    if live(known, 1):
                        u = off(t, -1)
                        act.wait_ge(*after(l, "e_h", tno(u) + 1))
                        if l == 0:
                            if known > 2:
                                act.wait_ge(*after(l, "e_ht", tno(u) - 1))
                            act.activation(he[:, par(u), :], ps[:, 1 + par(u), :], ACT.Copy).then_inc(s["e_hcopy"], 1)
                        else:
                            if known > 2:
                                act.wait_ge(*after(l, "e_hcopy", tno(u) - 1))
                            act.activation(sg[:, par(u), :], ps[:, 1 + 2 * par(u), 0:F1], ACT.Silu).then_inc(s["e_hs"], 1)

                steps(act, step)

            experts(0)

            for w in range(3):
                act.wait_ge(s[f"st_in{w % 2}"], 16 * (1 + E // 2 + 1 + w // 2))
                act.activation(w1p[:, w, 0, :], stage[:, w % 2, :], ACT.Copy).then_inc(s["wl_hi"], 1)

            def qk_out(c, u):
                act.wait_ge(*after(1, "qk_psum", 8 * no(c) + u + 1))
                dst = (kt1 if u // 4 else qt1)[:, par(c), 2 * (u % 4):2 * (u % 4) + 2, :]
                act.activation(dst, m.rearrange("p (k n) -> p k n", k=2), ACT.Copy).then_inc(s["qk_ready"], 1)

            def exps1(b, pp, first):
                n = 8 * no(b) + pp
                act.wait_ge(s["s_nb"], n + 1)
                if not (first and pp < 2):
                    act.wait_ge(s["pt_psum"], n - 1)
                    act.wait_ge(s["s_rec"], n - 1)
                for e in range(2):
                    bk = ps[:, 2 * (pp % 2) + e, :]
                    for t, cols in ((0, slice(0, P)), (1, slice(P, 3 * P))):
                        ac = act.activation(p1[:, pp % 2, e, cols], bk[:, cols], ACT.Exp, scale=SC1,
                                            bias=nb1[:, pp % 2, e, t:t + 1], accum_out=rs1[:, pp % 2, e, t:t + 1])
                ac.then_inc(s["s_exp"], 1)

            def take_out1(b, k, first=False):
                act.wait_ge(*after(1, "pv_psum", 8 * no(b) + 2 * k + 2))
                if k == 0 and not first:
                    act.wait_ge(s["op_psum"], no(b))
                act.activation(ot1[:, 2 * k:2 * k + 2, :], ps[:, 6, :].rearrange("p (k n) -> p k n", k=2),
                               ACT.Copy).then_inc(s["pv_evac"], 1)

            def prologue1():
                c = (0, 0)
                x_high(1, c)
                for u in range(8):
                    qk_out(c, u)

            def body1(b, ahead, behind):
                first = no(b) == 0 if isinstance(b[0], int) else False
                c, d = off(b, 1), off(b, -1)
                if ahead:
                    x_high(1, c)
                    qk_out(c, 0)
                exps1(b, 0, first)
                if ahead:
                    qk_out(c, 1)
                    qk_out(c, 2)
                exps1(b, 1, first)
                if behind:
                    take_out1(d, 3)
                if ahead:
                    qk_out(c, 3)
                exps1(b, 2, first)
                if ahead:
                    qk_out(c, 4)
                    qk_out(c, 5)
                exps1(b, 3, first)
                take_out1(b, 0, first)
                if ahead:
                    qk_out(c, 6)
                if behind:
                    t2_out(1, d)
                exps1(b, 4, first)
                if ahead:
                    qk_out(c, 7)
                exps1(b, 5, first)
                take_out1(b, 1)
                if behind:
                    weight_exp(1, d)
                exps1(b, 6, first)
                exps1(b, 7, first)
                take_out1(b, 2)

            def epilogue1(b):
                take_out1(b, 3)
                t2_out(1, b)
                weight_exp(1, b)

            pipeline(act, prologue1, body1, epilogue1)
            experts(1)

            def store(c):
                act.wait_ge(*after(1, "comb", no(c) + 1))
                dst = out[bass.ds(no(c) * S, S), :].rearrange("(t p) d -> p t d", p=P)
                act.dma_start(dst, x_sb[:, bass.ds(QT * no(c), QT), :]).then_inc(s[f"out_done{par(c)}"], 16)

            with act.Fori(0, B // 2) as i:
                store((i, 0))
                store((i, 1))
            act.wait_ge(s["out_done0"], 16 * B // 2)
            act.wait_ge(s["out_done1"], 16 * B // 2)

        @block.vector
        def _(ve):
            m = ps[:, 7, :]

            def stats(l, c, z):
                n0 = 4 * no(c)
                settle(ve)
                for t in range(QT):
                    ve.bn_stats(bn6[:, z, t, :], tokens(c, t)).then_inc(s[f"ln_stats{z}"], 1)
                ve.wait_ge(*after(l, f"ln_stats{z}", n0 + 2))
                settle(ve)
                for t in range(QT):
                    ve.bn_aggr(mv[:, z, t, :], bn6[:, z, t, :]).then_inc(s[f"ln_stats{z}"], 1)

            def normalise(l, c, z, dst, ready):
                ve.wait_ge(*after(l, f"rs_ready{z}", no(c) + 1))
                for t in range(QT):
                    op = ve.tensor_scalar(dst(t), tokens(c, t), mv[:, z, t, 0:1], rstd[:, z, t:t + 1], ALU.subtract, ALU.mult)
                op.then_inc(s[ready], 1)
                ve.wait_ge(*after(l, ready, no(c) + 1))

            def tokens(b, t):
                return x_sb[:, bass.ds(QT * no(b) + t, 1), :].rearrange("p a d -> p (a d)")

            def norm_in(l, c, used=True):
                if used:
                    ve.wait_ge(*after(l, "xt_psum", no(c) - 1))
                normalise(l, c, 0, lambda t: xn[:, par(c), t, :], "xn_ready")

            def norm_out(l, b, used):
                if used:
                    ve.wait_ge(*after(l, f"sent{par(b)}", 16 * QT * TOPK * half(b)))
                normalise(l, b, 1, lambda t: pay[:, par(b), t, 0, 0:D], "pay_ready")

            def x_low(l, c):
                ve.wait_ge(*after(l, "x_hi", no(c) + 1))
                ve.tensor_tensor(hl[:, par(c), 0, 1, :], m[:, 0:S], hl[:, par(c), 0, 0, :], ALU.subtract).then_inc(s["x_split"], 1)

            def qk0(c, u):
                w, gp = 1 - u % 2, u // 2
                ve.wait_ge(s["qk_chi"], 4 * no(c) + u + 1)
                for gi in range(2):
                    g = 2 * gp + gi
                    op = ve.scalar_tensor_tensor(out=(kb if w else qb)[:, par(c), g, :], in0=m[:, gi * S:(gi + 1) * S],
                                                 scalar=bias0[:, w, g:g + 1], in1=chib[:, gi, :],
                                                 op0=ALU.add, op1=ALU.subtract)
                op.then_inc(s["qk_ready"], 1)

            def values0(c):
                ve.wait_ge(*after(0, "v_psum", no(c) + 1))
                for t in range(QT):
                    op = ve.tensor_tensor(v0[:, par(c), t, :, 0:DK0], m[:, t * P:(t + 1) * P].rearrange("p (h n) -> p h n", h=H),
                                          bv_bc[:, :].rearrange("p (h n) -> p h n", h=H), ALU.add)
                op.then_inc(s["v_evac"], 1)

            def row_max(c, h, first=False):
                g, j = divmod(h, HB)
                ve.wait_ge(s["a_psum"], H * no(c) + h + 1)
                if h % 8 == 0 and not first:
                    ve.wait_ge(s["mt_psum"], 2 * no(c) - 1 + h // 8)
                ve.tensor_reduce(mx0[:, g, :, 32 * j + 26], ps[:, h % 2, :].rearrange("p (t n) -> p t n", t=QT), AX, ALU.max).then_inc(s["a_max"], 1)

            def place_max(c, gp):
                ve.wait_ge(s["mt_psum"], 2 * no(c) + gp + 1)
                q = qb[:, par(c), 2 * gp:2 * gp + 2, :]
                ve.scalar_tensor_tensor(out=q, in0=m.rearrange("p (g n) -> p g n", g=2), scalar=-1.0, in1=q,
                                        op0=ALU.mult, op1=ALU.add).then_inc(s["qm_ready"], 1)

            def attend0(b, t):
                n = 2 * no(b) + t
                o = m.rearrange("p (h n) -> p h n", h=H)
                ve.wait_ge(s["ot_psum"], n + 1)
                ve.reciprocal(rec0[:, :], o[:, :, DK0]).then_inc(s["o_rec"], 1)
                ve.wait_ge(s["o_rec"], n + 1)
                ve.tensor_tensor(att0[:, :, :], o[:, :, 0:DK0], rec0[:, :, None].broadcast_to([P, H, DK0]), ALU.mult).then_inc(s["o_mul"], 1)
                ve.wait_ge(s["o_mul"], n + 1)
                ve.tensor_tensor(tokens(b, t), tokens(b, t), att0[:, :, :].rearrange("p h n -> p (h n)"), ALU.add).then_inc(s["x_add"], 1)
                ve.wait_ge(*after(0, "x_add", n + 1))

            def choose(l, b):
                n = no(b)
                ve.wait_ge(*after(l, "lg_psum", n + 1))
                src = m[:, 0:QT * E].rearrange("p (t e) -> p t e", t=QT)
                if l == 0:
                    ve.tensor_tensor(lg[:, :, :], src, br_bc[:, None, :].broadcast_to([P, QT, E]), ALU.add).then_inc(s["lg_done"], 1)
                else:
                    ve.tensor_copy(lg[:, :, :], src).then_inc(s["lg_done"], 1)
                ve.wait_ge(*after(l, "lg_done", n + 1))
                settle(ve)
                for t in range(QT):
                    ve.max(top[:, t, :], lg[:, t, :]).then_inc(s["top_done"], 1)
                ve.wait_ge(*after(l, "top_done", 5 * n + 2))
                settle(ve)
                for t in range(QT):
                    ve.max_index(topi[:, t, :], top[:, t, :], lg[:, t, :]).then_inc(s["top_done"], 1)
                ve.tensor_tensor(dlt[:, :], top[:, :, 1], top[:, :, 0], ALU.subtract).then_inc(s["diff_done"], 1)
                ve.wait_ge(*after(l, "top_done", 5 * n + 4))
                ve.tensor_copy(topf[:, :, :], topi[:, :, 0:TOPK]).then_inc(s["top_done"], 1)
                ve.wait_ge(*after(l, "top_done", 5 * n + 5))
                ve.tensor_tensor(hot[:, :, :, :].rearrange("p t c e -> p (t c) e"),
                                 cst("choice")[:, None, 0:E].broadcast_to([P, QT * TOPK, E]),
                                 topf[:, :, :].rearrange("p t c -> p (t c)")[:, :, None].broadcast_to([P, QT * TOPK, E]),
                                 ALU.is_equal).then_inc(s["hot_done"], 1)
                ve.wait_ge(*after(l, "hot_done", n + 1))
                ve.tensor_tensor(hotb[:, :, :], hot[:, :, 0, :], hot[:, :, 1, :], ALU.add).then_inc(s["hotb_done"], 1)

            def weigh(l, b):
                n = no(b)
                ve.wait_ge(*after(l, "exp_done", n + 1))
                ve.tensor_scalar(den[:, :], edl[:, :], 1.0, None, ALU.add).then_inc(s["wts_den"], 1)
                ve.wait_ge(*after(l, "wts_den", n + 1))
                w = wts[:, l, bass.ds(QT * n, QT), :]
                ve.reciprocal(w[:, :, 0], den[:, :]).then_inc(s["wts_one"], 1)
                ve.wait_ge(*after(l, "wts_one", n + 1))
                ve.tensor_tensor(w[:, :, 1], edl[:, :], w[:, :, 0], ALU.mult).then_inc(s["wts_done"], 1)

            def place(l, b):
                n = no(b)
                ve.wait_ge(*after(l, "pfx_psum", n + 1))
                bs = base[:, l, :]
                ve.tensor_tensor(pos[:, :, :], m[:, 0:QT * E].rearrange("p (t e) -> p t e", t=QT),
                                 bs[:, None, :].broadcast_to([P, QT, E]), ALU.add).then_inc(s["slot_chain"], 1)
                ve.wait_ge(*after(l, "slot_chain", 3 * n + 1))
                ve.tensor_tensor(bs, bs, m[:, QT * E:(QT + 1) * E], ALU.add).then_inc(s["pos_done"], 1)
                ve.tensor_tensor(hp[:, :, :, :], hot[:, :, :, :], pos[:, :, None, :].broadcast_to([P, QT, TOPK, E]),
                                 ALU.mult).then_inc(s["slot_chain"], 1)
                ve.wait_ge(*after(l, "slot_chain", 3 * n + 2))
                ve.tensor_reduce(slotf[:, :, :], hp[:, :, :, :], AX, ALU.add).then_inc(s["slot_chain"], 1)
                ve.wait_ge(*after(l, "slot_chain", 3 * n + 3))
                ve.tensor_copy(sloti[:, par(b), :, :], slotf[:, :, :]).then_inc(s["slot_ready"], 1)
                ve.wait_ge(*after(l, "pos_done", n + 1))

            def table(l):
                k = 0

                def link(op):
                    nonlocal k
                    k += 1
                    op.then_inc(s["table"], 1)
                    ve.wait_ge(*after(l, "table", k))

                one = slice(0, 1)
                link(ve.tensor_tensor(cnt[:, :], base[one, l, :], cst("region")[one, :], ALU.subtract))
                link(ve.tensor_tensor(lots[:, :, :], cnt[:, :, None].broadcast_to([1, E, T // P]),
                                      cst("lots")[one, None, :].broadcast_to([1, E, T // P]), ALU.is_gt))
                link(ve.tensor_reduce(ntl[:, :], lots[:, :, :], AX, ALU.add))
                link(ve.tensor_tensor_scan(ends[:, :], cst("one8")[one, :], ntl[:, :], 0.0, ALU.mult, ALU.add))
                link(ve.tensor_tensor(past[:, :, :], cst("tile")[one, :, None].broadcast_to([1, NTILE, E]),
                                      ends[:, None, :].broadcast_to([1, NTILE, E]), ALU.is_ge))
                link(ve.tensor_reduce(which[:, :], past[:, :, :], AX, ALU.add))
                link(ve.tensor_tensor(pastn[:, :, :], past[:, :, :], ntl[:, None, :].broadcast_to([1, NTILE, E]), ALU.mult))
                link(ve.tensor_reduce(before[:, :], pastn[:, :, :], AX, ALU.add))
                link(ve.tensor_tensor(before[:, :], cst("tile")[one, :], before[:, :], ALU.subtract))
                link(ve.tensor_scalar(before[:, :], before[:, :], float(P), None, ALU.mult))
                link(ve.scalar_tensor_tensor(out=before[:, :], in0=which[:, :], scalar=float(T), in1=before[:, :],
                                             op0=ALU.mult, op1=ALU.add))
                link(ve.tensor_copy(tile_row[:, l, :], before[:, :]))
                link(ve.tensor_scalar(which[:, :], which[:, :], float(E - 1), None, ALU.min))
                ve.tensor_copy(tile_e[:, l, :], which[:, :]).then_inc(s["table_ready"], 1)
                ve.wait_ge(*after(l, "table_ready", 1))

            ve.wait_ge(s["consts_in"], 16)
            ve.wait_ge(s["bias_in"], 16)
            for w, c in ((0, "cq"), (1, "ck")):
                ve.tensor_scalar(bias0c[:, w, :], bias0[:, w, :], cst(c), None, ALU.mult).then_inc(s["bias_ready"], 1)
            for l in range(2):
                ve.tensor_copy(base[:, l, :], cst("region")).then_inc(s["base_set"], 1)
            ve.memset(mx0[:, :, :, :].rearrange("p g t n -> p (g t n)"), 0.0).then_inc(s["mx_clear"], 1)
            ve.wait_ge(s["mx_clear"], 1)
            ve.wait_ge(s["xa_in"], 16)

            def prologue0():
                c = (0, 0)
                stats(0, c, 0)
                norm_in(0, c, False)
                x_low(0, c)
                stats(0, (0, 1), 0)
                qk0(c, 0)
                qk0(c, 1)
                ve.wait_ge(s["wv_in"], 32)
                ve.wait_ge(s["v0_ready"], 1)
                values0(c)
                qk0(c, 2)
                qk0(c, 3)
                for h in range(H):
                    row_max(c, h, True)
                place_max(c, 0)
                place_max(c, 1)
                norm_in(0, (0, 1), False)
                ve.wait_ge(s["xb_in"], 16)
                ve.wait_ge(s["wr_in"], 48)
                ve.wait_ge(s["base_set"], 2)

            def body0(b, ahead, behind, more=True):
                c, d = off(b, 1), off(b, -1)
                if ahead:
                    x_low(0, c)
                    qk0(c, 0)
                    qk0(c, 1)
                    if more:
                        stats(0, off(b, 2), 0)
                    values0(c)
                    for h in (0, 1, 2):
                        row_max(c, h)
                    qk0(c, 2)
                    for h in (3, 4, 5):
                        row_max(c, h)
                    qk0(c, 3)
                    for h in (6, 7, 8):
                        row_max(c, h)
                if behind:
                    attend0(d, 0)
                    attend0(d, 1)
                    stats(0, d, 1)
                if ahead:
                    for h in (9, 10, 11):
                        row_max(c, h)
                    place_max(c, 0)
                if behind:
                    norm_out(0, d, not (isinstance(d[0], int) and no(d) < 2))
                if ahead:
                    for h in (12, 13, 14):
                        row_max(c, h)
                if behind:
                    choose(0, d)
                if ahead:
                    row_max(c, 15)
                if behind:
                    place(0, d)
                    weigh(0, d)
                if ahead:
                    place_max(c, 1)

            def next_norm(l, b):
                norm_in(l, off(b, 2))

            def epilogue0(b):
                attend0(b, 0)
                attend0(b, 1)
                stats(0, b, 1)
                norm_out(0, b, True)
                choose(0, b)
                place(0, b)
                table(0)
                weigh(0, b)

            prologue0()
            body0((0, 0), True, False)
            next_norm(0, (0, 0))
            with ve.Fori(0, 2) as i:
                for k in (1, 2):
                    body0((i, k), True, True)
                    next_norm(0, (i, k))
            body0((0, 5), True, True)
            next_norm(0, (0, 5))
            body0((0, 6), True, True, False)
            body0((0, 7), False, True, False)
            epilogue0((0, 7))

            def experts(l):
                if l == 0:
                    ve.wait_ge(s["b1_in"], 16)
                    ve.wait_ge(s["b2_in"], 16)
                else:
                    ve.memset(he[:, :, F1:FP1], 0.0).then_inc(s["he_pad"], 1)

                def expert(t):
                    return ve.value_load(tile_e[0:1, l, bass.ds(tno(t), 1)], min_val=0, max_val=E - 1)

                def step(t, known):
                    if live(known, 0):
                        ve.wait_ge(*after(l, "e_xhi", tno(t) + 1))
                        ve.tensor_tensor(ex[:, par(t), 1, :], ps[:, 0, 0:P], ex[:, par(t), 0, :], ALU.subtract).then_inc(s["e_xlo"], 1)
                    if l == 1 and live(known, 1):
                        u = off(t, -1)
                        ve.wait_ge(*after(l, "e_hs", tno(u) + 1))
                        if known > 2:
                            ve.wait_ge(*after(l, "e_ht", tno(u) - 1))
                        ve.tensor_tensor(he[:, par(u), 0:F1], sg[:, par(u), :], ps[:, 2 + 2 * par(u), 0:F1], ALU.mult).then_inc(s["e_hcopy"], 1)
                    if live(known, 2):
                        u = off(t, -2)
                        if l == 0:
                            e = expert(u)
                            ve.wait_ge(*after(l, "e_ht", tno(u) + 1))
                            if known > 3:
                                ve.wait_ge(*after(l, "e_htev", tno(u) - 1))
                            bias = b1t[:, bass.ds(e, 1), :].rearrange("p a c -> p (a c)")[:, :, None].broadcast_to([P, C0, P])
                            ve.tensor_tensor(hb[:, par(u), :].rearrange("p (c n) -> p c n", c=C0),
                                             ps[:, 5 + par(u), :].rearrange("p (c n) -> p c n", c=C0), bias, ALU.add).then_inc(s["e_hb"], 1)
                        else:
                            ve.wait_ge(*after(l, "e_ht", tno(u) + 1))
                            if known > 3:
                                ve.wait_ge(*after(l, "e_y", tno(u) - 1))
                            ve.tensor_copy(ht[:, par(u), 0:FP1], ps[:, 5 + par(u), 0:FP1]).then_inc(s["e_htev"], 1)
                    if live(known, 3):
                        u = off(t, -3)
                        if l == 0:
                            e = expert(u)
                        ve.wait_ge(*after(l, "e_y", tno(u) + 1))
                        if not (known < 4 or (isinstance(u[0], int) and tno(u) < 4)):
                            ve.wait_ge(*after(l, f"es_out{u[1] % 4}", 16 * tq(u)))
                        if l == 0:
                            ve.tensor_tensor(ye[:, u[1] % 4, :], ps[:, 7, 0:D], b2_bc[:, bass.ds(e * D, D)], ALU.add).then_inc(s["e_yev"], 1)
                        else:
                            ve.tensor_copy(ye[:, u[1] % 4, :], ps[:, 7, 0:D]).then_inc(s["e_yev"], 1)

                steps(ve, step)

            experts(0)

            for w in range(3):
                ve.wait_ge(s["wl_hi"], w + 1)
                ve.tensor_tensor(w1p[:, w, 1, :], stage[:, w % 2, :], w1p[:, w, 0, :], ALU.subtract).then_inc(s["wl_split"], 1)

            def combine(l, c):
                ve.wait_ge(*after(l, f"y_in{par(c)}", 32 * (half(c) + 1)))
                for ch in range(TOPK):
                    for t in range(QT):
                        w = wts[:, l, bass.ds(QT * no(c) + t, 1), ch]
                        op = ve.scalar_tensor_tensor(out=tokens(c, t), in0=ybuf[:, par(c), ch, t, :], scalar=w,
                                                     in1=tokens(c, t), op0=ALU.mult, op1=ALU.add)
                    if ch == 0:
                        op.then_inc(s["comb_one"], 1)
                        ve.wait_ge(*after(l, "comb_one", no(c) + 1))
                op.then_inc(s["comb"], 1)
                ve.wait_ge(*after(l, "comb", no(c) + 1))

            def enter1(c):
                combine(0, c)
                stats(1, c, 0)

            def v_out(c, n):
                t, hf = divmod(n, 2)
                ve.wait_ge(*after(1, "v_psum", 4 * no(c) + n + 1))
                ve.tensor_copy(v1[:, par(c), t, hf * 512:(hf + 1) * 512], m).then_inc(s["v1_evac"], 1)

            def row_max1(b, pp, first):
                n = 8 * no(b) + pp
                r = pp % 2
                ve.wait_ge(s["s_psum"], n + 1)
                ve.tensor_reduce(mx1[:, r, :, :], ps[:, 2 * r:2 * r + 2, 0:3 * P].rearrange("p h (c n) -> p h c n", c=3),
                                 AX, ALU.max).then_inc(s["s_max"], 1)
                ve.wait_ge(s["s_max"], 2 * n + 1)
                ve.tensor_tensor(mx1[:, r, :, 1], mx1[:, r, :, 1], mx1[:, r, :, 2], ALU.max).then_inc(s["s_max"], 1)
                ve.wait_ge(s["s_max"], 2 * n + 2)
                if not (first and pp < 2):
                    ve.wait_ge(s["s_exp"], n - 1)
                ve.tensor_scalar(nb1[:, r, :, :], mx1[:, r, :, 0:2], -SC1, None, ALU.mult).then_inc(s["s_nb"], 1)

            def recip1(b, pp, first):
                n = 8 * no(b) + pp
                r = pp % 2
                ve.wait_ge(s["s_exp"], n + 1)
                if not (first and pp < 2):
                    ve.wait_ge(s["s_norm"], n - 1)
                ve.reciprocal(rc1[:, r, :, :], rs1[:, r, :, :]).then_inc(s["s_rec"], 1)

            def pt_out(b, pp, first):
                n = 8 * no(b) + pp
                ve.wait_ge(s["pt_psum"], n + 1)
                if not (first and pp < 2):
                    ve.wait_ge(*after(1, "pv_psum", n - 1))
                ve.tensor_copy(pt1[:, pp % 2, :, :], ps[:, 4:6, 0:3 * P]).then_inc(s["pt_evac"], 1)

            def attend1(b):
                ve.wait_ge(s["op_psum"], no(b) + 1)
                for t in range(QT):
                    ve.tensor_tensor(tokens(b, t), tokens(b, t), m[:, t * P:(t + 1) * P], ALU.add).then_inc(s["x_add"], 1)
                ve.wait_ge(*after(1, "x_add", 2 * no(b) + 2))

            def body1(b, ahead, behind, more=True):
                first = no(b) == 0 if isinstance(b[0], int) else False
                c, d = off(b, 1), off(b, -1)

                def slot(p):
                    if p >= 1:
                        recip1(b, p - 1, first)
                    elif behind:
                        recip1(d, 7, False)
                    if p >= 2:
                        pt_out(b, p - 2, first)
                    elif behind:
                        pt_out(d, 6 + p, False)
                    row_max1(b, p, first)

                slot(0)
                if ahead:
                    x_low(1, c)
                slot(1)
                if more:
                    enter1(off(b, 2))
                slot(2)
                if behind:
                    attend1(d)
                    stats(1, d, 1)
                slot(3)
                if behind:
                    norm_out(1, d, not (isinstance(d[0], int) and no(d) < 2))
                slot(4)
                slot(5)
                if behind:
                    choose(1, d)
                if ahead:
                    v_out(c, 0)
                slot(6)
                if behind:
                    place(1, d)
                    weigh(1, d)
                if ahead:
                    v_out(c, 1)
                slot(7)
                if ahead:
                    v_out(c, 2)
                    v_out(c, 3)
                if more:
                    norm_in(1, off(b, 2))

            def epilogue1(b):
                recip1(b, 7, False)
                pt_out(b, 6, False)
                pt_out(b, 7, False)
                attend1(b)
                stats(1, b, 1)
                norm_out(1, b, True)
                choose(1, b)
                place(1, b)
                table(1)
                weigh(1, b)

            enter1((0, 0))
            norm_in(1, (0, 0), False)
            x_low(1, (0, 0))
            enter1((0, 1))
            norm_in(1, (0, 1), False)
            for n in range(4):
                v_out((0, 0), n)
            body1((0, 0), True, False)
            with ve.Fori(0, 2) as i:
                for k in (1, 2):
                    body1((i, k), True, True)
            body1((0, 5), True, True)
            body1((0, 6), True, True, False)
            body1((0, 7), False, True, False)
            epilogue1((0, 7))
            experts(1)

            with ve.Fori(0, B // 2) as i:
                for k in range(2):
                    combine(1, (i, k))

        @block.gpsimd
        def _(po):
            po.memset(blank[:, 0:D], 0.0).then_inc(s["blank_set"], 1)
            po.memset(blank[:, D:PAY].bitcast(I32), NOWHERE).then_inc(s["blank_set"], 1)
            po.wait_ge(s["blank_set"], 2)
            po.memset(v0[:, :, :, :, :].rearrange("p r t h n -> p (r t h n)"), 0.0).then_inc(s["v0_clear"], 1)
            po.sem_inc(s["blank_ready"], 1)

            def context_split(l, c):
                po.wait_ge(*after(l, f"ctx_in{par(c)}", 16 * (half(c) + 1)))
                settle(po)
                po.tensor_copy(hl[:, par(c), 1, 0, :], ct[:, par(c), :]).then_inc(s["ctx_hi"], 1)
                po.wait_ge(*after(l, "ctx_hi", no(c) + 1))
                po.tensor_tensor(hl[:, par(c), 1, 1, :], ct[:, par(c), :], hl[:, par(c), 1, 0, :], ALU.subtract).then_inc(s["ctx_split"], 1)

            def inverse_root(l, c, z):
                n0, ch = 14 * no(c), f"rs_chain{z}"
                k = 0
                v, vh, y, t = var[:, z, :], varh[:, z, :], rstd[:, z, :], rsq[:, z, :]

                def link(op):
                    nonlocal k
                    k += 1
                    op.then_inc(s[ch], 1)
                    po.wait_ge(*after(l, ch, n0 + k))
                    settle(po)

                po.wait_ge(*after(l, f"ln_stats{z}", 4 * no(c) + 4))
                settle(po)
                link(po.tensor_scalar(v, mv[:, z, :, 1], EPS, None, ALU.add))
                link(po.tensor_scalar(vh, v, -0.5, None, ALU.mult))
                link(po.tensor_scalar(y.bitcast(I32), v.bitcast(I32), -0.5, float(0x5F3759DF), ALU.mult, ALU.add))
                for n in range(3):
                    link(po.tensor_tensor(t, y, y, ALU.mult))
                    link(po.tensor_tensor(t, t, vh, ALU.mult))
                    link(po.tensor_scalar(t, t, 1.5, None, ALU.add))
                    op = po.tensor_tensor(y, t, y, ALU.mult)
                    if n < 2:
                        link(op)
                op.then_inc(s[f"rs_ready{z}"], 1)

            po.wait_ge(s["wqk_in"], 16)
            src = stage[:, 0, :].rearrange("p (w n) -> p w n", w=2)
            for w in range(2):
                po.tensor_copy(wqk[:, w, 0, :], src[:, w, :]).then_inc(s["wqk_split"], 1)
            po.wait_ge(s["wqk_split"], 2)
            for w in range(2):
                po.tensor_tensor(wqk[:, w, 1, :], src[:, w, :], wqk[:, w, 0, :], ALU.subtract).then_inc(s["wqk_split"], 1)
            po.wait_ge(s["xa_in"], 16)
            inverse_root(0, (0, 0), 0)
            context_split(0, (0, 0))
            po.dma_start(stage[:, 1, 0:1024], a["cb0"]).then_inc(s["st_in1"], 16)
            po.wait_ge(s["wqk_split"], 4)
            po.dma_start(stage[:, 0, 0:CB - 1024], a["cb1"]).then_inc(s["st_in0"], 16)
            po.wait_ge(s["mask_in"], 16)
            po.tensor_copy(maskb[:, :, :], maskraw).then_inc(s["mask_ready"], 1)
            po.wait_ge(s["st_in1"], 16)
            po.tensor_copy(cb[:, 0:1024], stage[:, 1, :]).then_inc(s["st_split"], 1)
            po.wait_ge(s["st_in0"], 16)
            po.tensor_copy(cb[:, 1024:CB], stage[:, 0, 0:CB - 1024]).then_inc(s["cb_ready"], 1)
            po.wait_ge(s["v0_clear"], 1)
            po.memset(v0[:, :, :, :, DK0], 1.0).then_inc(s["v0_ready"], 1)
            context_split(0, (0, 1))
            inverse_root(0, (0, 1), 0)

            had = [1, 1]
            done = [1]

            def load(k, src, n):
                po.dma_start(stage[:, k, 0:n], src).then_inc(s[f"st_in{k}"], 16)
                had[k] += 1

            def split_weights(l, src, n, first, pieces):
                po.wait_ge(s["st_split"], done[0])
                load(first % 2, src(first), n)
                for q in range(first, first + pieces):
                    k = q % 2
                    if q + 1 < first + pieces:
                        load(1 - k, src(q + 1), n)
                    po.wait_ge(s[f"st_in{k}"], 16 * had[k])
                    hi, lo, st = w_up[:, 2 * q * n:(2 * q + 1) * n], w_up[:, (2 * q + 1) * n:(2 * q + 2) * n], stage[:, k, 0:n]
                    po.tensor_copy(hi, st).then_inc(s["st_split"], 1)
                    done[0] += 1
                    po.wait_ge(s["st_split"], done[0])
                    po.tensor_tensor(lo, st, hi, ALU.subtract).then_inc(s["wup_split"], 1)
                    split[0] += 1
                    po.wait_ge(s["wup_split"], split[0])

            split = [0]
            po.wait_ge(s["cb_ready"], 1)
            split_weights(0, lambda q: a["w1"][:, q * F0:(q + 1) * F0], F0, 0, E)

            def send(l, b):
                po.wait_ge(*after(l, "pay_ready", no(b) + 1))
                settle(po)
                for t in range(QT):
                    po.tensor_copy(pay[:, par(b), t, :, D].bitcast(U32),
                                   dest[:, bass.ds(QT * no(b) + t, 1), :].rearrange("p a c -> p (a c)")).then_inc(s["pay_dest"], 1)
                po.tensor_copy(pay[:, par(b), :, 1, 0:D], pay[:, par(b), :, 0, 0:D]).then_inc(s["pay_copy"], 1)
                po.wait_ge(*after(l, "pay_dest", 2 * no(b) + 2))
                po.wait_ge(*after(l, "pay_copy", no(b) + 1))
                po.wait_ge(*after(l, "slot_ready", no(b) + 1))
                settle(po)
                for t in range(QT):
                    for ch in range(TOPK):
                        po.indirect_dma_start(xs[l], bass.IndirectOffsetOnAxis(ap=sloti[:, par(b), t, ch:ch + 1], axis=0),
                                              pay[:, par(b), t, ch, :], None, bounds_check=ROWS - 1,
                                              oob_is_err=False).then_inc(s[f"sent{par(b)}"], 16)

            def sends(l, body, weights=False):
                def split_up(n):
                    if weights:
                        split_weights(1, lambda q: a["wgu"][:, q * F1:(q + 1) * F1], F1, 4 * n, 4)

                po.wait_ge(s[f"slots_blank{l}"], 16)
                body((0, 0), True, False)
                split_up(0)
                with po.Fori(0, 2) as i:
                    for k in (1, 2):
                        body((i, k), True, True)
                for n, b in enumerate((5, 6, 7)):
                    body((0, b), b < 6, True)
                    split_up(n + 1)

            def body0(b, more, behind):
                if more:
                    inverse_root(0, off(b, 2), 0)
                    po.wait_ge(*after(0, "qk_psum", 4 * no(b) + 4))
                    settle(po)
                    context_split(0, off(b, 2))
                if behind:
                    inverse_root(0, off(b, -1), 1)
                    send(0, off(b, -1))

            sends(0, body0)
            inverse_root(0, (0, 7), 1)
            send(0, (0, 7))
            for w in range(2):
                po.dma_start(stage[:, w, :], a["w1p"][:, w * 1024:(w + 1) * 1024]).then_inc(s[f"st_in{w}"], 16)
                had[w] += 1

            def experts(l):
                def scatter(u):
                    po.wait_ge(*after(l, "e_dst", tno(u) + 1))
                    po.wait_ge(*after(l, "e_yev", tno(u) + 1))
                    settle(po)
                    k = u[1] % 4
                    po.indirect_dma_start(yc[l], bass.IndirectOffsetOnAxis(ap=dsti[:, k:k + 1], axis=0), ye[:, k, :], None,
                                          bounds_check=TOPK * T - 1, oob_is_err=False).then_inc(s[f"es_out{k}"], 16)

                def step(t, known):
                    if live(known, 2) and l == 0:
                        u = off(t, -2)
                        po.wait_ge(*after(l, "e_hb", tno(u) + 1))
                        settle(po)
                        if known > 3:
                            po.wait_ge(*after(l, "e_y", tno(u) - 1))
                            settle(po)
                        po.tensor_scalar(ht[:, par(u), :], hb[:, par(u), :], 0.0, None, ALU.max).then_inc(s["e_htev"], 1)
                    if live(known, 3):
                        scatter(off(t, -3))
                    if live(known, 0):
                        k = t[1] % 4
                        po.wait_ge(*after(l, f"xe_in{k}", 16 * (tq(t) + 1)))
                        if not (known < 4):
                            po.wait_ge(*after(l, f"es_out{k}", 16 * tq(t)))
                            settle(po)
                        po.tensor_copy(dsti[:, k:k + 1], xt[:, k, D:PAY].bitcast(U32)).then_inc(s["e_dst"], 1)

                steps(po, step)

            experts(0)
            po.wait_ge(s["wl_split"], 1)
            po.dma_start(stage[:, 0, :], a["w1p"][:, 2048:3072]).then_inc(s["st_in0"], 16)
            had[0] += 1
            context_split(1, (0, 0))

            def norm1(b, pp):
                n = 8 * no(b) + pp
                r = pp % 2
                po.wait_ge(s["s_rec"], n + 1)
                po.tensor_tensor(p1[:, r, :, 0:P], p1[:, r, :, 0:P], rc1[:, r, :, 0:1].broadcast_to([P, 2, P]), ALU.mult)
                po.tensor_tensor(p1[:, r, :, P:3 * P], p1[:, r, :, P:3 * P], rc1[:, r, :, 1:2].broadcast_to([P, 2, 2 * P]),
                                 ALU.mult).then_inc(s["s_norm"], 1)

            def body1(b, more, behind):
                norm1(b, 0)
                norm1(b, 1)
                if more:
                    inverse_root(1, off(b, 2), 0)
                norm1(b, 2)
                if behind:
                    inverse_root(1, off(b, -1), 1)
                norm1(b, 3)
                if more:
                    po.wait_ge(*after(1, "v_psum", 4 * no(b) + 4))
                    settle(po)
                    context_split(1, off(b, 2))
                norm1(b, 4)
                norm1(b, 5)
                norm1(b, 6)
                if behind:
                    send(1, off(b, -1))
                norm1(b, 7)

            inverse_root(1, (0, 0), 0)
            context_split(1, (0, 1))
            inverse_root(1, (0, 1), 0)
            po.wait_ge(s["wl_split"], 3)
            sends(1, body1, True)
            inverse_root(1, (0, 7), 1)
            send(1, (0, 7))
            experts(1)

    return nc


_OUT = (B, S, D)


def kernel(**inputs):
    import concourse.bacc as bacc
    from concourse.bass_utils import run_bass_kernel_spmd

    v = {n: np.asarray(x) for n, x in inputs.items()}
    f, cbv = constants()
    bands = np.zeros((2, G, P), np.float32)
    wband = np.zeros((2, G, P, D), np.float32)
    for w, n in ((0, "q"), (1, "k")):
        for h in range(H):
            g, j = divmod(h, HB)
            for r in range(3):
                rows = slice(32 * j + DK0 * r, 32 * j + DK0 * (r + 1))
                bands[w, g, rows] = v[f"L0_xattn_b{n}"][h * DK0:(h + 1) * DK0]
                wband[w, g, rows] = v[f"L0_xattn_W{n}"][h * DK0:(h + 1) * DK0]
    bands[0, :, 25::32] = 1
    bands[1, :, 24::32] = -MASKED0
    bands[1, :, 26::32] = 1
    wd = np.zeros((E, FP1, D), np.float32)
    wd[:, :F1] = v["L1_ffn_Wd"]
    up = np.stack([v["L1_ffn_Wg"], v["L1_ffn_Wu"]], 2)
    arrays = {
        "cf": f,
        "cb0": cbv[:, :1024],
        "cb1": cbv[:, 1024:],
        "x": v["x"].reshape(T, D),
        "ctxT": v["ctx_1024"].reshape(T, D).T,
        "mask": v["mask_Bx16xS2_ik1"].transpose(1, 0, 2),
        "wqk": wband.transpose(3, 0, 1, 2).reshape(D, 2 * G * P),
        "bias0": bands.transpose(2, 0, 1),
        "wv0": v["L0_xattn_Wv"].T,
        "bv": v["L0_xattn_bv"].reshape(1, D),
        "wr0": v["L0_ffn_W_router"],
        "wr1": v["L1_ffn_W_gate"],
        "br": v["L0_ffn_b_router"].reshape(1, E),
        "w1": v["L0_ffn_W1"].transpose(1, 0, 2).reshape(D, E * F0),
        "b1t": v["L0_ffn_b1"].reshape(E, C0, P).transpose(2, 0, 1),
        "w2": v["L0_ffn_W2"].reshape(E, C0, P, D).transpose(2, 0, 1, 3).reshape(P, E * C0 * D),
        "b2": v["L0_ffn_b2"].reshape(1, E * D),
        "w1p": np.concatenate([v["L1_xattn_w_q"].T, v["L1_xattn_w_k"].T, v["L1_xattn_w_v"].T], 1),
        "wo1": v["L1_xattn_w_o"].T.reshape(M1, P, D).transpose(1, 0, 2),
        "wgu": up.transpose(1, 0, 2, 3).reshape(D, E * 2 * F1),
        "wd": wd.reshape(E, C1, P, D).transpose(2, 0, 1, 3).reshape(P, E * C1 * D),
    }
    arrays = {n: np.ascontiguousarray(x) for n, x in arrays.items()}
    nc = bacc.Bacc("TRN2", target_bir_lowering=False, num_devices=1)
    a = {n: nc.dram_tensor(f"in_{n}", x.shape, mybir.dt.from_np(x.dtype), kind="ExternalInput").ap() for n, x in arrays.items()}
    out = nc.dram_tensor("out_0", (T, D), F32, kind="ExternalOutput").ap()
    program(nc, a, out)
    r = run_bass_kernel_spmd(nc, [{f"in_{n}": x for n, x in arrays.items()}], core_ids=[0])
    return np.asarray(r.results[0]["out_0"]).reshape(_OUT)
```

```python
from contextlib import ExitStack

import numpy as np

import concourse.bass as bass
import concourse.mybir as mybir
from concourse.alu_op_type import AluOpType as ALU

F32, F32R, BF16 = mybir.dt.float32, mybir.dt.float32r, mybir.dt.bfloat16
I32, U32 = mybir.dt.int32, mybir.dt.uint32
ACT = mybir.ActivationFunctionType
AX = mybir.AxisListType.X

P = 128
B, S, D, H = 8, 256, 128, 16
QT = S // P
T = B * S
TT = T // P
DK0 = D // H
DK1 = 64
HB = 4
G = H // HB
M1 = H // 2
E, TOPK = 8, 2
F0, F1 = 512, 352
C0 = F0 // P
C1 = -(-F1 // P)
FP1 = C1 * P
NTILE = 40
REGION = T + P
ROWS = E * REGION + P
PAY = D + 1
NOWHERE = 5000
EPS = 1e-5
MASKED0 = float(2 ** 30)
MASKED1 = 1e30
BANK0 = (5, 4, 4, 5)
SC0 = float(DK0) ** -0.5
SC1 = float(DK1) ** -0.5

_c = {}
_n = 0
for _name, _w in (("ident", P), ("cq", 1), ("ck", 1), ("one8", E), ("choice", TOPK * E), ("region", E),
                  ("lots", T // P), ("tile", NTILE), ("dest", TT * TOPK)):
    _c[_name] = (_n, _n + _w)
    _n += _w
CF = _n
_b = {}
_n = 0
for _name, _w in (("tri", P), ("ones", P), ("ident", P), ("causal", 2 * P), ("selq", G * P), ("selk", G * P)):
    _b[_name] = (_n, _n + _w)
    _n += _w
CB = _n


def constants():
    f = np.zeros((P, CF), np.float32)
    p = np.arange(P)
    f[:, slice(*_c["ident"])] = np.eye(P)
    f[:, _c["cq"][0]] = (p % 32 >= 16) & (p % 32 < 24)
    f[:, _c["ck"][0]] = (p % 32 >= 8) & (p % 32 < 16)
    f[:, slice(*_c["one8"])] = 1
    f[:, slice(*_c["choice"])] = np.tile(np.arange(E), TOPK)
    f[:, slice(*_c["region"])] = np.arange(E) * REGION
    f[:, slice(*_c["lots"])] = np.arange(T // P) * P
    f[:, slice(*_c["tile"])] = np.arange(NTILE)
    dest = p[:, None, None] + P * np.arange(TT)[None, :, None] + T * np.arange(TOPK)[None, None, :]
    f[:, slice(*_c["dest"])] = dest.reshape(P, -1)
    b = np.zeros((P, CB), np.float32)
    b[:, slice(*_b["tri"])] = p[:, None] < p[None, :]
    b[:, slice(*_b["ones"])] = 1
    b[:, slice(*_b["ident"])] = np.eye(P)
    b[:, slice(*_b["causal"])] = np.tile(np.where(p[None, :] > p[:, None], -MASKED1, 0), (1, 2))
    for h in range(H):
        g, j = divmod(h, HB)
        b[h, _b["selq"][0] + g * P + 32 * j + 24] = 1
        b[h, _b["selq"][0] + g * P + 32 * j + 25] = -1
        b[h, _b["selk"][0] + g * P + 32 * j + 24] = MASKED0
        b[h, _b["selk"][0] + g * P + 32 * j + 25] = -MASKED0
    return f, b


def program(nc, a, out):
    xs = [nc.dram_tensor(f"dispatch{n}", (ROWS, PAY), F32, kind="Internal").ap() for n in range(2)]
    yc = [nc.dram_tensor(f"results{n}", (TOPK * T, D), F32, kind="Internal").ap() for n in range(2)]

    with ExitStack() as ctx:
        def sb(name, shape, dt=F32):
            return ctx.enter_context(nc.sbuf_tensor(name, shape, dt))

        ps = ctx.enter_context(nc.psum_tensor("ps", [P, 8, 512], F32))

        x_sb = sb("x_sb", [P, TT, D])
        cf = sb("cf", [P, CF])
        cbi = sb("cbi", [P, CB // 2], I32)
        cb = cbi[:, :].bitcast(BF16)
        bias0 = sb("bias0", [P, 2, G])
        bias0c = sb("bias0c", [P, 2, G])
        bv_bc = sb("bv_bc", [P, D])
        br_bc = sb("br_bc", [P, E])
        wv0 = sb("wv0", [P, D])
        wr = sb("wr", [P, 2, E])
        wo1 = sb("wo1", [P, M1, D])
        b1t = sb("b1t", [P, E, C0])
        stage = sb("stage", [P, 2, 1024])
        w_up = sb("w_up", [P, E * 2 * 2 * F1], F32R)
        w_dn = sb("w_dn", [P, E * C0 * D])
        ra = sb("ra", [P, 3 * 2 * H * DK1], F32R)
        hl = sb("hl", [P, 2, 2, 2, S], F32R)
        ct = sb("ct", [P, 2, S])
        work = sb("work", [P, 17408])
        pay = sb("pay", [P, 2, QT, TOPK, PAY])
        xnt = sb("xnt", [P, S])
        ybuf = sb("ybuf", [P, 2, TOPK, QT, D])
        blank = sb("blank", [P, PAY])
        bn6 = sb("bn6", [P, 2, QT, 6])
        mv = sb("mv", [P, 2, QT, 2])
        rstd = sb("rstd", [P, 2, QT])
        var = sb("var", [P, 2, QT])
        varh = sb("varh", [P, 2, QT])
        rsq = sb("rsq", [P, 2, QT])
        xn = sb("xn", [P, 2, QT, D])
        wts = sb("wts", [P, 2, TT, TOPK])
        lg = sb("lg", [P, QT, E])
        top = sb("top", [P, QT, 8])
        topi = sb("topi", [P, QT, 8], U32)
        topf = sb("topf", [P, QT, TOPK])
        hot = sb("hot", [P, QT, TOPK, E])
        hotb = sb("hotb", [P, QT, E], BF16)
        dlt = sb("dlt", [P, QT])
        edl = sb("edl", [P, QT])
        den = sb("den", [P, QT])
        base = sb("base", [P, 2, E])
        pos = sb("pos", [P, QT, E])
        hp = sb("hp", [P, QT, TOPK, E])
        slotf = sb("slotf", [P, QT, TOPK])
        sloti = sb("sloti", [P, 2, QT, TOPK], U32)
        cnt = sb("cnt", [1, E])
        ntl = sb("ntl", [1, E])
        ends = sb("ends", [1, E])
        whichp = sb("whichp", [1, NTILE + 8])
        which = whichp[:, 3:3 + NTILE]
        packf = sb("packf", [1, NTILE // 4 + 1])
        before = sb("before", [1, NTILE])
        ends_i = sb("ends_i", [1, 2, E], I32)
        tile_e = sb("tile_e", [1, 2, NTILE // 4 + 1], I32)
        tile_row = sb("tile_row", [1, 2, NTILE], I32)
        rec0 = sb("rec0", [P, H])
        att0 = sb("att0", [P, H, DK0])
        chib = sb("chib", [P, 2, S], F32R)
        ex = chib[:, :, :].rearrange("p r (l n) -> p r l n", l=2)
        dsti = sb("dsti", [P, 4], U32)
        mx1 = sb("mx1", [P, 2, 2, 3])
        nb1 = sb("nb1", [P, 2, 2, 2])
        rs1 = sb("rs1", [P, 2, 2, 2])
        rc1 = sb("rc1", [P, 2, 2, 2])

        def cst(name):
            return cf[:, slice(*_c[name])]

        def cstb(name):
            return cb[:, slice(*_b[name])]

        ident = cst("ident")
        maskraw = work[0:H, 8192:8192 + T].bitcast(I32).rearrange("h (b s) -> h b s", b=B)
        dest = cst("dest").rearrange("p (t c) -> p t c", c=TOPK)
        maskb = work[0:H, 13312:14336].bitcast(BF16).rearrange("h (b s) -> h b s", b=B)
        b2_bc = work[:, 12288:13312]
        mx0 = work[:, 14336:15360].rearrange("p (g t n) -> p g t n", g=G, t=QT)
        scratch = ybuf[0:1, :, :, :, :].rearrange("p r c t d -> p (r c t d)")
        lots = scratch[:, 0:E * T // P].rearrange("p (e n) -> p e n", e=E)
        past = scratch[:, 256:256 + NTILE * E].rearrange("p (n e) -> p n e", e=E)
        pastn = scratch[:, 640:640 + NTILE * E].rearrange("p (n e) -> p n e", e=E)
        wqk = ra[:, 0:2048].rearrange("p (w l n) -> p w l n", w=2, l=2)
        qb = ra[:, 2048:4096].rearrange("p (r g n) -> p r g n", r=2, g=G)
        kb = ra[:, 4096:6144].rearrange("p (r g n) -> p r g n", r=2, g=G)
        v0 = work[:, 0:2048].rearrange("p (r t h n) -> p r t h n", r=2, t=QT, h=H)
        pt0 = work[:, 2048:6144].rearrange("p (h n) -> p h n", h=8)
        ot0 = work[:, 6144:8192].rearrange("p (r g n) -> p r g n", r=2, g=G)
        w1p = ra[:, :].rearrange("p (w l n) -> p w l n", w=3, l=2)
        qt1 = work[:, 0:4096].rearrange("p (r m n) -> p r m n", r=2, m=M1)
        kt1 = work[:, 4096:8192].rearrange("p (r m n) -> p r m n", r=2, m=M1)
        v1 = work[:, 8192:12288].rearrange("p (r t n) -> p r t n", r=2, t=QT)
        p1 = work[:, 12288:13824].rearrange("p (r h n) -> p r h n", r=2, h=2)
        pt1 = work[:, 13824:15360].rearrange("p (r h n) -> p r h n", r=2, h=2)
        ot1 = work[:, 15360:17408].rearrange("p (m n) -> p m n", m=M1)
        xt = work[:, 0:4 * PAY].rearrange("p (r n) -> p r n", r=4)
        he = work[:, 1024:2048].rearrange("p (r n) -> p r n", r=2)
        ht = work[:, 2048:3072].rearrange("p (r n) -> p r n", r=2)
        hb = work[:, 3072:4096].rearrange("p (r n) -> p r n", r=2)
        ye = work[:, 4096:4096 + 4 * D].rearrange("p (r n) -> p r n", r=4)
        sg = work[:, 5120:5120 + 2 * F1].rearrange("p (r n) -> p r n", r=2)

        yfin = work[:, 8192:12288].rearrange("p (c t d) -> p c t d", c=TOPK, t=TT)

        once = """consts_in bias_in xa_in xb_in wv_in wr_in wo_in b1_in b2_in mask_in
            st_in0 st_in1 wqk_in he_pad wqk_split wup_split st_split w2_in wd_in
            cb_ready mask_ready v0_clear v0_ready bias_ready blank_set blank_ready slots_blank0 slots_blank1
            qk_chi v_evac a_psum a_max mt_psum qm_ready b_psum b_exp ot_psum o_rec o_mul base_set mx_clear
            s_psum s_max s_nb s_exp s_rec s_norm pt_psum pt_evac v1_evac op_psum wl_hi wl_split fin_in0 fin_in1 fin_in2 fin_in3 fin_one fin_sum out_done
            passed_sp passed_ve passed_po""".split()
        twice = dict(ctx_in0=64, ctx_in1=64, ctx_hi=B, ctx_split=B, ln_stats0=4 * B, ln_stats1=4 * B, rs_chain0=14 * B, rs_chain1=14 * B, rs_ready0=B, rs_ready1=B, xn_ready=B, xt_psum=B, x_hi=B, x_split=B,
                     qk_psum=4 * B, qk_ready=4 * B, v_psum=B, pv_psum=4 * B, pv_evac=2 * B, x_add=2 * B, 
                     pay_ready=B, pay_dest=2 * B, pay_copy=B, t2_psum=B, t2_evac=B, lg_psum=B, lg_done=B, top_done=5 * B,
                     hot_done=B, hotb_done=B, diff_done=B, exp_done=B, wts_den=B, wts_one=B, wts_done=B, pfx_psum=B,
                     pos_done=B, slot_chain=3 * B, slot_ready=B, sent0=256, sent1=256, table=19, table_ready=1, ends_ready=1,
                     e_x=NTILE, e_xhi=NTILE, e_xlo=NTILE, e_h=NTILE, e_hs=0, e_hcopy=NTILE, e_ht=NTILE,
                     e_htev=NTILE, e_y=NTILE, e_yev=NTILE, e_dst=NTILE, comb_one=B, comb=B, y_in0=128, y_in1=128)
        for k in range(4):
            twice.update({f"xe_in{k}": 4 * NTILE, f"es_out{k}": 4 * NTILE})
        s = {n: ctx.enter_context(nc.semaphore(n)) for n in [*once, *twice]}

        def after(l, name, count):
            return s[name], count + l * twice[name]

        block = ctx.enter_context(nc.Block())

        def settle(eng):
            eng.sem_inc(s[{nc.sync: "passed_sp", nc.vector: "passed_ve"}.get(eng, "passed_po")], 1)

        def no(b):
            return 2 * b[0] + b[1]

        def par(b):
            return b[1] % 2

        def half(b):
            return b[0] + b[1] // 2

        def off(b, d):
            return (b[0], b[1] + d)

        def tno(t):
            return 4 * t[0] + t[1]

        def tq(t):
            return t[0] + t[1] // 4

        def pipeline(eng, prologue, body, epilogue):
            prologue()
            body((0, 0), True, False)
            with eng.Fori(0, 3) as i:
                body((i, 1), True, True)
                body((i, 2), True, True)
            body((0, 7), False, True)
            epilogue((0, 7))

        def ahead(b, d):
            return not isinstance(b[0], int) or 0 <= no(b) + d < B

        def need(eng, sem, count):
            if not (isinstance(count, int) and count <= 0):
                eng.wait_ge(sem, count)

        def batches(eng, body):
            body((0, -1))
            body((0, 0))
            with eng.Fori(0, 2) as i:
                body((i, 1))
                body((i, 2))
            for k in (5, 6, 7, 8):
                body((0, k))

        def steps(eng, step, begin=lambda i: None):
            table = begin(0)
            for k in range(4):
                step((0, k), k, table)
            with eng.Fori(1, NTILE // 4) as i:
                table = begin(i)
                for k in range(4):
                    step((i, k), 4, table)
            table = begin(NTILE // 4)
            for k in range(3):
                step((0, NTILE + k), NTILE + k, table)

        def experts_of(eng, l, i):
            return eng.value_load(tile_e[0:1, l, bass.ds(i, 1)], min_val=0, max_val=8 ** 6 - 1)

        def expert(table, t, d):
            return (table >> (3 * (t[1] % 4 - d + 3))) & 7

        def live(known, d):
            return known - d >= 0 and (known < NTILE or known - d < NTILE)

        @block.sync
        def _(sp):
            sp.dma_start(cf[:, :], a["cf"]).then_inc(s["consts_in"], 16)
            sp.dma_start(x_sb[:, 0:4, :], a["x"][0:4 * P, :].rearrange("(t p) d -> p t d", p=P)).then_inc(s["xa_in"], 16)
            sp.dma_start(ct[:, 0, :], a["ctxT"][:, 0:S]).then_inc(s["ctx_in0"], 16)
            sp.dma_start(cbi[:, :], a["cb"]).then_inc(s["cb_ready"], 16)
            sp.dma_start(wv0[:, :], a["wv0"]).then_inc(s["wv_in"], 16)
            sp.dma_start(ct[:, 1, :], a["ctxT"][:, S:2 * S]).then_inc(s["ctx_in1"], 16)
            sp.dma_start(bv_bc[:, :], a["bv"].to_broadcast([P, D])).then_inc(s["wv_in"], 16)
            sp.dma_start(x_sb[:, 4:TT, :], a["x"][4 * P:T, :].rearrange("(t p) d -> p t d", p=P)).then_inc(s["xb_in"], 16)
            sp.dma_start(wr[:, 0, :], a["wr0"]).then_inc(s["wr_in"], 16)
            sp.dma_start(wr[:, 1, :], a["wr1"]).then_inc(s["wr_in"], 16)
            sp.dma_start(br_bc[:, :], a["br"].to_broadcast([P, E])).then_inc(s["wr_in"], 16)
            sp.dma_start(b1t[:, :, :], a["b1t"]).then_inc(s["b1_in"], 16)
            sp.dma_start(b2_bc[:, :], a["b2"].to_broadcast([P, E * D])).then_inc(s["b2_in"], 16)
            sp.dma_start(wo1[:, :, :], a["wo1"]).then_inc(s["wo_in"], 16)
            sp.wait_ge(s["blank_ready"], 1)
            for l in range(2):
                sp.dma_start(xs[l][ROWS - P:ROWS, :], blank[:, :]).then_inc(s[f"slots_blank{l}"], 16)
            sp.dma_start(w_dn[:, :], a["w2"]).then_inc(s["w2_in"], 16)

            def context(l, c):
                sp.wait_ge(*after(l, "v_psum", (no(c) - 1) * (4 if l else 1)))
                settle(sp)
                sp.wait_ge(*after(l, "ctx_split", no(c) - 1))
                settle(sp)
                sp.dma_start(ct[:, par(c), :], a["ctxT"][:, bass.ds(no(c) * S, S)]).then_inc(s[f"ctx_in{par(c)}"], 16)

            with sp.Fori(0, 3) as i:
                for k in (2, 3):
                    context(0, (i, k))

            def tiles(l):
                sp.wait_ge(*after(l, "ends_ready", 1))
                for e in range(E):
                    row = sp.value_load(ends_i[0:1, l, e:e + 1], min_val=e * REGION, max_val=e * REGION + T)
                    sp.dma_start(xs[l][bass.ds(row, P), :], blank[:, :]).then_inc(s[f"slots_blank{l}"], 16)
                sp.wait_ge(s[f"slots_blank{l}"], 16 * (1 + E))
                sp.wait_ge(*after(l, "table_ready", 1))
                sp.wait_ge(*after(l, "sent0", 16 * QT * TOPK * B // 2))
                sp.wait_ge(*after(l, "sent1", 16 * QT * TOPK * B // 2))
                for k in range(4):
                    row = sp.value_load(tile_row[0:1, l, k:k + 1], min_val=0, max_val=ROWS - P)
                    sp.dma_start(xt[:, k, :], xs[l][bass.ds(row, P), :]).then_inc(s[f"xe_in{k}"], 16)
                with sp.Fori(1, NTILE // 4) as i:
                    for k in range(4):
                        sp.wait_ge(*after(l, "e_x", 4 * i + k - 3))
                        sp.wait_ge(*after(l, "e_dst", 4 * i + k - 3))
                        settle(sp)
                        row = sp.value_load(tile_row[0:1, l, bass.ds(4 * i + k, 1)], min_val=0, max_val=ROWS - P)
                        sp.dma_start(xt[:, k, :], xs[l][bass.ds(row, P), :]).then_inc(s[f"xe_in{k}"], 16)

            def results(l, c):
                for ch in range(TOPK):
                    src = yc[l][bass.ds(ch * T + no(c) * S, S), :].rearrange("(t p) d -> p t d", p=P)
                    sp.dma_start(ybuf[:, par(c), ch, :, :], src).then_inc(s[f"y_in{par(c)}"], 16)

            def all_out(l):
                for k in range(4):
                    sp.wait_ge(*after(l, f"es_out{k}", 16 * (NTILE // 4)))

            tiles(0)
            all_out(0)

            for k in range(2):
                results(0, (0, k))
                sp.dma_start(ct[:, k, :], a["ctxT"][:, k * S:(k + 1) * S]).then_inc(s[f"ctx_in{k}"], 16)
            sp.dma_start(w_dn[:, 0:E * C1 * D], a["wd"]).then_inc(s["wd_in"], 16)
            with sp.Fori(0, 3) as i:
                for k in (2, 3):
                    sp.wait_ge(*after(0, "comb", no((i, k)) - 1))
                    settle(sp)
                    results(0, (i, k))
                    context(1, (i, k))
            tiles(1)
            all_out(1)
            for q in range(4):
                for ch in range(TOPK):
                    src = yc[1][ch * T + q * T // 4:ch * T + (q + 1) * T // 4, :].rearrange("(t p) d -> p t d", p=P)
                    sp.dma_start(yfin[:, ch, q * TT // 4:(q + 1) * TT // 4, :], src).then_inc(s[f"fin_in{q}"], 16)
        @block.tensor
        def _(pe):
            m = ps[:, 7, :]

            def transpose_x(l, c, free):
                if free:
                    pe.wait_ge(*free)
                pe.wait_ge(*after(l, "xn_ready", no(c) + 1))
                for t in range(QT):
                    tr = pe.transpose(m[:, t * P:(t + 1) * P], xn[:, par(c), t, :], ident)
                tr.then_inc(s["xt_psum"], 1)

            def project0(c, u):
                w, gp = 1 - u % 2, u // 2
                if u == 0:
                    pe.wait_ge(*after(0, "x_split", no(c) + 1))
                    pe.wait_ge(*after(0, "ctx_split", no(c) + 1))
                    need(pe, *after(0, "qk_ready", 4 * no(c)))
                elif u == 1:
                    need(pe, s["v_evac"], no(c))
                else:
                    pe.wait_ge(*after(0, "qk_ready", 4 * no(c) + 4 - u))
                sel = cstb("selk" if w else "selq")[0:H, :]
                for gi in range(2):
                    g = 2 * gp + gi
                    o = ps[:, BANK0[u], gi * S:(gi + 1) * S]
                    for n, (i, j) in enumerate(((0, 0), (1, 0), (0, 1))):
                        pe.matmul(o, wqk[:, w, i, g * P:(g + 1) * P], hl[:, par(c), w, j, :], start=(n == 0), stop=False)
                    mm = pe.matmul(o, sel[:, g * P:(g + 1) * P], maskb[:, bass.ds(no(c), 1), :], start=False, stop=True)
                mm.then_inc(s["qk_psum"], 1)

            def values0(c):
                pe.wait_ge(*after(0, "qk_ready", 4 * no(c) + 3))
                for t in range(QT):
                    mm = pe.matmul(ps[:, 4, t * P:(t + 1) * P], ct[:, par(c), t * P:(t + 1) * P], wv0[:, :],
                                   start=True, stop=True)
                mm.then_inc(s["v_psum"], 1)

            def scores_q(c, h):
                g, j = divmod(h, HB)
                if h % 8 == 0:
                    pe.wait_ge(*after(0, "qk_ready", 4 * no(c) + 2 + h // 4))
                need(pe, s["a_max"], H * no(c) + h - 1)
                for t in range(QT):
                    mm = pe.matmul(ps[:, h % 2, t * S:(t + 1) * S], qb[32 * j:32 * j + 32, par(c), g, t * P:(t + 1) * P],
                                   kb[32 * j:32 * j + 32, par(c), g, :], start=True, stop=True)
                mm.then_inc(s["a_psum"], 1)

            def transpose_max(c, gp):
                pe.wait_ge(s["a_max"], H * no(c) + 8 * gp + 8)
                for gi in range(2):
                    for t in range(QT):
                        tr = pe.transpose(m[:, (2 * gi + t) * P:(2 * gi + t + 1) * P], mx0[:, 2 * gp + gi, t, :], ident)
                tr.then_inc(s["mt_psum"], 1)

            def scores_k(b, h):
                g, j = divmod(h, HB)
                if h % 8 == 0:
                    pe.wait_ge(s["qm_ready"], 2 * no(b) + h // 8 + 1)
                need(pe, s["b_exp"], H * no(b) + h - 1)
                for t in range(QT):
                    mm = pe.matmul(ps[:, 2 + h % 2, t * S:(t + 1) * S], kb[32 * j:32 * j + 32, par(b), g, t * P:(t + 1) * P],
                                   qb[32 * j:32 * j + 32, par(b), g, :], start=True, stop=True)
                mm.then_inc(s["b_psum"], 1)

            def mix0(b, g):
                pe.wait_ge(s["b_exp"], H * no(b) + HB * (g + 1))
                if g == 0:
                    pe.wait_ge(s["v_evac"], no(b) + 1)
                if g % 2 == 0:
                    need(pe, *after(0, "pv_evac", 2 * no(b) + g // 2))
                for t in range(QT):
                    for j in range(HB):
                        h = HB * g + j
                        mm = pe.matmul(ps[32 * j:32 * j + 32, 6, (g % 2) * S:(g % 2 + 1) * S], v0[:, par(b), t, h, :],
                                       pt0[:, h % 8, t * S:(t + 1) * S], start=(t == 0), stop=(t == QT - 1),
                                       skip_group_check=True)
                mm.then_inc(s["pv_psum"], 1)

            def untranspose0(b, t):
                if t == 0:
                    pe.wait_ge(*after(0, "pv_evac", 2 * no(b) + 2))
                else:
                    pe.wait_ge(s["o_mul"], 2 * no(b) + 1)
                for g in range(G):
                    tr = pe.transpose(m[:, g * P:(g + 1) * P], ot0[:, par(b), g, t * P:(t + 1) * P], ident)
                tr.then_inc(s["ot_psum"], 1)
            def transpose_t2(l, b, free):
                if free:
                    pe.wait_ge(*free)
                pe.wait_ge(*after(l, "pay_ready", no(b) + 1))
                for t in range(QT):
                    tr = pe.transpose(m[:, t * P:(t + 1) * P], pay[:, par(b), t, 0, 0:D], ident)
                tr.then_inc(s["t2_psum"], 1)

            def logits(l, b, free):
                if free:
                    pe.wait_ge(*free)
                pe.wait_ge(*after(l, "t2_evac", no(b) + 1))
                for t in range(QT):
                    mm = pe.matmul(m[:, t * E:(t + 1) * E], xnt[:, t * P:(t + 1) * P], wr[:, l, :], start=True, stop=True)
                mm.then_inc(s["lg_psum"], 1)

            def prefix(l, b, free):
                if free:
                    pe.wait_ge(*free)
                pe.wait_ge(*after(l, "hotb_done", no(b) + 1))
                tri, ones = cstb("tri"), cstb("ones")
                pe.matmul(m[:, 0:E], tri, hotb[:, 0, :], start=True, stop=True)
                pe.matmul(m[:, E:2 * E], tri, hotb[:, 1, :], start=True, stop=False)
                pe.matmul(m[:, E:2 * E], ones, hotb[:, 0, :], start=False, stop=True)
                pe.matmul(m[:, 2 * E:3 * E], ones, hotb[:, 0, :], start=True, stop=False)
                pe.matmul(m[:, 2 * E:3 * E], ones, hotb[:, 1, :], start=False, stop=True).then_inc(s["pfx_psum"], 1)

            pe.wait_ge(s["consts_in"], 16)
            pe.wait_ge(s["cb_ready"], 16)
            pe.wait_ge(s["wqk_split"], 4)
            pe.wait_ge(s["mask_ready"], 1)
            pe.wait_ge(s["wv_in"], 32)
            pe.wait_ge(s["wr_in"], 48)

            def body0(b):
                c, c2, d = off(b, 1), off(b, 2), off(b, -1)
                for n in range(H):
                    if n == 1 and ahead(b, -1):
                        mix0(d, 3)
                    if n == 0 and ahead(b, 0):
                        pe.wait_ge(s["qm_ready"], 2 * no(b) + 1)
                        need(pe, *after(0, "pos_done", no(b) - 1))
                        transpose_max(b, 1)
                    if ahead(b, 0):
                        scores_k(b, n)
                    if ahead(b, 1):
                        scores_q(c, n)
                    if n in (0, 2) and ahead(b, 1):
                        project0(c, 2 + n // 2)
                    if n == 2 and ahead(b, -1):
                        if ahead(b, 0):
                            pe.wait_ge(s["qm_ready"], 2 * no(b) + 2)
                        else:
                            pe.wait_ge(*after(0, "pos_done", no(d)))
                        untranspose0(d, 0)
                    if n == 3 and ahead(b, -1):
                        untranspose0(d, 1)
                    if n == 4 and ahead(b, 1):
                        values0(c)
                    if n == 6 and ahead(b, 2):
                        need(pe, s["qm_ready"], 2 * no(b) + 2)
                        need(pe, s["o_mul"], 2 * no(d) + 2)
                        need(pe, *after(0, "x_split", no(c) + 1))
                        transpose_x(0, c2, None)
                    if n == 8 and ahead(b, 1):
                        if ahead(b, 2):
                            pe.wait_ge(*after(0, "x_split", no(c2) + 1))
                        else:
                            pe.wait_ge(s["o_mul"], 2 * no(d) + 2)
                        transpose_max(c, 0)
                    if n in (5, 9, 13) and ahead(b, 0):
                        mix0(b, n // 4 - 1)
                    if n in (9, 11) and ahead(b, 2):
                        project0(c2, (n - 9) // 2)
                    if n == 10 and ahead(b, -1):
                        transpose_t2(0, d, (s["qm_ready"], 2 * no(c) + 1) if ahead(b, 1) else (s["o_mul"], 2 * no(d) + 2))
                    if n == 11 and ahead(b, -1):
                        logits(0, d, None)
                    if n == 14 and ahead(b, -1):
                        prefix(0, d, None)

            transpose_x(0, (0, 0), None)
            project0((0, 0), 0)
            project0((0, 0), 1)
            batches(pe, body0)
            def experts(l):
                pe.wait_ge(*after(l, "table_ready", 1))
                pe.wait_ge(s["wup_split"], E if l == 0 else 3 * E)
                pe.wait_ge(s["wd_in" if l else "w2_in"], 16)
                pe.wait_ge(*after(l, "pos_done", B))
                if l == 1:
                    pe.wait_ge(s["he_pad"], 1)
                cc, ff = (C1, F1) if l else (C0, F0)

                def step(t, known, table):
                    e_up = expert(table, t, 1) if live(known, 1) else None
                    e_dn = expert(table, t, 3) if live(known, 3) else None
                    if live(known, 0):
                        pe.wait_ge(*after(l, f"xe_in{t[1] % 4}", 16 * (tq(t) + 1)))
                        if known:
                            pe.wait_ge(*after(l, "e_xlo", tno(t)))
                        pe.transpose(ps[:, 0, 0:P], xt[:, t[1] % 4, 0:D], ident).then_inc(s["e_x"], 1)
                    if live(known, 1):
                        u = off(t, -1)
                        pe.wait_ge(*after(l, "e_xlo", tno(u) + 1))
                        if known > 2:
                            pe.wait_ge(*after(l, "e_hcopy", tno(u) - 1))
                        for half_ in range(2 if l else 1):
                            bk = 1 + 2 * par(u) + half_ if l else 1 + par(u)
                            for n, (i, j) in enumerate(((0, 0), (1, 0), (0, 1))):
                                w = w_up[:, bass.ds(e_up * (ff * (4 if l else 2)) + (2 * half_ + j) * ff, ff)]
                                mm = pe.matmul(ps[:, bk, 0:ff], ex[:, par(u), i, :], w, start=(n == 0), stop=(n == 2))
                        mm.then_inc(s["e_h"], 1)
                    if live(known, 2):
                        u = off(t, -2)
                        pe.wait_ge(*after(l, "e_hcopy", tno(u) + 1))
                        if known > 3:
                            pe.wait_ge(*after(l, "e_htev", tno(u) - 1))
                        for k in range(cc):
                            tr = pe.transpose(ps[:, 5 + par(u), k * P:(k + 1) * P], he[:, par(u), k * P:(k + 1) * P], ident)
                        tr.then_inc(s["e_ht"], 1)
                    if live(known, 3):
                        u = off(t, -3)
                        pe.wait_ge(*after(l, "e_htev", tno(u) + 1))
                        if known > 3:
                            pe.wait_ge(*after(l, "e_yev", tno(u)))
                        for k in range(cc):
                            mm = pe.matmul(ps[:, 7, 0:D], ht[:, par(u), k * P:(k + 1) * P],
                                           w_dn[:, bass.ds(e_dn * (cc * D) + k * D, D)], start=(k == 0), stop=(k == cc - 1))
                        mm.then_inc(s["e_y"], 1)

                steps(pe, step, lambda i: experts_of(pe, l, i))

            experts(0)

            def project1(c, u, bank=7):
                w, mm_ = u // 4, 2 * (u % 4)
                if u == 0:
                    pe.wait_ge(*after(1, "x_split", no(c) + 1))
                if u == 4:
                    pe.wait_ge(*after(1, "ctx_split", no(c) + 1))
                for k in range(2):
                    for n, (i, j) in enumerate(((0, 0), (1, 0), (0, 1))):
                        mm = pe.matmul(ps[:, bank, k * S:(k + 1) * S], w1p[:, w, i, (mm_ + k) * P:(mm_ + k + 1) * P],
                                       hl[:, par(c), w, j, :], start=(n == 0), stop=(n == 2))
                mm.then_inc(s["qk_psum"], 1)

            def project1_after(c, u, free):
                if free:
                    pe.wait_ge(*free)
                project1(c, u)

            def values1(c, n, free, bank=7):
                t, hf = divmod(n, 2)
                pe.wait_ge(*free)
                for k, (i, j) in enumerate(((0, 0), (1, 0), (0, 1))):
                    mm = pe.matmul(ps[:, bank, :], hl[:, par(c), 1, i, t * P:(t + 1) * P], w1p[:, 2, j, hf * 512:(hf + 1) * 512],
                                   start=(k == 0), stop=(k == 2))
                mm.then_inc(s["v_psum"], 1)

            def scores1(b, pp, first):
                if pp == 0:
                    pe.wait_ge(*after(1, "qk_ready", 8 * no(b) + 8))
                if not (first and pp < 2):
                    pe.wait_ge(s["s_exp"], 8 * no(b) + pp - 1)
                for e in range(2):
                    bk = ps[:, 2 * (pp % 2) + e, :]
                    rows = slice(64 * e, 64 * e + 64)
                    pe.matmul(bk[:, 0:P], qt1[rows, par(b), pp, 0:P], kt1[rows, par(b), pp, 0:P],
                              start=True, stop=True, skip_group_check=True)
                    pe.matmul(bk[:, P:3 * P], qt1[rows, par(b), pp, P:2 * P], kt1[rows, par(b), pp, :],
                              start=False, stop=True, skip_group_check=True)
                    mm = pe.matmul(bk[:, 0:3 * P].rearrange("p (c n) -> p c n", c=3)[:, 0:3:2, :], cstb("ident"),
                                   cstb("causal").rearrange("p (c n) -> p c n", c=2), start=False, stop=True,
                                   skip_group_check=True)
                mm.then_inc(s["s_psum"], 1)

            def turn1(b, pp, first):
                n = 8 * no(b) + pp
                pe.wait_ge(s["s_norm"], n + 1)
                if not (first and pp == 0):
                    pe.wait_ge(s["pt_evac"], n)
                for e in range(2):
                    for k in range(3):
                        tr = pe.transpose(ps[:, 4 + e, k * P:(k + 1) * P], p1[:, pp % 2, e, k * P:(k + 1) * P], ident)
                tr.then_inc(s["pt_psum"], 1)

            def mix1(b, pp, first):
                n = 8 * no(b) + pp
                pe.wait_ge(s["pt_evac"], n + 1)
                if pp == 0:
                    pe.wait_ge(s["v1_evac"], 4 * no(b) + 4)
                if pp % 2 == 0 and not (first and pp == 0):
                    pe.wait_ge(*after(1, "pv_evac", 4 * no(b) + pp // 2))
                c0 = (pp % 2) * S
                for e in range(2):
                    pe.matmul(ps[64 * e:64 * e + 64, 6, c0:c0 + S], v1[:, par(b), 0, (2 * pp + e) * DK1:(2 * pp + e + 1) * DK1],
                              pt1[:, pp % 2, e, 0:S], start=True, stop=False, skip_group_check=True)
                for e in range(2):
                    mm = pe.matmul(ps[64 * e:64 * e + 64, 6, c0 + P:c0 + S],
                                   v1[:, par(b), 1, (2 * pp + e) * DK1:(2 * pp + e + 1) * DK1],
                                   pt1[:, pp % 2, e, S:3 * P], start=False, stop=True, skip_group_check=True)
                mm.then_inc(s["pv_psum"], 1)

            def output1(b, free):
                pe.wait_ge(*free)
                pe.wait_ge(*after(1, "pv_evac", 4 * no(b) + 4))
                for t in range(QT):
                    for k in range(M1):
                        mm = pe.matmul(m[:, t * P:(t + 1) * P], ot1[:, k, t * P:(t + 1) * P], wo1[:, k, :],
                                       start=(k == 0), stop=(k == M1 - 1))
                mm.then_inc(s["op_psum"], 1)

            pe.wait_ge(s["wl_split"], 3)
            pe.wait_ge(s["wo_in"], 16)
            pe.wait_ge(*after(0, "e_yev", NTILE))

            def qk(c, u):
                return after(1, "qk_ready", 8 * no(c) + u)

            def vv(c, n):
                return (s["v1_evac"], 4 * no(c) + n)

            def prologue1():
                c = (0, 0)
                transpose_x(1, c, None)
                for u in range(8):
                    project1(c, u, u)
                for n in range(4):
                    values1(c, n, qk(c, 5 + n), 4 + n)
                pe.wait_ge(*vv(c, 4))

            def body1(b, ahead, behind):
                first = no(b) == 0 if isinstance(b[0], int) else False
                c, d = off(b, 1), off(b, -1)
                if behind:
                    turn1(d, 6, False)
                scores1(b, 0, first)
                if ahead:
                    transpose_x(1, c, vv(c, 0))
                    project1_after(c, 0, None)
                if behind:
                    mix1(d, 6, False)
                    turn1(d, 7, False)
                scores1(b, 1, first)
                if ahead:
                    project1_after(c, 1, qk(c, 1))
                    project1_after(c, 2, qk(c, 2))
                if behind:
                    mix1(d, 7, False)
                turn1(b, 0, first)
                scores1(b, 2, first)
                if ahead:
                    project1_after(c, 3, qk(c, 3))
                if behind:
                    output1(d, qk(c, 4) if ahead else (s["v1_evac"], 4 * B))
                mix1(b, 0, first)
                turn1(b, 1, first)
                scores1(b, 3, first)
                if ahead:
                    project1_after(c, 4, after(1, "x_add", 2 * no(d) + 2) if behind else qk(c, 4))
                    project1_after(c, 5, qk(c, 5))
                mix1(b, 1, first)
                turn1(b, 2, first)
                scores1(b, 4, first)
                if ahead:
                    project1_after(c, 6, qk(c, 6))
                if behind:
                    transpose_t2(1, d, qk(c, 7) if ahead else None)
                mix1(b, 2, first)
                turn1(b, 3, first)
                scores1(b, 5, first)
                if ahead:
                    project1_after(c, 7, after(1, "t2_evac", no(d) + 1) if behind else qk(c, 7))
                if behind:
                    logits(1, d, qk(c, 8) if ahead else None)
                if ahead:
                    values1(c, 0, after(1, "lg_done", no(d) + 1) if behind else qk(c, 8))
                mix1(b, 3, first)
                turn1(b, 4, first)
                scores1(b, 6, first)
                if behind:
                    prefix(1, d, vv(c, 1) if ahead else None)
                if ahead:
                    values1(c, 1, after(1, "pos_done", no(d) + 1) if behind else vv(c, 1))
                mix1(b, 4, first)
                turn1(b, 5, first)
                scores1(b, 7, first)
                if ahead:
                    values1(c, 2, vv(c, 2))
                    values1(c, 3, vv(c, 3))
                mix1(b, 5, first)

            def epilogue1(b):
                for pp in (6, 7):
                    turn1(b, pp, False)
                    mix1(b, pp, False)
                output1(b, after(1, "pos_done", no(b)))
                transpose_t2(1, b, None)
                logits(1, b, None)
                prefix(1, b, None)

            pipeline(pe, prologue1, body1, epilogue1)
            experts(1)

        @block.scalar
        def _(act):
            act.dma_start(stage[:, 0, :], a["wqk"]).then_inc(s["wqk_in"], 16)
            act.dma_start(bias0[:, :, :], a["bias0"]).then_inc(s["bias_in"], 16)
            act.dma_start(maskraw, a["mask"]).then_inc(s["mask_in"], 16)
            m = ps[:, 7, :]

            def x_high(l, c):
                act.wait_ge(*after(l, "xt_psum", no(c) + 1))
                act.activation(hl[:, par(c), 0, 0, :], m[:, 0:S], ACT.Copy).then_inc(s["x_hi"], 1)

            def low_base(c, u):
                w, gp = 1 - u % 2, u // 2
                act.wait_ge(*after(0, "qk_psum", 4 * no(c) + u + 1))
                need(act, *after(0, "qk_ready", 4 * no(c) + u))
                for gi in range(2):
                    g = 2 * gp + gi
                    ac = act.activation(chib[:, gi, :], ps[:, BANK0[u], gi * S:(gi + 1) * S], ACT.Identity,
                                        bias=bias0c[:, w, g:g + 1], scale=cst("ck" if w else "cq"))
                ac.then_inc(s["qk_chi"], 1)

            def exps0(b, h):
                act.wait_ge(s["b_psum"], H * no(b) + h + 1)
                if h % HB == 0:
                    need(act, *after(0, "pv_psum", 4 * no(b) + h // HB - 1))
                act.activation(pt0[:, h % 8, :], ps[:, 2 + h % 2, :], ACT.Exp, scale=SC0).then_inc(s["b_exp"], 1)

            def take_out0(b, hf):
                act.wait_ge(*after(0, "pv_psum", 4 * no(b) + 2 * hf + 2))
                act.activation(ot0[:, par(b), 2 * hf:2 * hf + 2, :], ps[:, 6, :].rearrange("p (g n) -> p g n", g=2),
                               ACT.Copy).then_inc(s["pv_evac"], 1)
            def t2_out(l, b):
                act.wait_ge(*after(l, "t2_psum", no(b) + 1))
                act.activation(xnt[:, :], m[:, 0:S], ACT.Copy).then_inc(s["t2_evac"], 1)

            def weight_exp(l, b):
                act.wait_ge(*after(l, "diff_done", no(b) + 1))
                act.activation(edl[:, :], dlt[:, :], ACT.Exp).then_inc(s["exp_done"], 1)

            act.wait_ge(s["consts_in"], 16)
            act.wait_ge(s["bias_ready"], 2)

            def body0(b):
                c, c2, d = off(b, 1), off(b, 2), off(b, -1)
                for n in range(H):
                    if ahead(b, 0):
                        exps0(b, n)
                    if n == 1 and ahead(b, -1):
                        take_out0(d, 1)
                    if n in (0, 2) and ahead(b, 1):
                        low_base(c, 2 + n // 2)
                    if n == 6 and ahead(b, 2):
                        x_high(0, c2)
                    if n == 9 and ahead(b, 0):
                        take_out0(b, 0)
                    if n in (9, 11) and ahead(b, 2):
                        low_base(c2, (n - 9) // 2)
                    if n == 10 and ahead(b, -1):
                        t2_out(0, d)
                    if n == 15 and ahead(b, -1):
                        weight_exp(0, d)

            x_high(0, (0, 0))
            low_base((0, 0), 0)
            low_base((0, 0), 1)
            batches(act, body0)
            def experts(l):
                def step(t, known, table):
                    if live(known, 0):
                        act.wait_ge(*after(l, "e_x", tno(t) + 1))
                        if known > 1:
                            act.wait_ge(*after(l, "e_h", tno(t) - 1))
                        act.activation(ex[:, par(t), 0, :], ps[:, 0, 0:P], ACT.Copy).then_inc(s["e_xhi"], 1)
                    if live(known, 1):
                        u = off(t, -1)
                        act.wait_ge(*after(l, "e_h", tno(u) + 1))
                        if l == 0:
                            if known > 2:
                                act.wait_ge(*after(l, "e_ht", tno(u) - 1))
                            act.activation(he[:, par(u), :], ps[:, 1 + par(u), :], ACT.Copy).then_inc(s["e_hcopy"], 1)
                        else:
                            if known > 2:
                                act.wait_ge(*after(l, "e_hcopy", tno(u) - 1))
                            act.activation(sg[:, par(u), :], ps[:, 1 + 2 * par(u), 0:F1], ACT.Silu).then_inc(s["e_hs"], 1)

                steps(act, step)

            for w in range(3):
                act.wait_ge(s[f"st_in{w % 2}"], 16 * (E // 2 + 1 + w // 2))
                act.activation(w1p[:, w, 0, :], stage[:, w % 2, :], ACT.Copy).then_inc(s["wl_hi"], 1)

            experts(0)

            def qk_out(c, u, bank=7):
                act.wait_ge(*after(1, "qk_psum", 8 * no(c) + u + 1))
                dst = (kt1 if u // 4 else qt1)[:, par(c), 2 * (u % 4):2 * (u % 4) + 2, :]
                act.activation(dst, ps[:, bank, :].rearrange("p (k n) -> p k n", k=2), ACT.Copy).then_inc(s["qk_ready"], 1)

            def exps1(b, pp, first):
                n = 8 * no(b) + pp
                act.wait_ge(s["s_nb"], n + 1)
                if not (first and pp < 2):
                    act.wait_ge(s["pt_psum"], n - 1)
                    act.wait_ge(s["s_rec"], n - 1)
                for e in range(2):
                    bk = ps[:, 2 * (pp % 2) + e, :]
                    for t, cols in ((0, slice(0, P)), (1, slice(P, 3 * P))):
                        ac = act.activation(p1[:, pp % 2, e, cols], bk[:, cols], ACT.Exp, scale=SC1,
                                            bias=nb1[:, pp % 2, e, t:t + 1], accum_out=rs1[:, pp % 2, e, t:t + 1])
                ac.then_inc(s["s_exp"], 1)

            def take_out1(b, k, first=False):
                act.wait_ge(*after(1, "pv_psum", 8 * no(b) + 2 * k + 2))
                if k == 0 and not first:
                    act.wait_ge(s["op_psum"], no(b))
                act.activation(ot1[:, 2 * k:2 * k + 2, :], ps[:, 6, :].rearrange("p (k n) -> p k n", k=2),
                               ACT.Copy).then_inc(s["pv_evac"], 1)

            def prologue1():
                c = (0, 0)
                x_high(1, c)
                for u in range(8):
                    qk_out(c, u, u)

            def body1(b, ahead, behind):
                first = no(b) == 0 if isinstance(b[0], int) else False
                c, d = off(b, 1), off(b, -1)
                if ahead:
                    x_high(1, c)
                    qk_out(c, 0)
                exps1(b, 0, first)
                if ahead:
                    qk_out(c, 1)
                    qk_out(c, 2)
                exps1(b, 1, first)
                if behind:
                    take_out1(d, 3)
                if ahead:
                    qk_out(c, 3)
                exps1(b, 2, first)
                if ahead:
                    qk_out(c, 4)
                    qk_out(c, 5)
                exps1(b, 3, first)
                take_out1(b, 0, first)
                if ahead:
                    qk_out(c, 6)
                if behind:
                    t2_out(1, d)
                exps1(b, 4, first)
                if ahead:
                    qk_out(c, 7)
                exps1(b, 5, first)
                take_out1(b, 1)
                if behind:
                    weight_exp(1, d)
                exps1(b, 6, first)
                exps1(b, 7, first)
                take_out1(b, 2)

            def epilogue1(b):
                take_out1(b, 3)
                t2_out(1, b)
                weight_exp(1, b)

            pipeline(act, prologue1, body1, epilogue1)
            experts(1)

            for q in range(4):
                act.wait_ge(s["fin_sum"], q + 1)
                dst = out[q * T // 4:(q + 1) * T // 4, :].rearrange("(t p) d -> p t d", p=P)
                act.dma_start(dst, x_sb[:, q * TT // 4:(q + 1) * TT // 4, :]).then_inc(s["out_done"], 16)
            act.wait_ge(s["out_done"], 64)
        @block.vector
        def _(ve):
            m = ps[:, 7, :]

            def stats(l, c, z, parts=(0, 1)):
                if 0 in parts:
                    settle(ve)
                    for t in range(QT):
                        ve.bn_stats(bn6[:, z, t, :], tokens(c, t)).then_inc(s[f"ln_stats{z}"], 1)
                if 1 in parts:
                    ve.wait_ge(*after(l, f"ln_stats{z}", 4 * no(c) + 2))
                    settle(ve)
                    for t in range(QT):
                        ve.bn_aggr(mv[:, z, t, :], bn6[:, z, t, :]).then_inc(s[f"ln_stats{z}"], 1)

            def normalise(l, c, z, dst, ready):
                ve.wait_ge(*after(l, f"rs_ready{z}", no(c) + 1))
                for t in range(QT):
                    op = ve.tensor_scalar(dst(t), tokens(c, t), mv[:, z, t, 0:1], rstd[:, z, t:t + 1], ALU.subtract, ALU.mult)
                op.then_inc(s[ready], 1)
                ve.wait_ge(*after(l, ready, no(c) + 1))

            def tokens(b, t):
                return x_sb[:, bass.ds(QT * no(b) + t, 1), :].rearrange("p a d -> p (a d)")

            def norm_in(l, c, used=True):
                if used:
                    ve.wait_ge(*after(l, "xt_psum", no(c) - 1))
                normalise(l, c, 0, lambda t: xn[:, par(c), t, :], "xn_ready")

            def norm_out(l, b, used):
                if used:
                    ve.wait_ge(*after(l, f"sent{par(b)}", 16 * QT * TOPK * half(b)))
                normalise(l, b, 1, lambda t: pay[:, par(b), t, 0, 0:D], "pay_ready")

            def x_low(l, c):
                ve.wait_ge(*after(l, "x_hi", no(c) + 1))
                ve.tensor_tensor(hl[:, par(c), 0, 1, :], m[:, 0:S], hl[:, par(c), 0, 0, :], ALU.subtract).then_inc(s["x_split"], 1)

            def qk0(c, u):
                w, gp = 1 - u % 2, u // 2
                ve.wait_ge(s["qk_chi"], 4 * no(c) + u + 1)
                for gi in range(2):
                    g = 2 * gp + gi
                    op = ve.scalar_tensor_tensor(out=(kb if w else qb)[:, par(c), g, :], in0=ps[:, BANK0[u], gi * S:(gi + 1) * S],
                                                 scalar=bias0[:, w, g:g + 1], in1=chib[:, gi, :],
                                                 op0=ALU.add, op1=ALU.subtract)
                op.then_inc(s["qk_ready"], 1)

            def values0(c):
                ve.wait_ge(*after(0, "v_psum", no(c) + 1))
                for t in range(QT):
                    op = ve.tensor_tensor(v0[:, par(c), t, :, 0:DK0], ps[:, 4, t * P:(t + 1) * P].rearrange("p (h n) -> p h n", h=H),
                                          bv_bc[:, :].rearrange("p (h n) -> p h n", h=H), ALU.add)
                op.then_inc(s["v_evac"], 1)

            def row_max(c, h):
                g, j = divmod(h, HB)
                ve.wait_ge(s["a_psum"], H * no(c) + h + 1)
                if h % 8 == 0:
                    need(ve, s["mt_psum"], 2 * no(c) - 1 + h // 8)
                ve.tensor_reduce(mx0[:, g, :, 32 * j + 26], ps[:, h % 2, :].rearrange("p (t n) -> p t n", t=QT), AX, ALU.max).then_inc(s["a_max"], 1)

            def place_max(c, gp):
                ve.wait_ge(s["mt_psum"], 2 * no(c) + gp + 1)
                q = qb[:, par(c), 2 * gp:2 * gp + 2, :]
                ve.scalar_tensor_tensor(out=q, in0=m.rearrange("p (g n) -> p g n", g=2), scalar=-1.0, in1=q,
                                        op0=ALU.mult, op1=ALU.add).then_inc(s["qm_ready"], 1)

            def attend0(b, t, parts=(0, 1, 2)):
                n = 2 * no(b) + t
                o = m.rearrange("p (h n) -> p h n", h=H)
                if 0 in parts:
                    ve.wait_ge(s["ot_psum"], n + 1)
                    ve.reciprocal(rec0[:, :], o[:, :, DK0]).then_inc(s["o_rec"], 1)
                if 1 in parts:
                    ve.wait_ge(s["o_rec"], n + 1)
                    ve.tensor_tensor(att0[:, :, :], o[:, :, 0:DK0], rec0[:, :, None].broadcast_to([P, H, DK0]), ALU.mult).then_inc(s["o_mul"], 1)
                if 2 in parts:
                    ve.wait_ge(s["o_mul"], n + 1)
                    ve.tensor_tensor(tokens(b, t), tokens(b, t), att0[:, :, :].rearrange("p h n -> p (h n)"), ALU.add).then_inc(s["x_add"], 1)

            def choose(l, b, parts=range(6)):
                n = no(b)
                if 0 in parts:
                    ve.wait_ge(*after(l, "lg_psum", n + 1))
                    src = m[:, 0:QT * E].rearrange("p (t e) -> p t e", t=QT)
                    if l == 0:
                        ve.tensor_tensor(lg[:, :, :], src, br_bc[:, None, :].broadcast_to([P, QT, E]), ALU.add).then_inc(s["lg_done"], 1)
                    else:
                        ve.tensor_copy(lg[:, :, :], src).then_inc(s["lg_done"], 1)
                if 1 in parts:
                    ve.wait_ge(*after(l, "lg_done", n + 1))
                    settle(ve)
                    for t in range(QT):
                        ve.max(top[:, t, :], lg[:, t, :]).then_inc(s["top_done"], 1)
                if 2 in parts:
                    ve.wait_ge(*after(l, "top_done", 5 * n + 2))
                    settle(ve)
                    for t in range(QT):
                        ve.max_index(topi[:, t, :], top[:, t, :], lg[:, t, :]).then_inc(s["top_done"], 1)
                    ve.tensor_tensor(dlt[:, :], top[:, :, 1], top[:, :, 0], ALU.subtract).then_inc(s["diff_done"], 1)
                if 3 in parts:
                    ve.wait_ge(*after(l, "top_done", 5 * n + 4))
                    ve.tensor_copy(topf[:, :, :], topi[:, :, 0:TOPK]).then_inc(s["top_done"], 1)
                if 4 in parts:
                    ve.wait_ge(*after(l, "top_done", 5 * n + 5))
                    ve.tensor_tensor(hot[:, :, :, :].rearrange("p t c e -> p (t c) e"),
                                     cst("choice")[:, None, 0:E].broadcast_to([P, QT * TOPK, E]),
                                     topf[:, :, :].rearrange("p t c -> p (t c)")[:, :, None].broadcast_to([P, QT * TOPK, E]),
                                     ALU.is_equal).then_inc(s["hot_done"], 1)
                if 5 in parts:
                    ve.wait_ge(*after(l, "hot_done", n + 1))
                    ve.tensor_tensor(hotb[:, :, :], hot[:, :, 0, :], hot[:, :, 1, :], ALU.add).then_inc(s["hotb_done"], 1)

            def weigh(l, b, parts=range(3)):
                n = no(b)
                w = wts[:, l, bass.ds(QT * n, QT), :]
                if 0 in parts:
                    ve.wait_ge(*after(l, "exp_done", n + 1))
                    ve.tensor_scalar(den[:, :], edl[:, :], 1.0, None, ALU.add).then_inc(s["wts_den"], 1)
                if 1 in parts:
                    ve.wait_ge(*after(l, "wts_den", n + 1))
                    ve.reciprocal(w[:, :, 0], den[:, :]).then_inc(s["wts_one"], 1)
                if 2 in parts:
                    ve.wait_ge(*after(l, "wts_one", n + 1))
                    ve.tensor_tensor(w[:, :, 1], edl[:, :], w[:, :, 0], ALU.mult).then_inc(s["wts_done"], 1)

            def place(l, b, parts=range(4)):
                n = no(b)
                bs = base[:, l, :]
                if 0 in parts:
                    ve.wait_ge(*after(l, "pfx_psum", n + 1))
                    need(ve, *after(l, "pos_done", n))
                    ve.tensor_tensor(pos[:, :, :], m[:, 0:QT * E].rearrange("p (t e) -> p t e", t=QT),
                                     bs[:, None, :].broadcast_to([P, QT, E]), ALU.add).then_inc(s["slot_chain"], 1)
                if 1 in parts:
                    ve.wait_ge(*after(l, "slot_chain", 3 * n + 1))
                    ve.tensor_tensor(bs, bs, m[:, QT * E:(QT + 1) * E], ALU.add).then_inc(s["pos_done"], 1)
                    ve.tensor_tensor(hp[:, :, :, :], hot[:, :, :, :], pos[:, :, None, :].broadcast_to([P, QT, TOPK, E]),
                                     ALU.mult).then_inc(s["slot_chain"], 1)
                if 2 in parts:
                    ve.wait_ge(*after(l, "slot_chain", 3 * n + 2))
                    ve.tensor_reduce(slotf[:, :, :], hp[:, :, :, :], AX, ALU.add).then_inc(s["slot_chain"], 1)
                if 3 in parts:
                    ve.wait_ge(*after(l, "slot_chain", 3 * n + 3))
                    ve.tensor_copy(sloti[:, par(b), :, :], slotf[:, :, :]).then_inc(s["slot_ready"], 1)

            def table(l):
                k = 0

                def link(op):
                    nonlocal k
                    k += 1
                    op.then_inc(s["table"], 1)
                    ve.wait_ge(*after(l, "table", k))

                one = slice(0, 1)
                ve.wait_ge(*after(l, "pos_done", B))
                ve.tensor_copy(ends_i[:, l, :], base[one, l, :]).then_inc(s["ends_ready"], 1)
                link(ve.tensor_tensor(cnt[:, :], base[one, l, :], cst("region")[one, :], ALU.subtract))
                link(ve.tensor_tensor(lots[:, :, :], cnt[:, :, None].broadcast_to([1, E, T // P]),
                                      cst("lots")[one, None, :].broadcast_to([1, E, T // P]), ALU.is_gt))
                link(ve.tensor_reduce(ntl[:, :], lots[:, :, :], AX, ALU.add))
                link(ve.tensor_tensor_scan(ends[:, :], cst("one8")[one, :], ntl[:, :], 0.0, ALU.mult, ALU.add))
                link(ve.tensor_tensor(past[:, :, :], cst("tile")[one, :, None].broadcast_to([1, NTILE, E]),
                                      ends[:, None, :].broadcast_to([1, NTILE, E]), ALU.is_ge))
                link(ve.tensor_reduce(which[:, :], past[:, :, :], AX, ALU.add))
                link(ve.tensor_tensor(pastn[:, :, :], past[:, :, :], ntl[:, None, :].broadcast_to([1, NTILE, E]), ALU.mult))
                link(ve.tensor_reduce(before[:, :], pastn[:, :, :], AX, ALU.add))
                link(ve.tensor_tensor(before[:, :], cst("tile")[one, :], before[:, :], ALU.subtract))
                link(ve.tensor_scalar(before[:, :], before[:, :], float(P), None, ALU.mult))
                link(ve.scalar_tensor_tensor(out=before[:, :], in0=which[:, :], scalar=float(REGION), in1=before[:, :],
                                             op0=ALU.mult, op1=ALU.add))
                link(ve.tensor_scalar(tile_row[:, l, :], before[:, :], float(E * REGION), None, ALU.min))
                link(ve.tensor_scalar(which[:, :], which[:, :], float(E - 1), None, ALU.min))
                for j in range(6):
                    part = whichp[:, j:j + 4 * (NTILE // 4) + 1:4]
                    if j == 0:
                        link(ve.tensor_copy(packf[:, :], part))
                    else:
                        link(ve.scalar_tensor_tensor(out=packf[:, :], in0=part, scalar=float(8 ** j), in1=packf[:, :],
                                                     op0=ALU.mult, op1=ALU.add))
                ve.tensor_copy(tile_e[:, l, :], packf[:, :]).then_inc(s["table_ready"], 1)
                ve.wait_ge(*after(l, "table_ready", 1))

            ve.wait_ge(s["consts_in"], 16)
            ve.wait_ge(s["bias_in"], 16)
            for w, c in ((0, "cq"), (1, "ck")):
                ve.tensor_scalar(bias0c[:, w, :], bias0[:, w, :], cst(c), None, ALU.mult).then_inc(s["bias_ready"], 1)
            for l in range(2):
                ve.tensor_copy(base[:, l, :], cst("region")).then_inc(s["base_set"], 1)
            ve.memset(whichp[:, :], 0.0).then_inc(s["base_set"], 1)
            ve.memset(mx0[:, :, :, :].rearrange("p g t n -> p (g t n)"), 0.0).then_inc(s["mx_clear"], 1)
            ve.wait_ge(s["mx_clear"], 1)
            ve.wait_ge(s["xa_in"], 16)

            def body0(b):
                c, c2, c3, d = off(b, 1), off(b, 2), off(b, 3), off(b, -1)
                has, has2, has3, behind = ahead(b, 1), ahead(b, 2), ahead(b, 3), ahead(b, -1)
                for n in range(H):
                    if has:
                        row_max(c, n)
                    if n == 0 and ahead(b, 0):
                        place_max(b, 1)
                    if n in (1, 3) and has:
                        qk0(c, 2 + n // 2)
                    if n == 2 and behind:
                        attend0(d, 0, (0,))
                        attend0(d, 0, (1,))
                    if n == 3 and behind:
                        attend0(d, 0, (2,))
                    if n == 4:
                        if behind:
                            attend0(d, 1, (0,))
                        if has2:
                            norm_in(0, c2, ahead(b, 0))
                        if behind:
                            attend0(d, 1, (1,))
                    if n == 5:
                        if behind:
                            attend0(d, 1, (2,))
                        if has:
                            values0(c)
                        if behind:
                            ve.wait_ge(*after(0, "x_add", 2 * no(d) + 2))
                            stats(0, d, 1, (0,))
                    if n == 6 and behind:
                        stats(0, d, 1, (1,))
                    if n == 7 and has2:
                        x_low(0, c2)
                    if n == 8 and has:
                        place_max(c, 0)
                    if n == 9 and behind:
                        norm_out(0, d, ahead(b, -3))
                    if n == 10 and has2:
                        qk0(c2, 0)
                    if n == 11 and behind:
                        choose(0, d, (0,))
                    if n == 12:
                        if behind:
                            choose(0, d, (1,))
                        if has2:
                            qk0(c2, 1)
                        if behind:
                            choose(0, d, (2,))
                    if n == 13:
                        if behind:
                            choose(0, d, (3,))
                        if has3:
                            stats(0, c3, 0, (0,))
                        if behind:
                            choose(0, d, (4,))
                        if has3:
                            stats(0, c3, 0, (1,))
                        if behind:
                            choose(0, d, (5,))
                    if n == 14 and behind and ahead(b, 0):
                        place(0, d, (0,))
                    if n == 15 and behind:
                        if not ahead(b, 0):
                            place(0, d)
                            table(0)
                            weigh(0, d)
                        else:
                            for k in range(3):
                                weigh(0, d, (k,))
                                place(0, d, (1 + k,))

            stats(0, (0, 0), 0)
            norm_in(0, (0, 0), False)
            stats(0, (0, 1), 0)
            x_low(0, (0, 0))
            qk0((0, 0), 0)
            qk0((0, 0), 1)
            for n in ("wv_in", "wr_in", "v0_ready", "xb_in", "base_set"):
                ve.wait_ge(s[n], {"wv_in": 32, "wr_in": 48, "v0_ready": 1, "xb_in": 16, "base_set": 3}[n])
            batches(ve, body0)
            def experts(l):
                if l == 0:
                    ve.wait_ge(s["b1_in"], 16)
                    ve.wait_ge(s["b2_in"], 16)
                else:
                    ve.memset(he[:, :, F1:FP1], 0.0).then_inc(s["he_pad"], 1)

                def step(t, known, table):
                    e2 = expert(table, t, 2) if l == 0 and live(known, 2) else None
                    e3 = expert(table, t, 3) if l == 0 and live(known, 3) else None
                    if live(known, 0):
                        ve.wait_ge(*after(l, "e_xhi", tno(t) + 1))
                        ve.tensor_tensor(ex[:, par(t), 1, :], ps[:, 0, 0:P], ex[:, par(t), 0, :], ALU.subtract).then_inc(s["e_xlo"], 1)
                    if l == 1 and live(known, 1):
                        u = off(t, -1)
                        ve.wait_ge(*after(l, "e_hs", tno(u) + 1))
                        if known > 2:
                            ve.wait_ge(*after(l, "e_ht", tno(u) - 1))
                        ve.tensor_tensor(he[:, par(u), 0:F1], sg[:, par(u), :], ps[:, 2 + 2 * par(u), 0:F1], ALU.mult).then_inc(s["e_hcopy"], 1)
                    if live(known, 2):
                        u = off(t, -2)
                        ve.wait_ge(*after(l, "e_ht", tno(u) + 1))
                        if known > 3:
                            ve.wait_ge(*after(l, "e_y", tno(u) - 1))
                        if l == 0:
                            for k in range(C0):
                                b1 = b1t[:, bass.ds(e2, 1), k]
                                op = ve.tensor_scalar(ht[:, par(u), k * P:(k + 1) * P], ps[:, 5 + par(u), k * P:(k + 1) * P],
                                                      b1, 0.0, ALU.add, ALU.max)
                            op.then_inc(s["e_htev"], 1)
                        else:
                            ve.tensor_copy(ht[:, par(u), 0:FP1], ps[:, 5 + par(u), 0:FP1]).then_inc(s["e_htev"], 1)
                    if live(known, 3):
                        u = off(t, -3)
                        ve.wait_ge(*after(l, "e_y", tno(u) + 1))
                        if not (known < 4 or (isinstance(u[0], int) and tno(u) < 4)):
                            ve.wait_ge(*after(l, f"es_out{u[1] % 4}", 16 * tq(u)))
                        if l == 0:
                            ve.tensor_tensor(ye[:, u[1] % 4, :], ps[:, 7, 0:D], b2_bc[:, bass.ds(e3 * D, D)], ALU.add).then_inc(s["e_yev"], 1)
                        else:
                            ve.tensor_copy(ye[:, u[1] % 4, :], ps[:, 7, 0:D]).then_inc(s["e_yev"], 1)

                steps(ve, step, (lambda i: None) if l else (lambda i: experts_of(ve, l, i)))

            for w in range(3):
                ve.wait_ge(s["wl_hi"], w + 1)
                ve.tensor_tensor(w1p[:, w, 1, :], stage[:, w % 2, :], w1p[:, w, 0, :], ALU.subtract).then_inc(s["wl_split"], 1)

            experts(0)

            def combine(l, c):
                ve.wait_ge(*after(l, f"y_in{par(c)}", 32 * (half(c) + 1)))
                for ch in range(TOPK):
                    for t in range(QT):
                        w = wts[:, l, bass.ds(QT * no(c) + t, 1), ch]
                        op = ve.scalar_tensor_tensor(out=tokens(c, t), in0=ybuf[:, par(c), ch, t, :], scalar=w,
                                                     in1=tokens(c, t), op0=ALU.mult, op1=ALU.add)
                    if ch == 0:
                        op.then_inc(s["comb_one"], 1)
                        ve.wait_ge(*after(l, "comb_one", no(c) + 1))
                op.then_inc(s["comb"], 1)
                ve.wait_ge(*after(l, "comb", no(c) + 1))

            def enter1(c):
                combine(0, c)
                stats(1, c, 0)

            def v_out(c, n, bank=7):
                t, hf = divmod(n, 2)
                ve.wait_ge(*after(1, "v_psum", 4 * no(c) + n + 1))
                ve.tensor_copy(v1[:, par(c), t, hf * 512:(hf + 1) * 512], ps[:, bank, :]).then_inc(s["v1_evac"], 1)

            def row_max1(b, pp, first):
                n = 8 * no(b) + pp
                r = pp % 2
                ve.wait_ge(s["s_psum"], n + 1)
                ve.tensor_reduce(mx1[:, r, :, :], ps[:, 2 * r:2 * r + 2, 0:3 * P].rearrange("p h (c n) -> p h c n", c=3),
                                 AX, ALU.max).then_inc(s["s_max"], 1)
                ve.wait_ge(s["s_max"], 2 * n + 1)
                ve.tensor_tensor(mx1[:, r, :, 1], mx1[:, r, :, 1], mx1[:, r, :, 2], ALU.max).then_inc(s["s_max"], 1)
                ve.wait_ge(s["s_max"], 2 * n + 2)
                if not (first and pp < 2):
                    ve.wait_ge(s["s_exp"], n - 1)
                ve.tensor_scalar(nb1[:, r, :, :], mx1[:, r, :, 0:2], -SC1, None, ALU.mult).then_inc(s["s_nb"], 1)

            def recip1(b, pp, first):
                n = 8 * no(b) + pp
                r = pp % 2
                ve.wait_ge(s["s_exp"], n + 1)
                if not (first and pp < 2):
                    ve.wait_ge(s["s_norm"], n - 1)
                ve.reciprocal(rc1[:, r, :, :], rs1[:, r, :, :]).then_inc(s["s_rec"], 1)

            def pt_out(b, pp, first):
                n = 8 * no(b) + pp
                ve.wait_ge(s["pt_psum"], n + 1)
                if not (first and pp < 2):
                    ve.wait_ge(*after(1, "pv_psum", n - 1))
                ve.tensor_copy(pt1[:, pp % 2, :, :], ps[:, 4:6, 0:3 * P]).then_inc(s["pt_evac"], 1)

            def attend1(b):
                ve.wait_ge(s["op_psum"], no(b) + 1)
                for t in range(QT):
                    ve.tensor_tensor(tokens(b, t), tokens(b, t), m[:, t * P:(t + 1) * P], ALU.add).then_inc(s["x_add"], 1)
                ve.wait_ge(*after(1, "x_add", 2 * no(b) + 2))

            def body1(b, ahead, behind, more=True):
                first = no(b) == 0 if isinstance(b[0], int) else False
                c, d = off(b, 1), off(b, -1)

                def slot(p):
                    if p >= 1:
                        recip1(b, p - 1, first)
                    elif behind:
                        recip1(d, 7, False)
                    if p >= 2:
                        pt_out(b, p - 2, first)
                    elif behind:
                        pt_out(d, 6 + p, False)
                    row_max1(b, p, first)

                slot(0)
                if ahead:
                    x_low(1, c)
                slot(1)
                if more:
                    enter1(off(b, 2))
                slot(2)
                if behind:
                    attend1(d)
                    stats(1, d, 1)
                slot(3)
                if behind:
                    norm_out(1, d, not (isinstance(d[0], int) and no(d) < 2))
                slot(4)
                slot(5)
                if behind:
                    choose(1, d)
                if ahead:
                    v_out(c, 0)
                slot(6)
                if behind:
                    place(1, d)
                    weigh(1, d)
                if ahead:
                    v_out(c, 1)
                slot(7)
                if ahead:
                    v_out(c, 2)
                    v_out(c, 3)
                if more:
                    norm_in(1, off(b, 2))

            def epilogue1(b):
                recip1(b, 7, False)
                pt_out(b, 6, False)
                pt_out(b, 7, False)
                attend1(b)
                stats(1, b, 1)
                norm_out(1, b, True)
                choose(1, b)
                place(1, b)
                table(1)
                weigh(1, b)

            enter1((0, 0))
            norm_in(1, (0, 0), False)
            x_low(1, (0, 0))
            enter1((0, 1))
            norm_in(1, (0, 1), False)
            for n in range(4):
                v_out((0, 0), n, 4 + n)
            body1((0, 0), True, False)
            with ve.Fori(0, 2) as i:
                for k in (1, 2):
                    body1((i, k), True, True)
            body1((0, 5), True, True)
            body1((0, 6), True, True, False)
            body1((0, 7), False, True, False)
            epilogue1((0, 7))
            experts(1)

            for q in range(4):
                ve.wait_ge(s[f"fin_in{q}"], 16 * TOPK)
                for ch in range(TOPK):
                    for t in range(q * TT // 4, (q + 1) * TT // 4):
                        op = ve.scalar_tensor_tensor(out=x_sb[:, t, :], in0=yfin[:, ch, t, :], scalar=wts[:, 1, t, ch:ch + 1],
                                                     in1=x_sb[:, t, :], op0=ALU.mult, op1=ALU.add)
                    if ch == 0:
                        op.then_inc(s["fin_one"], 1)
                        ve.wait_ge(s["fin_one"], q + 1)
                op.then_inc(s["fin_sum"], 1)
        @block.gpsimd
        def _(po):
            po.memset(blank[:, 0:D], 0.0).then_inc(s["blank_set"], 1)
            po.memset(blank[:, D:PAY].bitcast(I32), NOWHERE).then_inc(s["blank_set"], 1)
            po.wait_ge(s["blank_set"], 2)
            po.memset(v0[:, :, :, :, :].rearrange("p r t h n -> p (r t h n)"), 0.0).then_inc(s["v0_clear"], 1)
            po.sem_inc(s["blank_ready"], 1)

            def context_split(l, c):
                po.wait_ge(*after(l, f"ctx_in{par(c)}", 16 * (half(c) + 1)))
                settle(po)
                po.tensor_copy(hl[:, par(c), 1, 0, :], ct[:, par(c), :]).then_inc(s["ctx_hi"], 1)
                po.wait_ge(*after(l, "ctx_hi", no(c) + 1))
                po.tensor_tensor(hl[:, par(c), 1, 1, :], ct[:, par(c), :], hl[:, par(c), 1, 0, :], ALU.subtract).then_inc(s["ctx_split"], 1)

            def inverse_root(l, c, z):
                n0, ch = 14 * no(c), f"rs_chain{z}"
                k = 0
                v, vh, y, t = var[:, z, :], varh[:, z, :], rstd[:, z, :], rsq[:, z, :]

                def link(op):
                    nonlocal k
                    k += 1
                    op.then_inc(s[ch], 1)
                    po.wait_ge(*after(l, ch, n0 + k))
                    settle(po)

                po.wait_ge(*after(l, f"ln_stats{z}", 4 * no(c) + 4))
                settle(po)
                link(po.tensor_scalar(v, mv[:, z, :, 1], EPS, None, ALU.add))
                link(po.tensor_scalar(vh, v, -0.5, None, ALU.mult))
                link(po.tensor_scalar(y.bitcast(I32), v.bitcast(I32), -0.5, float(0x5F3759DF), ALU.mult, ALU.add))
                for n in range(3):
                    link(po.tensor_tensor(t, y, y, ALU.mult))
                    link(po.tensor_tensor(t, t, vh, ALU.mult))
                    link(po.tensor_scalar(t, t, 1.5, None, ALU.add))
                    op = po.tensor_tensor(y, t, y, ALU.mult)
                    if n < 2:
                        link(op)
                op.then_inc(s[f"rs_ready{z}"], 1)

            po.wait_ge(s["wqk_in"], 16)
            src = stage[:, 0, :].rearrange("p (w n) -> p w n", w=2)
            for w in range(2):
                po.tensor_copy(wqk[:, w, 0, :], src[:, w, :]).then_inc(s["wqk_split"], 1)
            po.wait_ge(s["wqk_split"], 2)
            for w in range(2):
                po.tensor_tensor(wqk[:, w, 1, :], src[:, w, :], wqk[:, w, 0, :], ALU.subtract).then_inc(s["wqk_split"], 1)
            po.wait_ge(s["xa_in"], 16)
            inverse_root(0, (0, 0), 0)
            context_split(0, (0, 0))
            po.wait_ge(s["mask_in"], 16)
            po.tensor_copy(maskb[:, :, :], maskraw).then_inc(s["mask_ready"], 1)
            po.wait_ge(s["v0_clear"], 1)
            po.memset(v0[:, :, :, :, DK0], 1.0).then_inc(s["v0_ready"], 1)
            inverse_root(0, (0, 1), 0)

            had = [0, 0]

            def load(q, src, n):
                po.dma_start(stage[:, q % 2, 0:n], src(q)).then_inc(s[f"st_in{q % 2}"], 16)
                had[q % 2] += 1

            def split_piece(src, n, q, more):
                if more:
                    load(q + 1, src, n)
                po.wait_ge(s[f"st_in{q % 2}"], 16 * had[q % 2])
                hi, lo, st = w_up[:, 2 * q * n:(2 * q + 1) * n], w_up[:, (2 * q + 1) * n:(2 * q + 2) * n], stage[:, q % 2, 0:n]
                po.tensor_copy(hi, st).then_inc(s["st_split"], 1)
                split[0] += 1
                po.wait_ge(s["st_split"], split[0])
                po.tensor_tensor(lo, st, hi, ALU.subtract).then_inc(s["wup_split"], 1)
                po.wait_ge(s["wup_split"], split[0])

            split = [0]

            def piece0(q):
                return a["w1"][:, q * F0:(q + 1) * F0]

            def piece1(q):
                return a["wgu"][:, q * F1:(q + 1) * F1]
            def send(l, b):
                po.wait_ge(*after(l, "pay_ready", no(b) + 1))
                settle(po)
                for t in range(QT):
                    po.tensor_copy(pay[:, par(b), t, :, D].bitcast(U32),
                                   dest[:, bass.ds(QT * no(b) + t, 1), :].rearrange("p a c -> p (a c)")).then_inc(s["pay_dest"], 1)
                po.tensor_copy(pay[:, par(b), :, 1, 0:D], pay[:, par(b), :, 0, 0:D]).then_inc(s["pay_copy"], 1)
                po.wait_ge(*after(l, "pay_dest", 2 * no(b) + 2))
                po.wait_ge(*after(l, "pay_copy", no(b) + 1))
                po.wait_ge(*after(l, "slot_ready", no(b) + 1))
                settle(po)
                for t in range(QT):
                    for ch in range(TOPK):
                        po.indirect_dma_start(xs[l], bass.IndirectOffsetOnAxis(ap=sloti[:, par(b), t, ch:ch + 1], axis=0),
                                              pay[:, par(b), t, ch, :], None, bounds_check=ROWS - 1,
                                              oob_is_err=False).then_inc(s[f"sent{par(b)}"], 16)

            def sends(l, body):
                po.wait_ge(s[f"slots_blank{l}"], 16)
                body((0, 0), True, False)

                with po.Fori(0, 2) as i:
                    for k in (1, 2):
                        body((i, k), True, True)
                for b in (5, 6, 7):
                    body((0, b), b < 6, True)

            def body0(b):
                if ahead(b, 2):
                    need(po, *after(0, "qk_psum", 4 * no(b) + 4))
                    settle(po)
                    context_split(0, off(b, 2))
                if ahead(b, -1):
                    inverse_root(0, off(b, -1), 1)
                if ahead(b, 3):
                    inverse_root(0, off(b, 3), 0)
                if ahead(b, -1):
                    send(0, off(b, -1))
                if isinstance(b[0], int) and no(b) in (0, 5):
                    q0 = E // 2 * (no(b) // 5)
                    load(q0, piece0, F0)
                    for q in range(q0, q0 + E // 2):
                        split_piece(piece0, F0, q, q + 1 < q0 + E // 2)
                if isinstance(b[0], int) and no(b) == 6:
                    for w in range(2):
                        po.dma_start(stage[:, w, :], a["w1p"][:, w * 1024:(w + 1) * 1024]).then_inc(s[f"st_in{w}"], 16)
                        had[w] += 1

            po.wait_ge(s["slots_blank0"], 16)
            batches(po, body0)
            po.wait_ge(s["wl_split"], 1)
            po.dma_start(stage[:, 0, :], a["w1p"][:, 2048:3072]).then_inc(s["st_in0"], 16)
            had[0] += 1
            def experts(l):
                def scatter(u):
                    po.wait_ge(*after(l, "e_dst", tno(u) + 1))
                    po.wait_ge(*after(l, "e_yev", tno(u) + 1))
                    settle(po)
                    k = u[1] % 4
                    po.indirect_dma_start(yc[l], bass.IndirectOffsetOnAxis(ap=dsti[:, k:k + 1], axis=0), ye[:, k, :], None,
                                          bounds_check=TOPK * T - 1, oob_is_err=False).then_inc(s[f"es_out{k}"], 16)

                def step(t, known, table):
                    if live(known, 3):
                        scatter(off(t, -3))
                    if live(known, 0):
                        k = t[1] % 4
                        po.wait_ge(*after(l, f"xe_in{k}", 16 * (tq(t) + 1)))
                        if not (known < 4):
                            po.wait_ge(*after(l, f"es_out{k}", 16 * tq(t)))
                            settle(po)
                        po.tensor_copy(dsti[:, k:k + 1], xt[:, k, D:PAY].bitcast(U32)).then_inc(s["e_dst"], 1)

                steps(po, step)

            experts(0)
            context_split(1, (0, 0))

            def norm1(b, pp):
                n = 8 * no(b) + pp
                r = pp % 2
                po.wait_ge(s["s_rec"], n + 1)
                po.tensor_tensor(p1[:, r, :, 0:P], p1[:, r, :, 0:P], rc1[:, r, :, 0:1].broadcast_to([P, 2, P]), ALU.mult)
                po.tensor_tensor(p1[:, r, :, P:3 * P], p1[:, r, :, P:3 * P], rc1[:, r, :, 1:2].broadcast_to([P, 2, 2 * P]),
                                 ALU.mult).then_inc(s["s_norm"], 1)

            def body1(b, more, behind):
                q0 = {0: 0, 5: E}.get(no(b)) if isinstance(b[0], int) else None
                if q0 is not None:
                    load(q0, piece1, F1)
                for pp in range(M1):
                    norm1(b, pp)
                    if pp == 1 and more:
                        inverse_root(1, off(b, 2), 0)
                    if pp == 2 and behind:
                        inverse_root(1, off(b, -1), 1)
                    if pp == 3 and more:
                        po.wait_ge(*after(1, "v_psum", 4 * no(b) + 4))
                        settle(po)
                        context_split(1, off(b, 2))
                    if pp == 6 and behind:
                        send(1, off(b, -1))
                    if q0 is not None:
                        split_piece(piece1, F1, q0 + pp, pp + 1 < M1)
            inverse_root(1, (0, 0), 0)
            context_split(1, (0, 1))
            inverse_root(1, (0, 1), 0)
            po.wait_ge(s["wl_split"], 3)
            sends(1, body1)
            inverse_root(1, (0, 7), 1)
            send(1, (0, 7))
            experts(1)

    return nc


_OUT = (B, S, D)


def kernel(**inputs):
    import concourse.bacc as bacc
    from concourse.bass_utils import run_bass_kernel_spmd

    v = {n: np.asarray(x) for n, x in inputs.items()}
    f, cbv = constants()
    bands = np.zeros((2, G, P), np.float32)
    wband = np.zeros((2, G, P, D), np.float32)
    for w, n in ((0, "q"), (1, "k")):
        for h in range(H):
            g, j = divmod(h, HB)
            for r in range(3):
                rows = slice(32 * j + DK0 * r, 32 * j + DK0 * (r + 1))
                bands[w, g, rows] = v[f"L0_xattn_b{n}"][h * DK0:(h + 1) * DK0]
                wband[w, g, rows] = v[f"L0_xattn_W{n}"][h * DK0:(h + 1) * DK0]
    bands[0, :, 25::32] = 1
    bands[1, :, 24::32] = -MASKED0
    bands[1, :, 26::32] = 1
    wd = np.zeros((E, FP1, D), np.float32)
    wd[:, :F1] = v["L1_ffn_Wd"]
    up = np.stack([v["L1_ffn_Wg"], v["L1_ffn_Wu"]], 2)
    arrays = {
        "cf": f,
        "cb": (cbv.view(np.uint32) >> 16).astype(np.uint16).view(np.int32),
        "x": v["x"].reshape(T, D),
        "ctxT": v["ctx_1024"].reshape(T, D).T,
        "mask": v["mask_Bx16xS2_ik1"].transpose(1, 0, 2),
        "wqk": wband.transpose(3, 0, 1, 2).reshape(D, 2 * G * P),
        "bias0": bands.transpose(2, 0, 1),
        "wv0": v["L0_xattn_Wv"].T,
        "bv": v["L0_xattn_bv"].reshape(1, D),
        "wr0": v["L0_ffn_W_router"],
        "wr1": v["L1_ffn_W_gate"],
        "br": v["L0_ffn_b_router"].reshape(1, E),
        "w1": v["L0_ffn_W1"].transpose(1, 0, 2).reshape(D, E * F0),
        "b1t": v["L0_ffn_b1"].reshape(E, C0, P).transpose(2, 0, 1),
        "w2": v["L0_ffn_W2"].reshape(E, C0, P, D).transpose(2, 0, 1, 3).reshape(P, E * C0 * D),
        "b2": v["L0_ffn_b2"].reshape(1, E * D),
        "w1p": np.concatenate([v["L1_xattn_w_q"].T, v["L1_xattn_w_k"].T, v["L1_xattn_w_v"].T], 1),
        "wo1": v["L1_xattn_w_o"].T.reshape(M1, P, D).transpose(1, 0, 2),
        "wgu": up.transpose(1, 0, 2, 3).reshape(D, E * 2 * F1),
        "wd": wd.reshape(E, C1, P, D).transpose(2, 0, 1, 3).reshape(P, E * C1 * D),
    }
    arrays = {n: np.ascontiguousarray(x) for n, x in arrays.items()}
    nc = bacc.Bacc("TRN2", target_bir_lowering=False, num_devices=1)
    a = {n: nc.dram_tensor(f"in_{n}", x.shape, mybir.dt.from_np(x.dtype), kind="ExternalInput").ap() for n, x in arrays.items()}
    out = nc.dram_tensor("out_0", (T, D), F32, kind="ExternalOutput").ap()
    program(nc, a, out)
    r = run_bass_kernel_spmd(nc, [{f"in_{n}": x for n, x in arrays.items()}], core_ids=[0])
    return np.asarray(r.results[0]["out_0"]).reshape(_OUT)
```

```python
from contextlib import ExitStack

import numpy as np

import concourse.bass as bass
import concourse.mybir as mybir
from concourse.alu_op_type import AluOpType as ALU

F32, F32R, BF16 = mybir.dt.float32, mybir.dt.float32r, mybir.dt.bfloat16
I32, U32 = mybir.dt.int32, mybir.dt.uint32
ACT = mybir.ActivationFunctionType
AX = mybir.AxisListType.X

P = 128
B, S, D, H = 8, 256, 128, 16
QT = S // P
T = B * S
TT = T // P
DK0 = D // H
DK1 = 64
HB = 4
G = H // HB
M1 = H // 2
E, TOPK = 8, 2
F0, F1 = 512, 352
C0 = F0 // P
C1 = -(-F1 // P)
FP1 = C1 * P
NTILE = 40
REGION = T + P
ROWS = E * REGION + P
PAY = D + 1
NOWHERE = 5000
EPS = 1e-5
MASKED0 = float(2 ** 30)
MASKED1 = 1e30
BANK0 = (5, 4, 4, 5)
SC0 = float(DK0) ** -0.5
SC1 = float(DK1) ** -0.5

_c = {}
_n = 0
for _name, _w in (("ident", P), ("cq", 1), ("ck", 1), ("one8", E), ("choice", TOPK * E), ("region", E),
                  ("lots", T // P), ("tile", NTILE), ("dest", TT * TOPK)):
    _c[_name] = (_n, _n + _w)
    _n += _w
CF = _n
_b = {}
_n = 0
for _name, _w in (("tri", P), ("ones", P), ("ident", P), ("causal", 2 * P), ("selq", G * P), ("selk", G * P)):
    _b[_name] = (_n, _n + _w)
    _n += _w
CB = _n


def constants():
    f = np.zeros((P, CF), np.float32)
    p = np.arange(P)
    f[:, slice(*_c["ident"])] = np.eye(P)
    f[:, _c["cq"][0]] = (p % 32 >= 16) & (p % 32 < 24)
    f[:, _c["ck"][0]] = (p % 32 >= 8) & (p % 32 < 16)
    f[:, slice(*_c["one8"])] = 1
    f[:, slice(*_c["choice"])] = np.tile(np.arange(E), TOPK)
    f[:, slice(*_c["region"])] = np.arange(E) * REGION
    f[:, slice(*_c["lots"])] = np.arange(T // P) * P
    f[:, slice(*_c["tile"])] = np.arange(NTILE)
    dest = p[:, None, None] + P * np.arange(TT)[None, :, None] + T * np.arange(TOPK)[None, None, :]
    f[:, slice(*_c["dest"])] = dest.reshape(P, -1)
    b = np.zeros((P, CB), np.float32)
    b[:, slice(*_b["tri"])] = p[:, None] < p[None, :]
    b[:, slice(*_b["ones"])] = 1
    b[:, slice(*_b["ident"])] = np.eye(P)
    b[:, slice(*_b["causal"])] = np.tile(np.where(p[None, :] > p[:, None], -MASKED1, 0), (1, 2))
    for h in range(H):
        g, j = divmod(h, HB)
        b[h, _b["selq"][0] + g * P + 32 * j + 24] = 1
        b[h, _b["selq"][0] + g * P + 32 * j + 25] = -1
        b[h, _b["selk"][0] + g * P + 32 * j + 24] = MASKED0
        b[h, _b["selk"][0] + g * P + 32 * j + 25] = -MASKED0
    return f, b


def program(nc, a, out):
    xs = [nc.dram_tensor(f"dispatch{n}", (ROWS, PAY), F32, kind="Internal").ap() for n in range(2)]
    yc = [nc.dram_tensor(f"results{n}", (TOPK * T, D), F32, kind="Internal").ap() for n in range(2)]

    with ExitStack() as ctx:
        def sb(name, shape, dt=F32):
            return ctx.enter_context(nc.sbuf_tensor(name, shape, dt))

        ps = ctx.enter_context(nc.psum_tensor("ps", [P, 8, 512], F32))

        x_sb = sb("x_sb", [P, TT, D])
        cf = sb("cf", [P, CF])
        cbi = sb("cbi", [P, CB // 2], I32)
        cb = cbi[:, :].bitcast(BF16)
        bias0 = sb("bias0", [P, 2, G])
        bias0c = sb("bias0c", [P, 2, G])
        bv_bc = sb("bv_bc", [P, D])
        br_bc = sb("br_bc", [P, E])
        wv0 = sb("wv0", [P, D])
        wr = sb("wr", [P, 2, E])
        wo1 = sb("wo1", [P, M1, D])
        b1t = sb("b1t", [P, E, C0])
        stage = sb("stage", [P, 2, 1024])
        w_up = sb("w_up", [P, E * 2 * 2 * F1], F32R)
        w_dn = sb("w_dn", [P, E * C0 * D])
        ra = sb("ra", [P, 3 * 2 * H * DK1], F32R)
        hl = sb("hl", [P, 2, 2, 2, S], F32R)
        ct = sb("ct", [P, 2, S])
        work = sb("work", [P, 17408])
        pay = sb("pay", [P, 2, QT, TOPK, PAY])
        xnt = sb("xnt", [P, S])
        ybuf = sb("ybuf", [P, 2, TOPK, QT, D])
        blank = sb("blank", [P, PAY])
        bn6 = sb("bn6", [P, 2, QT, 6])
        mv = sb("mv", [P, 2, QT, 2])
        rstd = sb("rstd", [P, 2, QT])
        var = sb("var", [P, 2, QT])
        varh = sb("varh", [P, 2, QT])
        rsq = sb("rsq", [P, 2, QT])
        xn = sb("xn", [P, 2, QT, D])
        wts = sb("wts", [P, 2, TT, TOPK])
        lg = sb("lg", [P, QT, E])
        top = sb("top", [P, QT, 8])
        topi = sb("topi", [P, QT, 8], U32)
        topf = sb("topf", [P, QT, TOPK])
        hot = sb("hot", [P, QT, TOPK, E])
        hotb = sb("hotb", [P, QT, E], BF16)
        dlt = sb("dlt", [P, QT])
        edl = sb("edl", [P, QT])
        den = sb("den", [P, QT])
        base = sb("base", [P, 2, E])
        pos = sb("pos", [P, QT, E])
        hp = sb("hp", [P, QT, TOPK, E])
        slotf = sb("slotf", [P, QT, TOPK])
        sloti = sb("sloti", [P, 2, QT, TOPK], U32)
        cnt = sb("cnt", [1, E])
        ntl = sb("ntl", [1, E])
        ends = sb("ends", [1, E])
        whichp = sb("whichp", [1, NTILE + 8])
        which = whichp[:, 3:3 + NTILE]
        packf = sb("packf", [1, NTILE // 4 + 1])
        before = sb("before", [1, NTILE])
        ends_i = sb("ends_i", [1, 2, E], I32)
        tile_e = sb("tile_e", [1, 2, NTILE // 4 + 1], I32)
        tile_row = sb("tile_row", [1, 2, NTILE], I32)
        rec0 = sb("rec0", [P, H])
        att0 = sb("att0", [P, H, DK0])
        chib = sb("chib", [P, 2, S], F32R)
        ex = chib[:, :, :].rearrange("p r (l n) -> p r l n", l=2)
        dsti = sb("dsti", [P, 4], U32)
        mx1 = sb("mx1", [P, 2, 2, 3])
        nb1 = sb("nb1", [P, 2, 2, 2])
        rs1 = sb("rs1", [P, 2, 2, 2])
        rc1 = sb("rc1", [P, 2, 2, 2])

        def cst(name):
            return cf[:, slice(*_c[name])]

        def cstb(name):
            return cb[:, slice(*_b[name])]

        ident = cst("ident")
        maskraw = work[0:H, 8192:8192 + T].bitcast(I32).rearrange("h (b s) -> h b s", b=B)
        dest = cst("dest").rearrange("p (t c) -> p t c", c=TOPK)
        maskb = work[0:H, 13312:14336].bitcast(BF16).rearrange("h (b s) -> h b s", b=B)
        b2_bc = work[:, 12288:13312]
        mx0 = work[:, 14336:14848].rearrange("p (g t n) -> p g t n", g=2, t=QT)
        scratch = ybuf[0:1, :, :, :, :].rearrange("p r c t d -> p (r c t d)")
        lots = scratch[:, 0:E * T // P].rearrange("p (e n) -> p e n", e=E)
        past = scratch[:, 256:256 + NTILE * E].rearrange("p (n e) -> p n e", e=E)
        pastn = scratch[:, 640:640 + NTILE * E].rearrange("p (n e) -> p n e", e=E)
        wqk = ra[:, 0:2048].rearrange("p (w l n) -> p w l n", w=2, l=2)
        qb = ra[:, 2048:4096].rearrange("p (r g n) -> p r g n", r=2, g=G)
        kb = ra[:, 4096:6144].rearrange("p (r g n) -> p r g n", r=2, g=G)
        km = w_up[:, (E - 1) * 2 * F0:(E - 1) * 2 * F0 + H * S].rearrange("p (h n) -> p h n", h=H)
        v0 = work[:, 0:2048].rearrange("p (r t h n) -> p r t h n", r=2, t=QT, h=H)
        pt0 = work[:, 2048:6144].rearrange("p (h n) -> p h n", h=8)
        ot0 = work[:, 6144:8192].rearrange("p (r g n) -> p r g n", r=2, g=G)
        w1p = ra[:, :].rearrange("p (w l n) -> p w l n", w=3, l=2)
        qt1 = work[:, 0:4096].rearrange("p (r m n) -> p r m n", r=2, m=M1)
        kt1 = work[:, 4096:8192].rearrange("p (r m n) -> p r m n", r=2, m=M1)
        v1 = work[:, 8192:12288].rearrange("p (r t n) -> p r t n", r=2, t=QT)
        p1 = work[:, 12288:13824].rearrange("p (r h n) -> p r h n", r=2, h=2)
        pt1 = work[:, 13824:15360].rearrange("p (r h n) -> p r h n", r=2, h=2)
        ot1 = work[:, 15360:17408].rearrange("p (m n) -> p m n", m=M1)
        xt = work[:, 0:4 * PAY].rearrange("p (r n) -> p r n", r=4)
        he = work[:, 1024:2048].rearrange("p (r n) -> p r n", r=2)
        ht = work[:, 2048:3072].rearrange("p (r n) -> p r n", r=2)
        hb = work[:, 3072:4096].rearrange("p (r n) -> p r n", r=2)
        ye = work[:, 4096:4096 + 4 * D].rearrange("p (r n) -> p r n", r=4)
        sg = work[:, 5120:5120 + 2 * F1].rearrange("p (r n) -> p r n", r=2)

        yfin = work[:, 8192:12288].rearrange("p (c t d) -> p c t d", c=TOPK, t=TT)

        once = """consts_in bias_in xa_in xb_in wv_in wr_in wo_in b1_in b2_in mask_in
            st_in0 st_in1 wqk_in wqk_hi he_pad wqk_split wup_split st_split w2_in wd_in
            cb_ready mask_ready v0_clear v0_ready bias_ready blank_set blank_ready slots_blank0 slots_blank1
            qk_chi v_evac a_psum a_max mt_psum qm_ready b_psum b_exp ot_psum o_rec o_mul base_set mx_clear
            s_psum s_max s_nb s_exp s_rec s_norm pt_psum pt_evac v1_evac op_psum wl_hi wl_split up_in0 up_in1 up_hi up_lo km_clear km_in0 km_in1 fin_in0 fin_in1 fin_in2 fin_in3 fin_one fin_sum out_done
            passed_sp passed_ve passed_po""".split()
        twice = dict(ctx_in0=64, ctx_in1=64, ctx_hi=B, ctx_split=B, ln_stats0=4 * B, ln_stats1=4 * B, rs_chain0=14 * B, rs_chain1=14 * B, rs_ready0=B, rs_ready1=B, xn_ready=B, xt_psum=B, x_hi=B, x_split=B,
                     qk_psum=4 * B, qk_ready=4 * B, v_psum=B, pv_psum=4 * B, pv_evac=2 * B, x_add=2 * B, 
                     pay_ready=B, pay_dest=2 * B, pay_copy=B, t2_psum=B, t2_evac=B, lg_psum=B, lg_done=B, top_done=5 * B,
                     hot_done=B, hotb_done=B, diff_done=B, exp_done=B, wts_den=B, wts_one=B, wts_done=B, pfx_psum=B,
                     pos_done=B, slot_chain=3 * B, slot_ready=B, sent0=256, sent1=256, table=19, table_ready=1, ends_ready=1,
                     e_x=NTILE, e_xhi=NTILE, e_xlo=NTILE, e_h=NTILE, e_hs=0, e_hcopy=NTILE, e_ht=NTILE,
                     e_htev=NTILE, e_y=NTILE, e_yev=NTILE, e_dst=NTILE, comb_one=B, comb=B, y_in0=128, y_in1=128)
        for k in range(4):
            twice.update({f"xe_in{k}": 4 * NTILE, f"es_out{k}": 4 * NTILE})
        s = {n: ctx.enter_context(nc.semaphore(n)) for n in [*once, *twice]}

        def after(l, name, count):
            return s[name], count + l * twice[name]

        block = ctx.enter_context(nc.Block())

        def settle(eng):
            eng.sem_inc(s[{nc.sync: "passed_sp", nc.vector: "passed_ve"}.get(eng, "passed_po")], 1)

        def no(b):
            return 2 * b[0] + b[1]

        def par(b):
            return b[1] % 2

        def half(b):
            return b[0] + b[1] // 2

        def off(b, d):
            return (b[0], b[1] + d)

        def tno(t):
            return 4 * t[0] + t[1]

        def tq(t):
            return t[0] + t[1] // 4

        def pipeline(eng, prologue, body, epilogue):
            prologue()
            body((0, 0), True, False)
            with eng.Fori(0, 2) as i:
                body((i, 1), True, True)
                body((i, 2), True, True)
            for k in (5, 6, 7):
                body((0, k), k < 7, True)
            epilogue((0, 7))

        def pieces(b):
            q0 = {0: 0, 5: 4, 6: 8, 7: 12}.get(no(b)) if isinstance(b[0], int) else None
            return [] if q0 is None else list(range(q0, q0 + 4))

        def piece_parts(q):
            return stage[:, q % 2, 0:F1], w_up[:, 2 * q * F1:(2 * q + 1) * F1], w_up[:, (2 * q + 1) * F1:(2 * q + 2) * F1]

        def ahead(b, d):
            return not isinstance(b[0], int) or 0 <= no(b) + d < B

        def need(eng, sem, count):
            if not (isinstance(count, int) and count <= 0):
                eng.wait_ge(sem, count)

        def batches(eng, body):
            body((0, -1))
            body((0, 0))
            with eng.Fori(0, 2) as i:
                body((i, 1))
                body((i, 2))
            for k in (5, 6, 7, 8):
                body((0, k))

        def steps(eng, step, begin=lambda i: None):
            table = begin(0)
            for k in range(4):
                step((0, k), k, table)
            with eng.Fori(1, NTILE // 4) as i:
                table = begin(i)
                for k in range(4):
                    step((i, k), 4, table)
            table = begin(NTILE // 4)
            for k in range(3):
                step((0, NTILE + k), NTILE + k, table)

        def experts_of(eng, l, i):
            return eng.value_load(tile_e[0:1, l, bass.ds(i, 1)], min_val=0, max_val=8 ** 6 - 1)

        def expert(table, t, d):
            return (table >> (3 * (t[1] % 4 - d + 3))) & 7

        def live(known, d):
            return known - d >= 0 and (known < NTILE or known - d < NTILE)

        @block.sync
        def _(sp):
            sp.dma_start(cf[:, :], a["cf"]).then_inc(s["consts_in"], 16)
            sp.dma_start(x_sb[:, 0:4, :], a["x"][0:4 * P, :].rearrange("(t p) d -> p t d", p=P)).then_inc(s["xa_in"], 16)
            sp.dma_start(ct[:, 0, :], a["ctxT"][:, 0:S]).then_inc(s["ctx_in0"], 16)
            sp.dma_start(cbi[:, :], a["cb"]).then_inc(s["cb_ready"], 16)
            sp.dma_start(wv0[:, :], a["wv0"]).then_inc(s["wv_in"], 16)
            sp.dma_start(ct[:, 1, :], a["ctxT"][:, S:2 * S]).then_inc(s["ctx_in1"], 16)
            sp.dma_start(bv_bc[:, :], a["bv"].to_broadcast([P, D])).then_inc(s["wv_in"], 16)
            sp.dma_start(x_sb[:, 4:TT, :], a["x"][4 * P:T, :].rearrange("(t p) d -> p t d", p=P)).then_inc(s["xb_in"], 16)
            sp.dma_start(wr[:, 0, :], a["wr0"]).then_inc(s["wr_in"], 16)
            sp.dma_start(wr[:, 1, :], a["wr1"]).then_inc(s["wr_in"], 16)
            sp.dma_start(br_bc[:, :], a["br"].to_broadcast([P, E])).then_inc(s["wr_in"], 16)
            sp.dma_start(b1t[:, :, :], a["b1t"]).then_inc(s["b1_in"], 16)
            sp.dma_start(b2_bc[:, :], a["b2"].to_broadcast([P, E * D])).then_inc(s["b2_in"], 16)
            sp.dma_start(wo1[:, :, :], a["wo1"]).then_inc(s["wo_in"], 16)
            sp.wait_ge(s["blank_ready"], 1)
            for l in range(2):
                sp.dma_start(xs[l][ROWS - P:ROWS, :], blank[:, :]).then_inc(s[f"slots_blank{l}"], 16)
            sp.dma_start(w_dn[:, :], a["w2"]).then_inc(s["w2_in"], 16)

            def context(l, c):
                sp.wait_ge(*after(l, "v_psum", (no(c) - 1) * (4 if l else 1)))
                settle(sp)
                sp.wait_ge(*after(l, "ctx_split", no(c) - 1))
                settle(sp)
                sp.dma_start(ct[:, par(c), :], a["ctxT"][:, bass.ds(no(c) * S, S)]).then_inc(s[f"ctx_in{par(c)}"], 16)

            def alone(c, hf):
                sp.wait_ge(*after(0, "qk_ready", 4 * no(c) + 1 + 2 * hf))
                settle(sp)
                need(sp, s["a_psum"], H * (no(c) - 1) + 8 * (hf + 1))
                settle(sp)
                for j in range(HB):
                    rows = slice(32 * j, 32 * j + 32)
                    dst = km[rows, 8 * hf:8 * hf + 8, :].rearrange("p (g j) n -> p g j n", g=2)[:, :, j, :]
                    sp.dma_start(dst.bitcast(F32), kb[rows, par(c), 2 * hf:2 * hf + 2, :].bitcast(F32)).then_inc(s[f"km_in{hf}"], 16)

            def body0(b):
                if ahead(b, 1):
                    alone(off(b, 1), 1)
                if ahead(b, 3):
                    context(0, off(b, 3))
                if ahead(b, 2):
                    alone(off(b, 2), 0)

            sp.wait_ge(s["km_clear"], 1)
            alone((0, 0), 0)
            batches(sp, body0)

            def tiles(l):
                sp.wait_ge(*after(l, "ends_ready", 1))
                for e in range(E):
                    row = sp.value_load(ends_i[0:1, l, e:e + 1], min_val=e * REGION, max_val=e * REGION + T)
                    sp.dma_start(xs[l][bass.ds(row, P), :], blank[:, :]).then_inc(s[f"slots_blank{l}"], 16)
                sp.wait_ge(s[f"slots_blank{l}"], 16 * (1 + E))
                sp.wait_ge(*after(l, "table_ready", 1))
                sp.wait_ge(*after(l, "sent0", 16 * QT * TOPK * B // 2))
                sp.wait_ge(*after(l, "sent1", 16 * QT * TOPK * B // 2))
                for k in range(4):
                    row = sp.value_load(tile_row[0:1, l, k:k + 1], min_val=0, max_val=ROWS - P)
                    sp.dma_start(xt[:, k, :], xs[l][bass.ds(row, P), :]).then_inc(s[f"xe_in{k}"], 16)
                with sp.Fori(1, NTILE // 4) as i:
                    for k in range(4):
                        sp.wait_ge(*after(l, "e_x", 4 * i + k - 3))
                        sp.wait_ge(*after(l, "e_dst", 4 * i + k - 3))
                        settle(sp)
                        row = sp.value_load(tile_row[0:1, l, bass.ds(4 * i + k, 1)], min_val=0, max_val=ROWS - P)
                        sp.dma_start(xt[:, k, :], xs[l][bass.ds(row, P), :]).then_inc(s[f"xe_in{k}"], 16)

            def results(l, c):
                for ch in range(TOPK):
                    src = yc[l][bass.ds(ch * T + no(c) * S, S), :].rearrange("(t p) d -> p t d", p=P)
                    sp.dma_start(ybuf[:, par(c), ch, :, :], src).then_inc(s[f"y_in{par(c)}"], 16)

            def all_out(l):
                for k in range(4):
                    sp.wait_ge(*after(l, f"es_out{k}", 16 * (NTILE // 4)))

            tiles(0)
            all_out(0)

            for k in range(2):
                results(0, (0, k))
                sp.dma_start(ct[:, k, :], a["ctxT"][:, k * S:(k + 1) * S]).then_inc(s[f"ctx_in{k}"], 16)
            sp.dma_start(w_dn[:, 0:E * C1 * D], a["wd"]).then_inc(s["wd_in"], 16)

            with sp.Fori(0, 3) as i:
                for k in (2, 3):
                    sp.wait_ge(*after(0, "comb", no((i, k)) - 1))
                    settle(sp)
                    results(0, (i, k))
                    context(1, (i, k))

            tiles(1)
            all_out(1)
            for q in range(4):
                for ch in range(TOPK):
                    src = yc[1][ch * T + q * T // 4:ch * T + (q + 1) * T // 4, :].rearrange("(t p) d -> p t d", p=P)
                    sp.dma_start(yfin[:, ch, q * TT // 4:(q + 1) * TT // 4, :], src).then_inc(s[f"fin_in{q}"], 16)
        @block.tensor
        def _(pe):
            m = ps[:, 7, :]

            def transpose_x(l, c, free):
                if free:
                    pe.wait_ge(*free)
                pe.wait_ge(*after(l, "xn_ready", no(c) + 1))
                for t in range(QT):
                    tr = pe.transpose(m[:, t * P:(t + 1) * P], xn[:, par(c), t, :], ident)
                tr.then_inc(s["xt_psum"], 1)

            def project0(c, u):
                w, gp = 1 - u % 2, u // 2
                if u == 0:
                    pe.wait_ge(*after(0, "x_split", no(c) + 1))
                    pe.wait_ge(*after(0, "ctx_split", no(c) + 1))
                    need(pe, *after(0, "qk_ready", 4 * no(c)))
                elif u == 1:
                    need(pe, s["v_evac"], no(c))
                else:
                    pe.wait_ge(*after(0, "qk_ready", 4 * no(c) + 4 - u))
                sel = cstb("selk" if w else "selq")[0:H, :]
                for gi in range(2):
                    g = 2 * gp + gi
                    o = ps[:, BANK0[u], gi * S:(gi + 1) * S]
                    for n, (i, j) in enumerate(((0, 0), (1, 0), (0, 1))):
                        pe.matmul(o, wqk[:, w, i, g * P:(g + 1) * P], hl[:, par(c), w, j, :], start=(n == 0), stop=False)
                    mm = pe.matmul(o, sel[:, g * P:(g + 1) * P], maskb[:, bass.ds(no(c), 1), :], start=False, stop=True)
                mm.then_inc(s["qk_psum"], 1)

            def values0(c):
                pe.wait_ge(*after(0, "qk_ready", 4 * no(c) + 3))
                for t in range(QT):
                    mm = pe.matmul(ps[:, 4, t * P:(t + 1) * P], ct[:, par(c), t * P:(t + 1) * P], wv0[:, :],
                                   start=True, stop=True)
                mm.then_inc(s["v_psum"], 1)

            def scores_q(c, h):
                g, j = divmod(h, HB)
                if h % 8 == 0:
                    pe.wait_ge(*after(0, "qk_ready", 4 * no(c) + 2 + h // 4))
                    pe.wait_ge(s[f"km_in{h // 8}"], 16 * HB * (no(c) + 1))
                need(pe, s["a_max"], H * no(c) + h - 1)
                for t in range(QT):
                    mm = pe.matmul(ps[:, h % 2, t * S:(t + 1) * S], qb[:, par(c), g, t * P:(t + 1) * P], km[:, h, :],
                                   start=True, stop=True)
                mm.then_inc(s["a_psum"], 1)

            def transpose_max(c, gp):
                pe.wait_ge(s["a_max"], H * no(c) + 8 * gp + 8)
                for t in range(QT):
                    tr = pe.transpose(m[:, t * P:(t + 1) * P], mx0[:, gp, t, :], ident)
                tr.then_inc(s["mt_psum"], 1)

            def scores_k(b, h):
                g, j = divmod(h, HB)
                if h % 8 == 0:
                    pe.wait_ge(s["qm_ready"], 2 * no(b) + h // 8 + 1)
                need(pe, s["b_exp"], H * no(b) + h - 1)
                for t in range(QT):
                    mm = pe.matmul(ps[:, 2 + h % 2, t * S:(t + 1) * S], kb[32 * j:32 * j + 32, par(b), g, t * P:(t + 1) * P],
                                   qb[32 * j:32 * j + 32, par(b), g, :], start=True, stop=True)
                mm.then_inc(s["b_psum"], 1)

            def mix0(b, g):
                pe.wait_ge(s["b_exp"], H * no(b) + HB * (g + 1))
                if g == 0:
                    pe.wait_ge(s["v_evac"], no(b) + 1)
                if g % 2 == 0:
                    need(pe, *after(0, "pv_evac", 2 * no(b) + g // 2))
                for t in range(QT):
                    for j in range(HB):
                        h = HB * g + j
                        mm = pe.matmul(ps[32 * j:32 * j + 32, 6, (g % 2) * S:(g % 2 + 1) * S], v0[:, par(b), t, h, :],
                                       pt0[:, h % 8, t * S:(t + 1) * S], start=(t == 0), stop=(t == QT - 1),
                                       skip_group_check=True)
                mm.then_inc(s["pv_psum"], 1)

            def untranspose0(b, t):
                if t == 0:
                    pe.wait_ge(*after(0, "pv_evac", 2 * no(b) + 2))
                else:
                    pe.wait_ge(s["o_mul"], 2 * no(b) + 1)
                for g in range(G):
                    tr = pe.transpose(m[:, g * P:(g + 1) * P], ot0[:, par(b), g, t * P:(t + 1) * P], ident)
                tr.then_inc(s["ot_psum"], 1)
            def transpose_t2(l, b, free):
                if free:
                    pe.wait_ge(*free)
                pe.wait_ge(*after(l, "pay_ready", no(b) + 1))
                for t in range(QT):
                    tr = pe.transpose(m[:, t * P:(t + 1) * P], pay[:, par(b), t, 0, 0:D], ident)
                tr.then_inc(s["t2_psum"], 1)

            def logits(l, b, free):
                if free:
                    pe.wait_ge(*free)
                pe.wait_ge(*after(l, "t2_evac", no(b) + 1))
                for t in range(QT):
                    mm = pe.matmul(m[:, t * E:(t + 1) * E], xnt[:, t * P:(t + 1) * P], wr[:, l, :], start=True, stop=True)
                mm.then_inc(s["lg_psum"], 1)

            def prefix(l, b, free):
                if free:
                    pe.wait_ge(*free)
                pe.wait_ge(*after(l, "hotb_done", no(b) + 1))
                tri, ones = cstb("tri"), cstb("ones")
                pe.matmul(m[:, 0:E], tri, hotb[:, 0, :], start=True, stop=True)
                pe.matmul(m[:, E:2 * E], tri, hotb[:, 1, :], start=True, stop=False)
                pe.matmul(m[:, E:2 * E], ones, hotb[:, 0, :], start=False, stop=True)
                pe.matmul(m[:, 2 * E:3 * E], ones, hotb[:, 0, :], start=True, stop=False)
                pe.matmul(m[:, 2 * E:3 * E], ones, hotb[:, 1, :], start=False, stop=True).then_inc(s["pfx_psum"], 1)

            pe.wait_ge(s["consts_in"], 16)
            def body0(b):
                c, c2, d = off(b, 1), off(b, 2), off(b, -1)
                for n in range(H):
                    if n == 1 and ahead(b, -1):
                        mix0(d, 3)
                    if ahead(b, 0):
                        scores_k(b, n)
                    if ahead(b, 1):
                        scores_q(c, n)
                    if n == 0 and ahead(b, 0):
                        pe.wait_ge(s["qm_ready"], 2 * no(b) + 1)
                        need(pe, *after(0, "pos_done", no(b) - 1))
                        transpose_max(b, 1)
                    if n in (0, 2) and ahead(b, 1):
                        project0(c, 2 + n // 2)
                    if n == 2 and ahead(b, -1):
                        if ahead(b, 0):
                            pe.wait_ge(s["qm_ready"], 2 * no(b) + 2)
                        else:
                            pe.wait_ge(*after(0, "pos_done", no(d)))
                        untranspose0(d, 0)
                    if n == 3 and ahead(b, -1):
                        untranspose0(d, 1)
                    if n == 4 and ahead(b, 1):
                        values0(c)
                    if n == 6 and ahead(b, 2):
                        need(pe, s["qm_ready"], 2 * no(b) + 2)
                        need(pe, s["o_mul"], 2 * no(d) + 2)
                        need(pe, *after(0, "x_split", no(c) + 1))
                        transpose_x(0, c2, None)
                    if n == 9 and ahead(b, 1):
                        if ahead(b, 2):
                            pe.wait_ge(*after(0, "x_split", no(c2) + 1))
                        else:
                            pe.wait_ge(s["o_mul"], 2 * no(d) + 2)
                        transpose_max(c, 0)
                    if n in (5, 9, 13) and ahead(b, 0):
                        mix0(b, n // 4 - 1)
                    if n == 11 and ahead(b, -1):
                        transpose_t2(0, d, (s["qm_ready"], 2 * no(c) + 1) if ahead(b, 1) else (s["o_mul"], 2 * no(d) + 2))
                    if n in (9, 11) and ahead(b, 2):
                        project0(c2, (n - 9) // 2)
                    if n == 12 and ahead(b, -1):
                        logits(0, d, None)
                    if n == 15 and ahead(b, -1):
                        prefix(0, d, None)

            transpose_x(0, (0, 0), None)
            pe.wait_ge(s["cb_ready"], 16)
            pe.wait_ge(s["wqk_split"], 1)
            pe.wait_ge(s["mask_ready"], 1)
            pe.wait_ge(s["wv_in"], 32)
            pe.wait_ge(s["wr_in"], 48)
            project0((0, 0), 0)
            project0((0, 0), 1)
            batches(pe, body0)
            def experts(l):
                pe.wait_ge(*after(l, "table_ready", 1))
                pe.wait_ge(s["up_lo" if l else "wup_split"], 2 * E if l else E)
                pe.wait_ge(s["wd_in" if l else "w2_in"], 16)
                pe.wait_ge(*after(l, "pos_done", B))
                if l == 1:
                    pe.wait_ge(s["he_pad"], 1)
                cc, ff = (C1, F1) if l else (C0, F0)

                def step(t, known, table):
                    e_up = expert(table, t, 1) if live(known, 1) else None
                    e_dn = expert(table, t, 3) if live(known, 3) else None
                    if live(known, 0):
                        pe.wait_ge(*after(l, f"xe_in{t[1] % 4}", 16 * (tq(t) + 1)))
                        if known:
                            pe.wait_ge(*after(l, "e_xlo", tno(t)))
                        pe.transpose(ps[:, 0, 0:P], xt[:, t[1] % 4, 0:D], ident).then_inc(s["e_x"], 1)
                    if live(known, 1):
                        u = off(t, -1)
                        pe.wait_ge(*after(l, "e_xlo", tno(u) + 1))
                        if known > 2:
                            pe.wait_ge(*after(l, "e_hcopy", tno(u) - 1))
                        for half_ in range(2 if l else 1):
                            bk = 1 + 2 * par(u) + half_ if l else 1 + par(u)
                            for n, (i, j) in enumerate(((0, 0), (1, 0), (0, 1))):
                                w = w_up[:, bass.ds(e_up * (ff * (4 if l else 2)) + (2 * half_ + j) * ff, ff)]
                                mm = pe.matmul(ps[:, bk, 0:ff], ex[:, par(u), i, :], w, start=(n == 0), stop=(n == 2))
                        mm.then_inc(s["e_h"], 1)
                    if live(known, 2):
                        u = off(t, -2)
                        pe.wait_ge(*after(l, "e_hcopy", tno(u) + 1))
                        if known > 3:
                            pe.wait_ge(*after(l, "e_htev", tno(u) - 1))
                        for k in range(cc):
                            tr = pe.transpose(ps[:, 5 + par(u), k * P:(k + 1) * P], he[:, par(u), k * P:(k + 1) * P], ident)
                        tr.then_inc(s["e_ht"], 1)
                    if live(known, 3):
                        u = off(t, -3)
                        pe.wait_ge(*after(l, "e_htev", tno(u) + 1))
                        if known > 3:
                            pe.wait_ge(*after(l, "e_yev", tno(u)))
                        for k in range(cc):
                            mm = pe.matmul(ps[:, 7, 0:D], ht[:, par(u), k * P:(k + 1) * P],
                                           w_dn[:, bass.ds(e_dn * (cc * D) + k * D, D)], start=(k == 0), stop=(k == cc - 1))
                        mm.then_inc(s["e_y"], 1)

                steps(pe, step, lambda i: experts_of(pe, l, i))

            experts(0)

            def project1(c, u, bank=7):
                w, mm_ = u // 4, 2 * (u % 4)
                if u == 0:
                    pe.wait_ge(*after(1, "x_split", no(c) + 1))
                if u == 4:
                    pe.wait_ge(*after(1, "ctx_split", no(c) + 1))
                for k in range(2):
                    for n, (i, j) in enumerate(((0, 0), (1, 0), (0, 1))):
                        mm = pe.matmul(ps[:, bank, k * S:(k + 1) * S], w1p[:, w, i, (mm_ + k) * P:(mm_ + k + 1) * P],
                                       hl[:, par(c), w, j, :], start=(n == 0), stop=(n == 2))
                mm.then_inc(s["qk_psum"], 1)

            def project1_after(c, u, free):
                if free:
                    pe.wait_ge(*free)
                project1(c, u)

            def values1(c, n, free, bank=7):
                t, hf = divmod(n, 2)
                pe.wait_ge(*free)
                for k, (i, j) in enumerate(((0, 0), (1, 0), (0, 1))):
                    mm = pe.matmul(ps[:, bank, :], hl[:, par(c), 1, i, t * P:(t + 1) * P], w1p[:, 2, j, hf * 512:(hf + 1) * 512],
                                   start=(k == 0), stop=(k == 2))
                mm.then_inc(s["v_psum"], 1)

            def scores1(b, pp, first):
                if pp == 0:
                    pe.wait_ge(*after(1, "qk_ready", 8 * no(b) + 8))
                if not (first and pp < 2):
                    pe.wait_ge(s["s_exp"], 8 * no(b) + pp - 1)
                for e in range(2):
                    bk = ps[:, 2 * (pp % 2) + e, :]
                    rows = slice(64 * e, 64 * e + 64)
                    pe.matmul(bk[:, 0:P], qt1[rows, par(b), pp, 0:P], kt1[rows, par(b), pp, 0:P],
                              start=True, stop=True, skip_group_check=True)
                    pe.matmul(bk[:, P:3 * P], qt1[rows, par(b), pp, P:2 * P], kt1[rows, par(b), pp, :],
                              start=False, stop=True, skip_group_check=True)
                    mm = pe.matmul(bk[:, 0:3 * P].rearrange("p (c n) -> p c n", c=3)[:, 0:3:2, :], cstb("ident"),
                                   cstb("causal").rearrange("p (c n) -> p c n", c=2), start=False, stop=True,
                                   skip_group_check=True)
                mm.then_inc(s["s_psum"], 1)

            def turn1(b, pp, first):
                n = 8 * no(b) + pp
                pe.wait_ge(s["s_norm"], n + 1)
                if not (first and pp == 0):
                    pe.wait_ge(s["pt_evac"], n)
                for e in range(2):
                    for k in range(3):
                        tr = pe.transpose(ps[:, 4 + e, k * P:(k + 1) * P], p1[:, pp % 2, e, k * P:(k + 1) * P], ident)
                tr.then_inc(s["pt_psum"], 1)

            def mix1(b, pp, first):
                n = 8 * no(b) + pp
                pe.wait_ge(s["pt_evac"], n + 1)
                if pp == 0:
                    pe.wait_ge(s["v1_evac"], 4 * no(b) + 4)
                if pp % 2 == 0 and not (first and pp == 0):
                    pe.wait_ge(*after(1, "pv_evac", 4 * no(b) + pp // 2))
                c0 = (pp % 2) * S
                for e in range(2):
                    pe.matmul(ps[64 * e:64 * e + 64, 6, c0:c0 + S], v1[:, par(b), 0, (2 * pp + e) * DK1:(2 * pp + e + 1) * DK1],
                              pt1[:, pp % 2, e, 0:S], start=True, stop=False, skip_group_check=True)
                for e in range(2):
                    mm = pe.matmul(ps[64 * e:64 * e + 64, 6, c0 + P:c0 + S],
                                   v1[:, par(b), 1, (2 * pp + e) * DK1:(2 * pp + e + 1) * DK1],
                                   pt1[:, pp % 2, e, S:3 * P], start=False, stop=True, skip_group_check=True)
                mm.then_inc(s["pv_psum"], 1)

            def output1(b, free):
                pe.wait_ge(*free)
                pe.wait_ge(*after(1, "pv_evac", 4 * no(b) + 4))
                for t in range(QT):
                    for k in range(M1):
                        mm = pe.matmul(m[:, t * P:(t + 1) * P], ot1[:, k, t * P:(t + 1) * P], wo1[:, k, :],
                                       start=(k == 0), stop=(k == M1 - 1))
                mm.then_inc(s["op_psum"], 1)

            pe.wait_ge(s["wl_split"], 3)
            pe.wait_ge(s["wo_in"], 16)
            pe.wait_ge(*after(0, "e_yev", NTILE))

            def qk(c, u):
                return after(1, "qk_ready", 8 * no(c) + u)

            def vv(c, n):
                return (s["v1_evac"], 4 * no(c) + n)

            def prologue1():
                c = (0, 0)
                transpose_x(1, c, None)
                for u in range(8):
                    project1(c, u, u)
                for n in range(4):
                    values1(c, n, qk(c, 5 + n), 4 + n)
                pe.wait_ge(*vv(c, 4))

            def body1(b, ahead, behind):
                first = no(b) == 0 if isinstance(b[0], int) else False
                c, d = off(b, 1), off(b, -1)
                for p in range(M1):
                    scores1(b, p, first)
                    if ahead:
                        if p == 0:
                            pe.wait_ge(*vv(c, 0))
                            need(pe, *after(1, "pos_done", no(d)))
                            transpose_x(1, c, None)
                        elif p < 4:
                            project1_after(c, 2 * p - 1, qk(c, 2 * p - 1))
                        elif p == 4:
                            project1_after(c, 6, after(1, "x_add", 2 * no(d) + 2) if behind else qk(c, 6))
                        elif p == 5:
                            values1(c, 0, qk(c, 8))
                        elif p == 6:
                            values1(c, 2, vv(c, 2))
                    if p == 7 and behind:
                        logits(1, d, None)

                    if p >= 2:
                        turn1(b, p - 2, first)
                    elif behind:
                        turn1(d, 6 + p, False)
                    if p == 7 and ahead:
                        values1(c, 3, after(1, "lg_done", no(d) + 1) if behind else vv(c, 3))

                    if p >= 3:
                        mix1(b, p - 3, first)
                    elif behind:
                        mix1(d, 5 + p, False)
                    if ahead:
                        if p == 0:
                            project1(c, 0)
                        elif p in (1, 2):
                            project1_after(c, 2 * p, qk(c, 2 * p))
                        elif p == 4:
                            project1_after(c, 7, qk(c, 7))
                        elif p == 5:
                            values1(c, 1, vv(c, 1))
                    if p == 3 and behind:
                        output1(d, qk(c, 6) if ahead else after(1, "pos_done", no(d)))
                    if p == 6 and behind:
                        transpose_t2(1, d, vv(c, 3) if ahead else None)
                    if p == 7 and behind:
                        prefix(1, d, vv(c, 4) if ahead else None)

            def epilogue1(b):
                mix1(b, 5, False)
                for pp in (6, 7):
                    turn1(b, pp, False)
                    mix1(b, pp, False)
                output1(b, after(1, "pos_done", no(b)))
                transpose_t2(1, b, None)
                logits(1, b, None)
                prefix(1, b, None)

            pipeline(pe, prologue1, body1, epilogue1)
            experts(1)

        @block.scalar
        def _(act):
            act.dma_start(stage[:, 0, :], a["wqk"]).then_inc(s["wqk_in"], 16)
            act.dma_start(bias0[:, :, :], a["bias0"]).then_inc(s["bias_in"], 16)
            act.dma_start(maskraw, a["mask"]).then_inc(s["mask_in"], 16)
            m = ps[:, 7, :]

            def x_high(l, c):
                act.wait_ge(*after(l, "xt_psum", no(c) + 1))
                act.activation(hl[:, par(c), 0, 0, :], m[:, 0:S], ACT.Copy).then_inc(s["x_hi"], 1)

            def low_base(c, u):
                w, gp = 1 - u % 2, u // 2
                act.wait_ge(*after(0, "qk_psum", 4 * no(c) + u + 1))
                need(act, *after(0, "qk_ready", 4 * no(c) + u))
                for gi in range(2):
                    g = 2 * gp + gi
                    ac = act.activation(chib[:, gi, :], ps[:, BANK0[u], gi * S:(gi + 1) * S], ACT.Identity,
                                        bias=bias0c[:, w, g:g + 1], scale=cst("ck" if w else "cq"))
                ac.then_inc(s["qk_chi"], 1)

            def exps0(b, h):
                act.wait_ge(s["b_psum"], H * no(b) + h + 1)
                if h % HB == 0:
                    need(act, *after(0, "pv_psum", 4 * no(b) + h // HB - 1))
                act.activation(pt0[:, h % 8, :], ps[:, 2 + h % 2, :], ACT.Exp, scale=SC0).then_inc(s["b_exp"], 1)

            def take_out0(b, hf):
                act.wait_ge(*after(0, "pv_psum", 4 * no(b) + 2 * hf + 2))
                act.activation(ot0[:, par(b), 2 * hf:2 * hf + 2, :], ps[:, 6, :].rearrange("p (g n) -> p g n", g=2),
                               ACT.Copy).then_inc(s["pv_evac"], 1)
            def t2_out(l, b):
                act.wait_ge(*after(l, "t2_psum", no(b) + 1))
                act.activation(xnt[:, :], m[:, 0:S], ACT.Copy).then_inc(s["t2_evac"], 1)

            def weight_exp(l, b):
                act.wait_ge(*after(l, "diff_done", no(b) + 1))
                act.activation(edl[:, :], dlt[:, :], ACT.Exp).then_inc(s["exp_done"], 1)

            act.wait_ge(s["wqk_in"], 16)
            act.activation(wqk[:, :, 0, :], stage[:, 0, :].rearrange("p (w n) -> p w n", w=2), ACT.Copy).then_inc(s["wqk_hi"], 1)
            act.wait_ge(s["mask_in"], 16)
            act.activation(maskb[:, :, :], maskraw, ACT.Copy).then_inc(s["mask_ready"], 1)
            act.wait_ge(s["consts_in"], 16)
            act.wait_ge(s["bias_ready"], 2)

            def body0(b):
                c, c2, d = off(b, 1), off(b, 2), off(b, -1)
                for n in range(H):
                    if ahead(b, 0):
                        exps0(b, n)
                    if n == 1 and ahead(b, -1):
                        take_out0(d, 1)
                    if n in (0, 2) and ahead(b, 1):
                        low_base(c, 2 + n // 2)
                    if n == 6 and ahead(b, 2):
                        x_high(0, c2)
                    if n == 9 and ahead(b, 0):
                        take_out0(b, 0)
                    if n == 11 and ahead(b, -1):
                        t2_out(0, d)
                    if n in (9, 11) and ahead(b, 2):
                        low_base(c2, (n - 9) // 2)
                    if n == 15 and ahead(b, -1):
                        weight_exp(0, d)

            x_high(0, (0, 0))
            low_base((0, 0), 0)
            low_base((0, 0), 1)
            batches(act, body0)
            def experts(l):
                def step(t, known, table):
                    if live(known, 0):
                        act.wait_ge(*after(l, "e_x", tno(t) + 1))
                        if known > 1:
                            act.wait_ge(*after(l, "e_h", tno(t) - 1))
                        act.activation(ex[:, par(t), 0, :], ps[:, 0, 0:P], ACT.Copy).then_inc(s["e_xhi"], 1)
                    if live(known, 1):
                        u = off(t, -1)
                        act.wait_ge(*after(l, "e_h", tno(u) + 1))
                        if l == 0:
                            if known > 2:
                                act.wait_ge(*after(l, "e_ht", tno(u) - 1))
                            act.activation(he[:, par(u), :], ps[:, 1 + par(u), :], ACT.Copy).then_inc(s["e_hcopy"], 1)
                        else:
                            if known > 2:
                                act.wait_ge(*after(l, "e_hcopy", tno(u) - 1))
                            act.activation(sg[:, par(u), :], ps[:, 1 + 2 * par(u), 0:F1], ACT.Silu).then_inc(s["e_hs"], 1)

                steps(act, step)

            for w in range(3):
                act.wait_ge(s[f"st_in{w % 2}"], 16 * (E // 2 + 1 + w // 2))
                act.activation(w1p[:, w, 0, :], stage[:, w % 2, :], ACT.Copy).then_inc(s["wl_hi"], 1)

            experts(0)

            def qk_out(c, u, bank=7):
                act.wait_ge(*after(1, "qk_psum", 8 * no(c) + u + 1))
                dst = (kt1 if u // 4 else qt1)[:, par(c), 2 * (u % 4):2 * (u % 4) + 2, :]
                act.activation(dst, ps[:, bank, :].rearrange("p (k n) -> p k n", k=2), ACT.Copy).then_inc(s["qk_ready"], 1)

            def v_out(c, n, bank=7):
                t, hf = divmod(n, 2)
                act.wait_ge(*after(1, "v_psum", 4 * no(c) + n + 1))
                act.activation(v1[:, par(c), t, hf * 512:(hf + 1) * 512], ps[:, bank, :], ACT.Copy).then_inc(s["v1_evac"], 1)

            def load_piece(q):
                if q:
                    act.wait_ge(s["wl_split"] if q == 1 else s["up_lo"], 3 if q == 1 else q - 1)
                act.dma_start(stage[:, q % 2, 0:F1], a["wgu"][:, q * F1:(q + 1) * F1]).then_inc(s[f"up_in{q % 2}"], 16)

            act.wait_ge(s["wl_split"], 3)
            load_piece(0)

            def exps1(b, pp, first):
                n = 8 * no(b) + pp
                act.wait_ge(s["s_nb"], n + 1)
                if not (first and pp < 2):
                    act.wait_ge(s["pt_psum"], n - 1)
                    act.wait_ge(s["s_rec"], n - 1)
                for e in range(2):
                    bk = ps[:, 2 * (pp % 2) + e, :]
                    for t, cols in ((0, slice(0, P)), (1, slice(P, 3 * P))):
                        ac = act.activation(p1[:, pp % 2, e, cols], bk[:, cols], ACT.Exp, scale=SC1,
                                            bias=nb1[:, pp % 2, e, t:t + 1], accum_out=rs1[:, pp % 2, e, t:t + 1])
                ac.then_inc(s["s_exp"], 1)

            def take_out1(b, k, first=False):
                act.wait_ge(*after(1, "pv_psum", 8 * no(b) + 2 * k + 2))
                if k == 0 and not first:
                    act.wait_ge(s["op_psum"], no(b))
                act.activation(ot1[:, 2 * k:2 * k + 2, :], ps[:, 6, :].rearrange("p (k n) -> p k n", k=2),
                               ACT.Copy).then_inc(s["pv_evac"], 1)

            def prologue1():
                c = (0, 0)
                x_high(1, c)
                for u in range(8):
                    qk_out(c, u, u)
                for n in range(4):
                    v_out(c, n, 4 + n)

            def body1(b, ahead, behind):
                first = no(b) == 0 if isinstance(b[0], int) else False
                c, d = off(b, 1), off(b, -1)
                for p in range(M1):
                    if ahead:
                        if p == 0:
                            x_high(1, c)
                        elif p in (1, 2, 3, 4):
                            qk_out(c, {1: 1, 2: 3, 3: 5, 4: 6}[p])
                        elif p in (5, 6):
                            v_out(c, 2 * p - 10)
                    if p == 7 and ahead:
                        v_out(c, 3)
                    exps1(b, p, first)
                    if p in (0, 2) and behind:
                        take_out1(d, 2 + p // 2)
                    if p in (4, 6):
                        take_out1(b, p // 2 - 2, first)
                    if ahead and p in (0, 1, 2, 4):
                        qk_out(c, {0: 0, 1: 2, 2: 4, 4: 7}[p])
                    if p == 6 and behind:
                        t2_out(1, d)
                    if p == 5 and ahead:
                        v_out(c, 1)
                    if p == 7 and behind:
                        weight_exp(1, d)
                    for q in pieces(b)[p:p + 1]:
                        if q + 1 < 2 * E:
                            load_piece(q + 1)
                        act.wait_ge(s[f"up_in{q % 2}"], 16 * (q // 2 + 1))
                        st, hi, _ = piece_parts(q)
                        act.activation(hi, st, ACT.Copy).then_inc(s["up_hi"], 1)

            def epilogue1(b):
                take_out1(b, 2)
                take_out1(b, 3)
                t2_out(1, b)
                weight_exp(1, b)

            pipeline(act, prologue1, body1, epilogue1)
            experts(1)

            for q in range(4):
                act.wait_ge(s["fin_sum"], q + 1)
                dst = out[q * T // 4:(q + 1) * T // 4, :].rearrange("(t p) d -> p t d", p=P)
                act.dma_start(dst, x_sb[:, q * TT // 4:(q + 1) * TT // 4, :]).then_inc(s["out_done"], 16)
            act.wait_ge(s["out_done"], 64)
        @block.vector
        def _(ve):
            m = ps[:, 7, :]

            def stats(l, c, z, parts=(0, 1)):
                if 0 in parts:
                    settle(ve)
                    for t in range(QT):
                        ve.bn_stats(bn6[:, z, t, :], tokens(c, t)).then_inc(s[f"ln_stats{z}"], 1)
                if 1 in parts:
                    ve.wait_ge(*after(l, f"ln_stats{z}", 4 * no(c) + 2))
                    settle(ve)
                    for t in range(QT):
                        ve.bn_aggr(mv[:, z, t, :], bn6[:, z, t, :]).then_inc(s[f"ln_stats{z}"], 1)

            def normalise(l, c, z, dst, ready):
                ve.wait_ge(*after(l, f"rs_ready{z}", no(c) + 1))
                for t in range(QT):
                    op = ve.tensor_scalar(dst(t), tokens(c, t), mv[:, z, t, 0:1], rstd[:, z, t:t + 1], ALU.subtract, ALU.mult)
                op.then_inc(s[ready], 1)
                ve.wait_ge(*after(l, ready, no(c) + 1))

            def tokens(b, t):
                return x_sb[:, bass.ds(QT * no(b) + t, 1), :].rearrange("p a d -> p (a d)")

            def norm_in(l, c, used=True):
                if used:
                    ve.wait_ge(*after(l, "xt_psum", no(c) - 1))
                normalise(l, c, 0, lambda t: xn[:, par(c), t, :], "xn_ready")

            def norm_out(l, b, used):
                if used:
                    ve.wait_ge(*after(l, f"sent{par(b)}", 16 * QT * TOPK * half(b)))
                normalise(l, b, 1, lambda t: pay[:, par(b), t, 0, 0:D], "pay_ready")

            def x_low(l, c):
                ve.wait_ge(*after(l, "x_hi", no(c) + 1))
                ve.tensor_tensor(hl[:, par(c), 0, 1, :], m[:, 0:S], hl[:, par(c), 0, 0, :], ALU.subtract).then_inc(s["x_split"], 1)

            def qk0(c, u):
                w, gp = 1 - u % 2, u // 2
                ve.wait_ge(s["qk_chi"], 4 * no(c) + u + 1)
                for gi in range(2):
                    g = 2 * gp + gi
                    op = ve.scalar_tensor_tensor(out=(kb if w else qb)[:, par(c), g, :], in0=ps[:, BANK0[u], gi * S:(gi + 1) * S],
                                                 scalar=bias0[:, w, g:g + 1], in1=chib[:, gi, :],
                                                 op0=ALU.add, op1=ALU.subtract)
                op.then_inc(s["qk_ready"], 1)

            def values0(c):
                ve.wait_ge(*after(0, "v_psum", no(c) + 1))
                for t in range(QT):
                    op = ve.tensor_tensor(v0[:, par(c), t, :, 0:DK0], ps[:, 4, t * P:(t + 1) * P].rearrange("p (h n) -> p h n", h=H),
                                          bv_bc[:, :].rearrange("p (h n) -> p h n", h=H), ALU.add)
                op.then_inc(s["v_evac"], 1)

            def row_max(c, h):
                g, j = divmod(h, HB)
                ve.wait_ge(s["a_psum"], H * no(c) + h + 1)
                if h % 8 == 0:
                    need(ve, s["mt_psum"], 2 * no(c) - 1 + h // 8)
                ve.tensor_reduce(mx0[:, g // 2, :, 32 * j + 26 + g], ps[:, h % 2, :].rearrange("p (t n) -> p t n", t=QT), AX, ALU.max).then_inc(s["a_max"], 1)

            def place_max(c, gp):
                ve.wait_ge(s["mt_psum"], 2 * no(c) + gp + 1)
                q = qb[:, par(c), 2 * gp:2 * gp + 2, :]
                ve.scalar_tensor_tensor(out=q, in0=m[:, None, 0:S].broadcast_to([P, 2, S]), scalar=-1.0, in1=q,
                                        op0=ALU.mult, op1=ALU.add).then_inc(s["qm_ready"], 1)

            def attend0(b, t, parts=(0, 1, 2)):
                n = 2 * no(b) + t
                o = m.rearrange("p (h n) -> p h n", h=H)
                if 0 in parts:
                    ve.wait_ge(s["ot_psum"], n + 1)
                    ve.reciprocal(rec0[:, :], o[:, :, DK0]).then_inc(s["o_rec"], 1)
                if 1 in parts:
                    ve.wait_ge(s["o_rec"], n + 1)
                    ve.tensor_tensor(att0[:, :, :], o[:, :, 0:DK0], rec0[:, :, None].broadcast_to([P, H, DK0]), ALU.mult).then_inc(s["o_mul"], 1)
                if 2 in parts:
                    ve.wait_ge(s["o_mul"], n + 1)
                    ve.tensor_tensor(tokens(b, t), tokens(b, t), att0[:, :, :].rearrange("p h n -> p (h n)"), ALU.add).then_inc(s["x_add"], 1)

            def choose(l, b, parts=range(6)):
                n = no(b)
                if 0 in parts:
                    ve.wait_ge(*after(l, "lg_psum", n + 1))
                    src = m[:, 0:QT * E].rearrange("p (t e) -> p t e", t=QT)
                    if l == 0:
                        ve.tensor_tensor(lg[:, :, :], src, br_bc[:, None, :].broadcast_to([P, QT, E]), ALU.add).then_inc(s["lg_done"], 1)
                    else:
                        ve.tensor_copy(lg[:, :, :], src).then_inc(s["lg_done"], 1)
                if 1 in parts:
                    ve.wait_ge(*after(l, "lg_done", n + 1))
                    settle(ve)
                    for t in range(QT):
                        ve.max(top[:, t, :], lg[:, t, :]).then_inc(s["top_done"], 1)
                if 2 in parts:
                    ve.wait_ge(*after(l, "top_done", 5 * n + 2))
                    settle(ve)
                    for t in range(QT):
                        ve.max_index(topi[:, t, :], top[:, t, :], lg[:, t, :]).then_inc(s["top_done"], 1)
                    ve.tensor_tensor(dlt[:, :], top[:, :, 1], top[:, :, 0], ALU.subtract).then_inc(s["diff_done"], 1)
                if 3 in parts:
                    ve.wait_ge(*after(l, "top_done", 5 * n + 4))
                    ve.tensor_copy(topf[:, :, :], topi[:, :, 0:TOPK]).then_inc(s["top_done"], 1)
                if 4 in parts:
                    ve.wait_ge(*after(l, "top_done", 5 * n + 5))
                    ve.tensor_tensor(hot[:, :, :, :].rearrange("p t c e -> p (t c) e"),
                                     cst("choice")[:, None, 0:E].broadcast_to([P, QT * TOPK, E]),
                                     topf[:, :, :].rearrange("p t c -> p (t c)")[:, :, None].broadcast_to([P, QT * TOPK, E]),
                                     ALU.is_equal).then_inc(s["hot_done"], 1)
                if 5 in parts:
                    ve.wait_ge(*after(l, "hot_done", n + 1))
                    ve.tensor_tensor(hotb[:, :, :], hot[:, :, 0, :], hot[:, :, 1, :], ALU.add).then_inc(s["hotb_done"], 1)

            def weigh(l, b, parts=range(3)):
                n = no(b)
                w = wts[:, l, bass.ds(QT * n, QT), :]
                if 0 in parts:
                    ve.wait_ge(*after(l, "exp_done", n + 1))
                    ve.tensor_scalar(den[:, :], edl[:, :], 1.0, None, ALU.add).then_inc(s["wts_den"], 1)
                if 1 in parts:
                    ve.wait_ge(*after(l, "wts_den", n + 1))
                    ve.reciprocal(w[:, :, 0], den[:, :]).then_inc(s["wts_one"], 1)
                if 2 in parts:
                    ve.wait_ge(*after(l, "wts_one", n + 1))
                    ve.tensor_tensor(w[:, :, 1], edl[:, :], w[:, :, 0], ALU.mult).then_inc(s["wts_done"], 1)

            def place(l, b, parts=range(4)):
                n = no(b)
                bs = base[:, l, :]
                if 0 in parts:
                    ve.wait_ge(*after(l, "pfx_psum", n + 1))
                    need(ve, *after(l, "pos_done", n))
                    ve.tensor_tensor(pos[:, :, :], m[:, 0:QT * E].rearrange("p (t e) -> p t e", t=QT),
                                     bs[:, None, :].broadcast_to([P, QT, E]), ALU.add).then_inc(s["slot_chain"], 1)
                if 1 in parts:
                    ve.wait_ge(*after(l, "slot_chain", 3 * n + 1))
                    ve.tensor_tensor(bs, bs, m[:, QT * E:(QT + 1) * E], ALU.add).then_inc(s["pos_done"], 1)
                    ve.tensor_tensor(hp[:, :, :, :], hot[:, :, :, :], pos[:, :, None, :].broadcast_to([P, QT, TOPK, E]),
                                     ALU.mult).then_inc(s["slot_chain"], 1)
                if 2 in parts:
                    ve.wait_ge(*after(l, "slot_chain", 3 * n + 2))
                    ve.tensor_reduce(slotf[:, :, :], hp[:, :, :, :], AX, ALU.add).then_inc(s["slot_chain"], 1)
                if 3 in parts:
                    ve.wait_ge(*after(l, "slot_chain", 3 * n + 3))
                    ve.tensor_copy(sloti[:, par(b), :, :], slotf[:, :, :]).then_inc(s["slot_ready"], 1)

            def table(l):
                k = 0

                def link(op):
                    nonlocal k
                    k += 1
                    op.then_inc(s["table"], 1)
                    ve.wait_ge(*after(l, "table", k))

                one = slice(0, 1)
                ve.wait_ge(*after(l, "pos_done", B))
                ve.tensor_copy(ends_i[:, l, :], base[one, l, :]).then_inc(s["ends_ready"], 1)
                link(ve.tensor_tensor(cnt[:, :], base[one, l, :], cst("region")[one, :], ALU.subtract))
                link(ve.tensor_tensor(lots[:, :, :], cnt[:, :, None].broadcast_to([1, E, T // P]),
                                      cst("lots")[one, None, :].broadcast_to([1, E, T // P]), ALU.is_gt))
                link(ve.tensor_reduce(ntl[:, :], lots[:, :, :], AX, ALU.add))
                link(ve.tensor_tensor_scan(ends[:, :], cst("one8")[one, :], ntl[:, :], 0.0, ALU.mult, ALU.add))
                link(ve.tensor_tensor(past[:, :, :], cst("tile")[one, :, None].broadcast_to([1, NTILE, E]),
                                      ends[:, None, :].broadcast_to([1, NTILE, E]), ALU.is_ge))
                link(ve.tensor_reduce(which[:, :], past[:, :, :], AX, ALU.add))
                link(ve.tensor_tensor(pastn[:, :, :], past[:, :, :], ntl[:, None, :].broadcast_to([1, NTILE, E]), ALU.mult))
                link(ve.tensor_reduce(before[:, :], pastn[:, :, :], AX, ALU.add))
                link(ve.tensor_tensor(before[:, :], cst("tile")[one, :], before[:, :], ALU.subtract))
                link(ve.tensor_scalar(before[:, :], before[:, :], float(P), None, ALU.mult))
                link(ve.scalar_tensor_tensor(out=before[:, :], in0=which[:, :], scalar=float(REGION), in1=before[:, :],
                                             op0=ALU.mult, op1=ALU.add))
                link(ve.tensor_scalar(tile_row[:, l, :], before[:, :], float(E * REGION), None, ALU.min))
                link(ve.tensor_scalar(which[:, :], which[:, :], float(E - 1), None, ALU.min))
                for j in range(6):
                    part = whichp[:, j:j + 4 * (NTILE // 4) + 1:4]
                    if j == 0:
                        link(ve.tensor_copy(packf[:, :], part))
                    else:
                        link(ve.scalar_tensor_tensor(out=packf[:, :], in0=part, scalar=float(8 ** j), in1=packf[:, :],
                                                     op0=ALU.mult, op1=ALU.add))
                ve.tensor_copy(tile_e[:, l, :], packf[:, :]).then_inc(s["table_ready"], 1)
                ve.wait_ge(*after(l, "table_ready", 1))

            ve.wait_ge(s["consts_in"], 16)
            ve.wait_ge(s["bias_in"], 16)
            for w, c in ((0, "cq"), (1, "ck")):
                ve.tensor_scalar(bias0c[:, w, :], bias0[:, w, :], cst(c), None, ALU.mult).then_inc(s["bias_ready"], 1)
            for l in range(2):
                ve.tensor_copy(base[:, l, :], cst("region")).then_inc(s["base_set"], 1)
            ve.memset(whichp[:, :], 0.0).then_inc(s["base_set"], 1)
            ve.memset(mx0[:, :, :, :].rearrange("p g t n -> p (g t n)"), 0.0).then_inc(s["mx_clear"], 1)
            ve.wait_ge(s["mx_clear"], 1)
            ve.wait_ge(s["xa_in"], 16)

            def body0(b):
                c, c2, c3, d = off(b, 1), off(b, 2), off(b, 3), off(b, -1)
                has, has2, has3, behind = ahead(b, 1), ahead(b, 2), ahead(b, 3), ahead(b, -1)
                for n in range(H):
                    if has:
                        row_max(c, n)
                    if n == 0 and ahead(b, 0):
                        place_max(b, 1)
                    if n in (1, 3) and has:
                        qk0(c, 2 + n // 2)
                    if n == 2 and behind:
                        attend0(d, 0, (0,))
                        attend0(d, 0, (1,))
                    if n == 3 and behind:
                        attend0(d, 0, (2,))
                        attend0(d, 1, (0,))
                        attend0(d, 1, (1,))
                    if n == 4:
                        if behind:
                            attend0(d, 1, (2,))
                        if has2:
                            norm_in(0, c2, ahead(b, 0))
                        if behind:
                            ve.wait_ge(*after(0, "x_add", 2 * no(d) + 2))
                            stats(0, d, 1, (0,))
                    if n == 5 and behind:
                        stats(0, d, 1, (1,))
                    if n == 7 and has2:
                        x_low(0, c2)
                    if n == 8 and has:
                        values0(c)
                    if n == 8 and has3:
                        stats(0, c3, 0, (0,))
                    if n == 9 and has3:
                        stats(0, c3, 0, (1,))
                    if n == 9 and has:
                        place_max(c, 0)
                    if n == 9 and behind:
                        norm_out(0, d, ahead(b, -3))
                    if n == 10 and has2:
                        qk0(c2, 0)
                    if n == 12:
                        if behind:
                            choose(0, d, (0,))
                        if has2:
                            qk0(c2, 1)
                        if behind:
                            choose(0, d, (1,))
                    if n == 13 and behind:
                        choose(0, d, (2,))
                        choose(0, d, (3,))
                    if n == 14:
                        if behind:
                            choose(0, d, (4,))
                            choose(0, d, (5,))
                    if n == 15 and behind:
                        if not ahead(b, 0):
                            place(0, d)
                            table(0)
                            weigh(0, d)
                        else:
                            place(0, d, (0,))
                            for k in range(3):
                                weigh(0, d, (k,))
                                place(0, d, (1 + k,))

            stats(0, (0, 0), 0)
            ve.wait_ge(s["wqk_hi"], 1)
            ve.tensor_tensor(wqk[:, :, 1, :], stage[:, 0, :].rearrange("p (w n) -> p w n", w=2), wqk[:, :, 0, :],
                             ALU.subtract).then_inc(s["wqk_split"], 1)
            norm_in(0, (0, 0), False)
            stats(0, (0, 1), 0)
            x_low(0, (0, 0))
            qk0((0, 0), 0)
            qk0((0, 0), 1)
            for n in ("wv_in", "wr_in", "v0_ready", "xb_in", "base_set"):
                ve.wait_ge(s[n], {"wv_in": 32, "wr_in": 48, "v0_ready": 1, "xb_in": 16, "base_set": 3}[n])
            batches(ve, body0)
            def experts(l):
                if l == 0:
                    ve.wait_ge(s["b1_in"], 16)
                    ve.wait_ge(s["b2_in"], 16)
                else:
                    ve.memset(he[:, :, F1:FP1], 0.0).then_inc(s["he_pad"], 1)

                def step(t, known, table):
                    e2 = expert(table, t, 2) if l == 0 and live(known, 2) else None
                    e3 = expert(table, t, 3) if l == 0 and live(known, 3) else None
                    if live(known, 0):
                        ve.wait_ge(*after(l, "e_xhi", tno(t) + 1))
                        ve.tensor_tensor(ex[:, par(t), 1, :], ps[:, 0, 0:P], ex[:, par(t), 0, :], ALU.subtract).then_inc(s["e_xlo"], 1)
                    if l == 1 and live(known, 1):
                        u = off(t, -1)
                        ve.wait_ge(*after(l, "e_hs", tno(u) + 1))
                        if known > 2:
                            ve.wait_ge(*after(l, "e_ht", tno(u) - 1))
                        ve.tensor_tensor(he[:, par(u), 0:F1], sg[:, par(u), :], ps[:, 2 + 2 * par(u), 0:F1], ALU.mult).then_inc(s["e_hcopy"], 1)
                    if live(known, 2):
                        u = off(t, -2)
                        ve.wait_ge(*after(l, "e_ht", tno(u) + 1))
                        if known > 3:
                            ve.wait_ge(*after(l, "e_y", tno(u) - 1))
                        if l == 0:
                            for k in range(C0):
                                b1 = b1t[:, bass.ds(e2, 1), k]
                                op = ve.tensor_scalar(ht[:, par(u), k * P:(k + 1) * P], ps[:, 5 + par(u), k * P:(k + 1) * P],
                                                      b1, 0.0, ALU.add, ALU.max)
                            op.then_inc(s["e_htev"], 1)
                        else:
                            ve.tensor_copy(ht[:, par(u), 0:FP1], ps[:, 5 + par(u), 0:FP1]).then_inc(s["e_htev"], 1)
                    if live(known, 3):
                        u = off(t, -3)
                        ve.wait_ge(*after(l, "e_y", tno(u) + 1))
                        if not (known < 4 or (isinstance(u[0], int) and tno(u) < 4)):
                            ve.wait_ge(*after(l, f"es_out{u[1] % 4}", 16 * tq(u)))
                        if l == 0:
                            ve.tensor_tensor(ye[:, u[1] % 4, :], ps[:, 7, 0:D], b2_bc[:, bass.ds(e3 * D, D)], ALU.add).then_inc(s["e_yev"], 1)
                        else:
                            ve.tensor_copy(ye[:, u[1] % 4, :], ps[:, 7, 0:D]).then_inc(s["e_yev"], 1)

                steps(ve, step, (lambda i: None) if l else (lambda i: experts_of(ve, l, i)))

            for w in range(3):
                ve.wait_ge(s["wl_hi"], w + 1)
                ve.tensor_tensor(w1p[:, w, 1, :], stage[:, w % 2, :], w1p[:, w, 0, :], ALU.subtract).then_inc(s["wl_split"], 1)

            experts(0)

            def combine(l, c):
                ve.wait_ge(*after(l, f"y_in{par(c)}", 32 * (half(c) + 1)))
                for ch in range(TOPK):
                    for t in range(QT):
                        w = wts[:, l, bass.ds(QT * no(c) + t, 1), ch]
                        op = ve.scalar_tensor_tensor(out=tokens(c, t), in0=ybuf[:, par(c), ch, t, :], scalar=w,
                                                     in1=tokens(c, t), op0=ALU.mult, op1=ALU.add)
                    if ch == 0:
                        op.then_inc(s["comb_one"], 1)
                        ve.wait_ge(*after(l, "comb_one", no(c) + 1))
                op.then_inc(s["comb"], 1)
                ve.wait_ge(*after(l, "comb", no(c) + 1))

            def enter1(c):
                combine(0, c)
                stats(1, c, 0)

            def row_max1(b, pp, first):
                n = 8 * no(b) + pp
                r = pp % 2
                ve.wait_ge(s["s_psum"], n + 1)
                ve.tensor_reduce(mx1[:, r, :, :], ps[:, 2 * r:2 * r + 2, 0:3 * P].rearrange("p h (c n) -> p h c n", c=3),
                                 AX, ALU.max).then_inc(s["s_max"], 1)
                ve.wait_ge(s["s_max"], 2 * n + 1)
                ve.tensor_tensor(mx1[:, r, :, 1], mx1[:, r, :, 1], mx1[:, r, :, 2], ALU.max).then_inc(s["s_max"], 1)
                ve.wait_ge(s["s_max"], 2 * n + 2)
                if not (first and pp < 2):
                    ve.wait_ge(s["s_exp"], n - 1)
                ve.tensor_scalar(nb1[:, r, :, :], mx1[:, r, :, 0:2], -SC1, None, ALU.mult).then_inc(s["s_nb"], 1)

            def recip1(b, pp, first):
                n = 8 * no(b) + pp
                r = pp % 2
                ve.wait_ge(s["s_exp"], n + 1)
                if not (first and pp < 2):
                    ve.wait_ge(s["s_norm"], n - 1)
                ve.reciprocal(rc1[:, r, :, :], rs1[:, r, :, :]).then_inc(s["s_rec"], 1)

            def pt_out(b, pp, first):
                n = 8 * no(b) + pp
                ve.wait_ge(s["pt_psum"], n + 1)
                if not (first and pp < 2):
                    ve.wait_ge(*after(1, "pv_psum", n - 1))
                ve.tensor_copy(pt1[:, pp % 2, :, :], ps[:, 4:6, 0:3 * P]).then_inc(s["pt_evac"], 1)

            def attend1(b):
                ve.wait_ge(s["op_psum"], no(b) + 1)
                for t in range(QT):
                    ve.tensor_tensor(tokens(b, t), tokens(b, t), m[:, t * P:(t + 1) * P], ALU.add).then_inc(s["x_add"], 1)
                ve.wait_ge(*after(1, "x_add", 2 * no(b) + 2))

            def body1(b, ahead, behind, more=True):
                first = no(b) == 0 if isinstance(b[0], int) else False
                c, d = off(b, 1), off(b, -1)
                for p in range(M1):
                    if p == 4 and behind:
                        attend1(d)
                    if p == 6 and behind:
                        norm_out(1, d, not (isinstance(d[0], int) and no(d) < 2))
                    if p == 0 and ahead:
                        x_low(1, c)
                    if p == 7 and behind:
                        choose(1, d, (0,))
                    row_max1(b, p, first)
                    if p >= 1:
                        recip1(b, p - 1, first)
                    elif behind:
                        recip1(d, 7, False)
                    if p == 4 and behind:
                        stats(1, d, 1)
                    if p == 7 and behind:
                        choose(1, d, range(1, 6))
                    if p >= 2:
                        pt_out(b, p - 2, first)
                    elif behind:
                        pt_out(d, 6 + p, False)
                    if p == 1 and more:
                        enter1(off(b, 2))
                    if p == 4 and more:
                        norm_in(1, off(b, 2))
                    for q in pieces(b)[p:p + 1]:
                        ve.wait_ge(s["up_hi"], q + 1)
                        st, hi, lo = piece_parts(q)
                        ve.tensor_tensor(lo, st, hi, ALU.subtract).then_inc(s["up_lo"], 1)
                    if p == 7 and behind:
                        place(1, d)
                        weigh(1, d)

            def epilogue1(b):
                recip1(b, 7, False)
                pt_out(b, 6, False)
                pt_out(b, 7, False)
                attend1(b)
                stats(1, b, 1)
                norm_out(1, b, True)
                choose(1, b)
                place(1, b)
                table(1)
                weigh(1, b)

            enter1((0, 0))
            norm_in(1, (0, 0), False)
            x_low(1, (0, 0))
            enter1((0, 1))
            norm_in(1, (0, 1), False)

            body1((0, 0), True, False)
            with ve.Fori(0, 2) as i:
                for k in (1, 2):
                    body1((i, k), True, True)
            body1((0, 5), True, True)
            body1((0, 6), True, True, False)
            body1((0, 7), False, True, False)
            epilogue1((0, 7))
            experts(1)

            for q in range(4):
                ve.wait_ge(s[f"fin_in{q}"], 16 * TOPK)
                for ch in range(TOPK):
                    for t in range(q * TT // 4, (q + 1) * TT // 4):
                        op = ve.scalar_tensor_tensor(out=x_sb[:, t, :], in0=yfin[:, ch, t, :], scalar=wts[:, 1, t, ch:ch + 1],
                                                     in1=x_sb[:, t, :], op0=ALU.mult, op1=ALU.add)
                    if ch == 0:
                        op.then_inc(s["fin_one"], 1)
                        ve.wait_ge(s["fin_one"], q + 1)
                op.then_inc(s["fin_sum"], 1)
        @block.gpsimd
        def _(po):
            po.memset(blank[:, 0:D], 0.0).then_inc(s["blank_set"], 1)
            po.memset(blank[:, D:PAY].bitcast(I32), NOWHERE).then_inc(s["blank_set"], 1)
            po.wait_ge(s["blank_set"], 2)
            po.memset(v0[:, :, :, :, :].rearrange("p r t h n -> p (r t h n)"), 0.0).then_inc(s["v0_clear"], 1)
            po.memset(km[:, :, :].rearrange("p h n -> p (h n)").bitcast(F32), 0.0).then_inc(s["km_clear"], 1)
            po.sem_inc(s["blank_ready"], 1)

            def context_split(l, c):
                po.wait_ge(*after(l, f"ctx_in{par(c)}", 16 * (half(c) + 1)))
                settle(po)
                po.tensor_copy(hl[:, par(c), 1, 0, :], ct[:, par(c), :]).then_inc(s["ctx_hi"], 1)
                po.wait_ge(*after(l, "ctx_hi", no(c) + 1))
                po.tensor_tensor(hl[:, par(c), 1, 1, :], ct[:, par(c), :], hl[:, par(c), 1, 0, :], ALU.subtract).then_inc(s["ctx_split"], 1)

            def inverse_root(l, c, z):
                n0, ch = 14 * no(c), f"rs_chain{z}"
                k = 0
                v, vh, y, t = var[:, z, :], varh[:, z, :], rstd[:, z, :], rsq[:, z, :]

                def link(op):
                    nonlocal k
                    k += 1
                    op.then_inc(s[ch], 1)
                    po.wait_ge(*after(l, ch, n0 + k))
                    settle(po)

                po.wait_ge(*after(l, f"ln_stats{z}", 4 * no(c) + 4))
                settle(po)
                link(po.tensor_scalar(v, mv[:, z, :, 1], EPS, None, ALU.add))
                link(po.tensor_scalar(vh, v, -0.5, None, ALU.mult))
                link(po.tensor_scalar(y.bitcast(I32), v.bitcast(I32), -0.5, float(0x5F3759DF), ALU.mult, ALU.add))
                for n in range(3):
                    link(po.tensor_tensor(t, y, y, ALU.mult))
                    link(po.tensor_tensor(t, t, vh, ALU.mult))
                    link(po.tensor_scalar(t, t, 1.5, None, ALU.add))
                    op = po.tensor_tensor(y, t, y, ALU.mult)
                    if n < 2:
                        link(op)
                op.then_inc(s[f"rs_ready{z}"], 1)

            po.wait_ge(s["xa_in"], 16)
            inverse_root(0, (0, 0), 0)
            context_split(0, (0, 0))

            po.wait_ge(s["v0_clear"], 1)
            po.memset(v0[:, :, :, :, DK0], 1.0).then_inc(s["v0_ready"], 1)
            inverse_root(0, (0, 1), 0)

            had = [0, 0]

            def load(q, src, n):
                po.dma_start(stage[:, q % 2, 0:n], src(q)).then_inc(s[f"st_in{q % 2}"], 16)
                had[q % 2] += 1

            def split_piece(src, n, q, more):
                if more:
                    load(q + 1, src, n)
                po.wait_ge(s[f"st_in{q % 2}"], 16 * had[q % 2])
                hi, lo, st = w_up[:, 2 * q * n:(2 * q + 1) * n], w_up[:, (2 * q + 1) * n:(2 * q + 2) * n], stage[:, q % 2, 0:n]
                po.tensor_copy(hi, st).then_inc(s["st_split"], 1)
                split[0] += 1
                po.wait_ge(s["st_split"], split[0])
                po.tensor_tensor(lo, st, hi, ALU.subtract).then_inc(s["wup_split"], 1)
                po.wait_ge(s["wup_split"], split[0])

            split = [0]

            def piece0(q):
                return a["w1"][:, q * F0:(q + 1) * F0]

            def pack(l, b):
                po.wait_ge(*after(l, "pay_ready", no(b) + 1))
                settle(po)
                for t in range(QT):
                    po.tensor_copy(pay[:, par(b), t, :, D].bitcast(U32),
                                   dest[:, bass.ds(QT * no(b) + t, 1), :].rearrange("p a c -> p (a c)")).then_inc(s["pay_dest"], 1)
                po.tensor_copy(pay[:, par(b), :, 1, 0:D], pay[:, par(b), :, 0, 0:D]).then_inc(s["pay_copy"], 1)
            def send(l, b):
                po.wait_ge(*after(l, "pay_dest", 2 * no(b) + 2))
                po.wait_ge(*after(l, "pay_copy", no(b) + 1))
                po.wait_ge(*after(l, "slot_ready", no(b) + 1))
                settle(po)
                for t in range(QT):
                    for ch in range(TOPK):
                        po.indirect_dma_start(xs[l], bass.IndirectOffsetOnAxis(ap=sloti[:, par(b), t, ch:ch + 1], axis=0),
                                              pay[:, par(b), t, ch, :], None, bounds_check=ROWS - 1,
                                              oob_is_err=False).then_inc(s[f"sent{par(b)}"], 16)

            def sends(l, body):
                po.wait_ge(s[f"slots_blank{l}"], 16)
                body((0, 0), True, False)

                with po.Fori(0, 2) as i:
                    for k in (1, 2):
                        body((i, k), True, True)
                for b in (5, 6, 7):
                    body((0, b), b < 6, True)

            def body0(b):
                if isinstance(b[0], int) and no(b) == B - 1:
                    load(E - 1, piece0, F0)
                    po.wait_ge(s["a_psum"], H * B)
                    split_piece(piece0, F0, E - 1, False)
                if ahead(b, 2):
                    need(po, *after(0, "qk_psum", 4 * no(b) + 4))
                    settle(po)
                    context_split(0, off(b, 2))
                if ahead(b, -1):
                    inverse_root(0, off(b, -1), 1)
                if ahead(b, 3):
                    inverse_root(0, off(b, 3), 0)
                if ahead(b, -1):
                    pack(0, off(b, -1))
                    send(0, off(b, -1))
                pieces = {-1: (0, 1, 2), 0: (3, 4, 5), 6: (6,)}
                if isinstance(b[0], int) and no(b) in pieces:
                    own = pieces[no(b)]
                    load(own[0], piece0, F0)
                    for q in own:
                        split_piece(piece0, F0, q, q != own[-1])
                if isinstance(b[0], int) and no(b) == B - 1:
                    for w in range(2):
                        po.dma_start(stage[:, w, :], a["w1p"][:, w * 1024:(w + 1) * 1024]).then_inc(s[f"st_in{w}"], 16)
                        had[w] += 1

            po.wait_ge(s["slots_blank0"], 16)
            batches(po, body0)
            po.wait_ge(s["wl_split"], 1)
            po.dma_start(stage[:, 0, :], a["w1p"][:, 2048:3072]).then_inc(s["st_in0"], 16)
            had[0] += 1
            def experts(l):
                def scatter(u):
                    po.wait_ge(*after(l, "e_dst", tno(u) + 1))
                    po.wait_ge(*after(l, "e_yev", tno(u) + 1))
                    settle(po)
                    k = u[1] % 4
                    po.indirect_dma_start(yc[l], bass.IndirectOffsetOnAxis(ap=dsti[:, k:k + 1], axis=0), ye[:, k, :], None,
                                          bounds_check=TOPK * T - 1, oob_is_err=False).then_inc(s[f"es_out{k}"], 16)

                def step(t, known, table):
                    if live(known, 3):
                        scatter(off(t, -3))
                    if live(known, 0):
                        k = t[1] % 4
                        po.wait_ge(*after(l, f"xe_in{k}", 16 * (tq(t) + 1)))
                        if not (known < 4):
                            po.wait_ge(*after(l, f"es_out{k}", 16 * tq(t)))
                            settle(po)
                        po.tensor_copy(dsti[:, k:k + 1], xt[:, k, D:PAY].bitcast(U32)).then_inc(s["e_dst"], 1)

                steps(po, step)

            experts(0)
            context_split(1, (0, 0))

            def norm1(b, pp):
                n = 8 * no(b) + pp
                r = pp % 2
                po.wait_ge(s["s_rec"], n + 1)
                po.tensor_tensor(p1[:, r, :, 0:P], p1[:, r, :, 0:P], rc1[:, r, :, 0:1].broadcast_to([P, 2, P]), ALU.mult)
                po.tensor_tensor(p1[:, r, :, P:3 * P], p1[:, r, :, P:3 * P], rc1[:, r, :, 1:2].broadcast_to([P, 2, 2 * P]),
                                 ALU.mult).then_inc(s["s_norm"], 1)

            def body1(b, more, behind):
                for pp in range(M1):
                    norm1(b, pp)
                    if pp == 2 and more:
                        inverse_root(1, off(b, 2), 0)
                    if pp == 3 and behind:
                        inverse_root(1, off(b, -1), 1)
                    if pp == 4 and more:
                        po.wait_ge(*after(1, "v_psum", 4 * no(b) + 4))
                        settle(po)
                        context_split(1, off(b, 2))
                    if pp == 6 and behind:
                        pack(1, off(b, -1))
                if behind:
                    send(1, off(b, -1))

            inverse_root(1, (0, 0), 0)
            context_split(1, (0, 1))
            inverse_root(1, (0, 1), 0)
            po.wait_ge(s["wl_split"], 3)
            sends(1, body1)
            inverse_root(1, (0, 7), 1)
            pack(1, (0, 7))
            send(1, (0, 7))
            experts(1)

    return nc


_OUT = (B, S, D)


def kernel(**inputs):
    import concourse.bacc as bacc
    from concourse.bass_utils import run_bass_kernel_spmd

    v = {n: np.asarray(x) for n, x in inputs.items()}
    f, cbv = constants()
    bands = np.zeros((2, G, P), np.float32)
    wband = np.zeros((2, G, P, D), np.float32)
    for w, n in ((0, "q"), (1, "k")):
        for h in range(H):
            g, j = divmod(h, HB)
            for r in range(3):
                rows = slice(32 * j + DK0 * r, 32 * j + DK0 * (r + 1))
                bands[w, g, rows] = v[f"L0_xattn_b{n}"][h * DK0:(h + 1) * DK0]
                wband[w, g, rows] = v[f"L0_xattn_W{n}"][h * DK0:(h + 1) * DK0]
    bands[0, :, 25::32] = 1
    bands[1, :, 24::32] = -MASKED0
    for g in range(G):
        bands[1, g, 26 + g::32] = 1
    wd = np.zeros((E, FP1, D), np.float32)
    wd[:, :F1] = v["L1_ffn_Wd"]
    up = np.stack([v["L1_ffn_Wg"], v["L1_ffn_Wu"]], 2)
    arrays = {
        "cf": f,
        "cb": (cbv.view(np.uint32) >> 16).astype(np.uint16).view(np.int32),
        "x": v["x"].reshape(T, D),
        "ctxT": v["ctx_1024"].reshape(T, D).T,
        "mask": v["mask_Bx16xS2_ik1"].transpose(1, 0, 2),
        "wqk": wband.transpose(3, 0, 1, 2).reshape(D, 2 * G * P),
        "bias0": bands.transpose(2, 0, 1),
        "wv0": v["L0_xattn_Wv"].T,
        "bv": v["L0_xattn_bv"].reshape(1, D),
        "wr0": v["L0_ffn_W_router"],
        "wr1": v["L1_ffn_W_gate"],
        "br": v["L0_ffn_b_router"].reshape(1, E),
        "w1": v["L0_ffn_W1"].transpose(1, 0, 2).reshape(D, E * F0),
        "b1t": v["L0_ffn_b1"].reshape(E, C0, P).transpose(2, 0, 1),
        "w2": v["L0_ffn_W2"].reshape(E, C0, P, D).transpose(2, 0, 1, 3).reshape(P, E * C0 * D),
        "b2": v["L0_ffn_b2"].reshape(1, E * D),
        "w1p": np.concatenate([v["L1_xattn_w_q"].T, v["L1_xattn_w_k"].T, v["L1_xattn_w_v"].T], 1),
        "wo1": v["L1_xattn_w_o"].T.reshape(M1, P, D).transpose(1, 0, 2),
        "wgu": up.transpose(1, 0, 2, 3).reshape(D, E * 2 * F1),
        "wd": wd.reshape(E, C1, P, D).transpose(2, 0, 1, 3).reshape(P, E * C1 * D),
    }
    arrays = {n: np.ascontiguousarray(x) for n, x in arrays.items()}
    nc = bacc.Bacc("TRN2", target_bir_lowering=False, num_devices=1)
    a = {n: nc.dram_tensor(f"in_{n}", x.shape, mybir.dt.from_np(x.dtype), kind="ExternalInput").ap() for n, x in arrays.items()}
    out = nc.dram_tensor("out_0", (T, D), F32, kind="ExternalOutput").ap()
    program(nc, a, out)
    r = run_bass_kernel_spmd(nc, [{f"in_{n}": x for n, x in arrays.items()}], core_ids=[0])
    return np.asarray(r.results[0]["out_0"]).reshape(_OUT)
```
